# Optimizing a Trainium2 kernel written in Bass

```python
import numpy as np
import jax
import jax.numpy as jnp

def _softmax(x, axis=-1):
    return jax.nn.softmax(x, axis=axis)

def _gelu(x):
    return jax.nn.gelu(x, approximate=True)

def _silu(x):
    return jax.nn.silu(x)

def _sigmoid(x):
    return jax.nn.sigmoid(x)

def _layernorm(x, axis=-1, eps=1e-05):
    m = jnp.mean(x, axis=axis, keepdims=True)
    v = jnp.var(x, axis=axis, keepdims=True)
    return (x - m) / jnp.sqrt(v + eps)

def _scatter_add(tgt, idx, src, axis=0):
    return tgt.at[idx].add(src)

def _segment_sum(src, seg, n):
    return jax.ops.segment_sum(src, seg, n)
kernel_name = 'mk_adaln_ffn_d2_seqx_r4_50f7b5'

def setup_inputs(seed: int=0):
    np.random.seed(seed)
    _w = jnp.asarray

    def _rec_inputs():
        import jax
        import jax.numpy as jnp
        _rk = jax.random.key(seed)
        x = -0.0003929 + 0.9999 * jax.random.normal(jax.random.fold_in(_rk, 1), (64, 64, 1024), jnp.float32)
        _lenS = 64 - jax.random.randint(jax.random.fold_in(_rk, 7), (64,), 0, max(1, 64 // 4) + 1, jnp.int32)
        _lenS2 = 64 - jax.random.randint(jax.random.fold_in(_rk, 8), (64,), 0, max(1, 64 // 4) + 1, jnp.int32)
        cond_512 = 0.00782532 + 1.00527 * jax.random.normal(jax.random.fold_in(_rk, 11), (64, 128), jnp.float32)
        return (x, cond_512)
    x, cond_512 = _rec_inputs()

    def _L0_cond_setup():
        import jax, jax.numpy as jnp
        from jax import lax
        import numpy as np
        CIN, COUT, K, STYLE_DIM = (64, 64, 3, 128)
        N_LAYERS = 4
        TYPES = ('same', 'upsample', 'same', 'downsample')
        SCALE = 1.0 / float(np.sqrt(CIN * K ** 2))
        EPS = 1e-08
        _BK = np.array([1.0, 3.0, 3.0, 1.0], dtype=np.float32)
        BLUR_K = _BK / _BK.sum()

        def _blur(x, kern, pad):
            B, C, _ = x.shape
            xp = jnp.pad(x, ((0, 0), (0, 0), (pad[0], pad[1])))
            w = jnp.broadcast_to(kern.astype(x.dtype)[None, None, :], (C, 1, kern.shape[0]))
            return lax.conv_general_dilated(xp, w, (1,), 'VALID', feature_group_count=C, dimension_numbers=('NCH', 'OIH', 'NCH'))

        def _conv_same(x, w):
            p = (K - 1) // 2
            return lax.conv_general_dilated(x[None], w, (1,), [(p, p)], dimension_numbers=('NCH', 'OIH', 'NCH'))[0]

        def _conv_down(x, w):
            return lax.conv_general_dilated(x[None], w, (2,), 'VALID', dimension_numbers=('NCH', 'OIH', 'NCH'))[0]

        def _conv_up(x, w_t):
            return lax.conv_transpose(x[None], w_t, (2,), 'VALID', dimension_numbers=('NCH', 'IOH', 'NCH'), transpose_kernel=True)[0]

        def _layer(x, style, w, b, mw, mb, typ):
            s = style @ mw.T + mb
            weight = SCALE * w * s[:, None, :, None]
            demod = lax.rsqrt(jnp.sum(weight * weight, axis=(2, 3)) + EPS)
            weight = weight * demod[:, :, None, None]
            blur_k = jnp.asarray(BLUR_K)
            if typ == 'same':
                out = jax.vmap(_conv_same)(x, weight) + b[None, :, None]
            elif typ == 'upsample':
                out = jax.vmap(_conv_up)(x, weight.transpose(0, 2, 1, 3)) + b[None, :, None]
                out = _blur(out, 2.0 * blur_k, (1, 1))
            elif typ == 'downsample':
                xb = _blur(x, blur_k, (2, 2))
                out = jax.vmap(_conv_down)(xb, weight) + b[None, :, None]
            else:
                raise NotImplementedError(typ)
            return out
        key = jax.random.key(seed)
        ks = jax.random.split(key, 6)
        B, L = (16, 1024)
        return {'x': jax.random.normal(ks[0], (B, CIN, L), dtype=jnp.float32), 'style': jax.random.normal(ks[1], (B, STYLE_DIM), dtype=jnp.float32), 'weights': jax.random.normal(ks[2], (N_LAYERS, COUT, CIN, K), dtype=jnp.float32), 'biases': jax.random.normal(ks[3], (N_LAYERS, COUT), dtype=jnp.float32) * 0.1, 'mod_w': jax.random.normal(ks[4], (N_LAYERS, CIN, STYLE_DIM), dtype=jnp.float32) / np.sqrt(STYLE_DIM), 'mod_b': 1.0 + 0.1 * jax.random.normal(ks[5], (N_LAYERS, CIN), dtype=jnp.float32)}
    _L0_cond_all = _L0_cond_setup()
    _L0_cond_in = {k: v for k, v in _L0_cond_all.items() if k in ('weights', 'biases', 'mod_w', 'mod_b')}
    del _L0_cond_all

    def _L0_ffn_setup():
        import jax, jax.numpy as jnp
        import numpy as np
        DIM = 1024
        key = jax.random.key(seed)
        x = jax.random.normal(key, (4, 1024, DIM), dtype=jnp.float32)
        identity = jnp.eye(DIM, dtype=jnp.float32)
        return {'x': x, 'identity': identity}
    _L0_ffn_all = _L0_ffn_setup()
    _L0_ffn_in = {k: v for k, v in _L0_ffn_all.items() if k in ('identity',)}
    del _L0_ffn_all

    def _L1_cond_setup():
        import jax, jax.numpy as jnp
        from jax import lax
        import numpy as np
        CIN, COUT, K, STYLE_DIM = (64, 64, 3, 128)
        N_LAYERS = 4
        TYPES = ('same', 'upsample', 'same', 'downsample')
        SCALE = 1.0 / float(np.sqrt(CIN * K ** 2))
        EPS = 1e-08
        _BK = np.array([1.0, 3.0, 3.0, 1.0], dtype=np.float32)
        BLUR_K = _BK / _BK.sum()

        def _blur(x, kern, pad):
            B, C, _ = x.shape
            xp = jnp.pad(x, ((0, 0), (0, 0), (pad[0], pad[1])))
            w = jnp.broadcast_to(kern.astype(x.dtype)[None, None, :], (C, 1, kern.shape[0]))
            return lax.conv_general_dilated(xp, w, (1,), 'VALID', feature_group_count=C, dimension_numbers=('NCH', 'OIH', 'NCH'))

        def _conv_same(x, w):
            p = (K - 1) // 2
            return lax.conv_general_dilated(x[None], w, (1,), [(p, p)], dimension_numbers=('NCH', 'OIH', 'NCH'))[0]

        def _conv_down(x, w):
            return lax.conv_general_dilated(x[None], w, (2,), 'VALID', dimension_numbers=('NCH', 'OIH', 'NCH'))[0]

        def _conv_up(x, w_t):
            return lax.conv_transpose(x[None], w_t, (2,), 'VALID', dimension_numbers=('NCH', 'IOH', 'NCH'), transpose_kernel=True)[0]

        def _layer(x, style, w, b, mw, mb, typ):
            s = style @ mw.T + mb
            weight = SCALE * w * s[:, None, :, None]
            demod = lax.rsqrt(jnp.sum(weight * weight, axis=(2, 3)) + EPS)
            weight = weight * demod[:, :, None, None]
            blur_k = jnp.asarray(BLUR_K)
            if typ == 'same':
                out = jax.vmap(_conv_same)(x, weight) + b[None, :, None]
            elif typ == 'upsample':
                out = jax.vmap(_conv_up)(x, weight.transpose(0, 2, 1, 3)) + b[None, :, None]
                out = _blur(out, 2.0 * blur_k, (1, 1))
            elif typ == 'downsample':
                xb = _blur(x, blur_k, (2, 2))
                out = jax.vmap(_conv_down)(xb, weight) + b[None, :, None]
            else:
                raise NotImplementedError(typ)
            return out
        key = jax.random.key(seed)
        ks = jax.random.split(key, 6)
        B, L = (16, 1024)
        return {'x': jax.random.normal(ks[0], (B, CIN, L), dtype=jnp.float32), 'style': jax.random.normal(ks[1], (B, STYLE_DIM), dtype=jnp.float32), 'weights': jax.random.normal(ks[2], (N_LAYERS, COUT, CIN, K), dtype=jnp.float32), 'biases': jax.random.normal(ks[3], (N_LAYERS, COUT), dtype=jnp.float32) * 0.1, 'mod_w': jax.random.normal(ks[4], (N_LAYERS, CIN, STYLE_DIM), dtype=jnp.float32) / np.sqrt(STYLE_DIM), 'mod_b': 1.0 + 0.1 * jax.random.normal(ks[5], (N_LAYERS, CIN), dtype=jnp.float32)}
    _L1_cond_all = _L1_cond_setup()
    _L1_cond_in = {k: v for k, v in _L1_cond_all.items() if k in ('weights', 'biases', 'mod_w', 'mod_b')}
    del _L1_cond_all

    def _L1_ffn_setup():
        import jax, jax.numpy as jnp
        import numpy as np
        SCALING = 16.0 / 8.0
        GAMMA = 1.0
        EPS = 1e-12
        key = jax.random.key(seed)
        ks = jax.random.split(key, 8)
        B, T, H, O = (4, 512, 1024, 1024)
        E_tot, E_act, r = (16, 4, 8)
        return {'x': jax.random.normal(ks[0], (B, T, H), jnp.float32), 'W_base': jax.random.normal(ks[1], (O, H), jnp.float32) * 0.02, 'b_base': jax.random.normal(ks[2], (O,), jnp.float32) * 0.02, 'lora_A': jax.random.normal(ks[3], (E_tot, r, H), jnp.float32) * 0.02, 'lora_B': jax.random.normal(ks[4], (E_tot, O, r), jnp.float32) * 0.02, 'router_W': jax.random.normal(ks[5], (E_tot, H), jnp.float32) * 0.02, 'router_b': jax.random.normal(ks[6], (E_tot,), jnp.float32) * 0.02, 'domain_prior': jax.random.uniform(ks[7], (E_tot,), jnp.float32), 'active': jnp.arange(E_act, dtype=jnp.int32)}
    _L1_ffn_all = _L1_ffn_setup()
    _L1_ffn_in = {k: v for k, v in _L1_ffn_all.items() if k in ('W_base', 'b_base', 'lora_A', 'lora_B', 'router_W', 'router_b', 'domain_prior', 'active')}
    del _L1_ffn_all
    return {'x': x, 'cond_512': cond_512, 'L0_cond_weights': _L0_cond_in['weights'], 'L0_cond_biases': _L0_cond_in['biases'], 'L0_cond_mod_w': _L0_cond_in['mod_w'], 'L0_cond_mod_b': _L0_cond_in['mod_b'], 'L0_ffn_identity': _L0_ffn_in['identity'], 'L1_cond_weights': _L1_cond_in['weights'], 'L1_cond_biases': _L1_cond_in['biases'], 'L1_cond_mod_w': _L1_cond_in['mod_w'], 'L1_cond_mod_b': _L1_cond_in['mod_b'], 'L1_ffn_W_base': _L1_ffn_in['W_base'], 'L1_ffn_b_base': _L1_ffn_in['b_base'], 'L1_ffn_lora_A': _L1_ffn_in['lora_A'], 'L1_ffn_lora_B': _L1_ffn_in['lora_B'], 'L1_ffn_router_W': _L1_ffn_in['router_W'], 'L1_ffn_router_b': _L1_ffn_in['router_b'], 'L1_ffn_domain_prior': _L1_ffn_in['domain_prior'], 'L1_ffn_active': _L1_ffn_in['active']}

def reference(x, cond_512, L0_cond_weights, L0_cond_biases, L0_cond_mod_w, L0_cond_mod_b, L0_ffn_identity, L1_cond_weights, L1_cond_biases, L1_cond_mod_w, L1_cond_mod_b, L1_ffn_W_base, L1_ffn_b_base, L1_ffn_lora_A, L1_ffn_lora_B, L1_ffn_router_W, L1_ffn_router_b, L1_ffn_domain_prior, L1_ffn_active):
    import jax
    import jax.numpy as jnp

    def _L0_cond_ref(x, style, weights, biases, mod_w, mod_b):
        import jax, jax.numpy as jnp
        from jax import lax
        import numpy as np
        CIN, COUT, K, STYLE_DIM = (64, 64, 3, 128)
        N_LAYERS = 4
        TYPES = ('same', 'upsample', 'same', 'downsample')
        SCALE = 1.0 / float(np.sqrt(CIN * K ** 2))
        EPS = 1e-08
        _BK = np.array([1.0, 3.0, 3.0, 1.0], dtype=np.float32)
        BLUR_K = _BK / _BK.sum()

        def _blur(x, kern, pad):
            B, C, _ = x.shape
            xp = jnp.pad(x, ((0, 0), (0, 0), (pad[0], pad[1])))
            w = jnp.broadcast_to(kern.astype(x.dtype)[None, None, :], (C, 1, kern.shape[0]))
            return lax.conv_general_dilated(xp, w, (1,), 'VALID', feature_group_count=C, dimension_numbers=('NCH', 'OIH', 'NCH'))

        def _conv_same(x, w):
            p = (K - 1) // 2
            return lax.conv_general_dilated(x[None], w, (1,), [(p, p)], dimension_numbers=('NCH', 'OIH', 'NCH'))[0]

        def _conv_down(x, w):
            return lax.conv_general_dilated(x[None], w, (2,), 'VALID', dimension_numbers=('NCH', 'OIH', 'NCH'))[0]

        def _conv_up(x, w_t):
            return lax.conv_transpose(x[None], w_t, (2,), 'VALID', dimension_numbers=('NCH', 'IOH', 'NCH'), transpose_kernel=True)[0]

        def _layer(x, style, w, b, mw, mb, typ):
            s = style @ mw.T + mb
            weight = SCALE * w * s[:, None, :, None]
            demod = lax.rsqrt(jnp.sum(weight * weight, axis=(2, 3)) + EPS)
            weight = weight * demod[:, :, None, None]
            blur_k = jnp.asarray(BLUR_K)
            if typ == 'same':
                out = jax.vmap(_conv_same)(x, weight) + b[None, :, None]
            elif typ == 'upsample':
                out = jax.vmap(_conv_up)(x, weight.transpose(0, 2, 1, 3)) + b[None, :, None]
                out = _blur(out, 2.0 * blur_k, (1, 1))
            elif typ == 'downsample':
                xb = _blur(x, blur_k, (2, 2))
                out = jax.vmap(_conv_down)(xb, weight) + b[None, :, None]
            else:
                raise NotImplementedError(typ)
            return out
        out = x
        for i, typ in enumerate(TYPES):
            out = _layer(out, style, weights[i], biases[i], mod_w[i], mod_b[i], typ)
        return out

    def _L0_ffn_ref(x, identity):
        import jax, jax.numpy as jnp
        import numpy as np
        DIM = 1024
        return jnp.einsum('bsd,ed->bse', x, identity)

    def _L1_cond_ref(x, style, weights, biases, mod_w, mod_b):
        import jax, jax.numpy as jnp
        from jax import lax
        import numpy as np
        CIN, COUT, K, STYLE_DIM = (64, 64, 3, 128)
        N_LAYERS = 4
        TYPES = ('same', 'upsample', 'same', 'downsample')
        SCALE = 1.0 / float(np.sqrt(CIN * K ** 2))
        EPS = 1e-08
        _BK = np.array([1.0, 3.0, 3.0, 1.0], dtype=np.float32)
        BLUR_K = _BK / _BK.sum()

        def _blur(x, kern, pad):
            B, C, _ = x.shape
            xp = jnp.pad(x, ((0, 0), (0, 0), (pad[0], pad[1])))
            w = jnp.broadcast_to(kern.astype(x.dtype)[None, None, :], (C, 1, kern.shape[0]))
            return lax.conv_general_dilated(xp, w, (1,), 'VALID', feature_group_count=C, dimension_numbers=('NCH', 'OIH', 'NCH'))

        def _conv_same(x, w):
            p = (K - 1) // 2
            return lax.conv_general_dilated(x[None], w, (1,), [(p, p)], dimension_numbers=('NCH', 'OIH', 'NCH'))[0]

        def _conv_down(x, w):
            return lax.conv_general_dilated(x[None], w, (2,), 'VALID', dimension_numbers=('NCH', 'OIH', 'NCH'))[0]

        def _conv_up(x, w_t):
            return lax.conv_transpose(x[None], w_t, (2,), 'VALID', dimension_numbers=('NCH', 'IOH', 'NCH'), transpose_kernel=True)[0]

        def _layer(x, style, w, b, mw, mb, typ):
            s = style @ mw.T + mb
            weight = SCALE * w * s[:, None, :, None]
            demod = lax.rsqrt(jnp.sum(weight * weight, axis=(2, 3)) + EPS)
            weight = weight * demod[:, :, None, None]
            blur_k = jnp.asarray(BLUR_K)
            if typ == 'same':
                out = jax.vmap(_conv_same)(x, weight) + b[None, :, None]
            elif typ == 'upsample':
                out = jax.vmap(_conv_up)(x, weight.transpose(0, 2, 1, 3)) + b[None, :, None]
                out = _blur(out, 2.0 * blur_k, (1, 1))
            elif typ == 'downsample':
                xb = _blur(x, blur_k, (2, 2))
                out = jax.vmap(_conv_down)(xb, weight) + b[None, :, None]
            else:
                raise NotImplementedError(typ)
            return out
        out = x
        for i, typ in enumerate(TYPES):
            out = _layer(out, style, weights[i], biases[i], mod_w[i], mod_b[i], typ)
        return out

    def _L1_ffn_ref(x, W_base, b_base, lora_A, lora_B, router_W, router_b, domain_prior, active):
        import jax, jax.numpy as jnp
        import numpy as np
        SCALING = 16.0 / 8.0
        GAMMA = 1.0
        EPS = 1e-12
        y = jnp.einsum('bth,oh->bto', x, W_base) + b_base
        A = lora_A[active]
        Bm = lora_B[active]
        z = jnp.einsum('bth,erh->bter', x, A)
        contribs = jnp.einsum('bter,eor->bteo', z, Bm) * SCALING
        logits = jnp.einsum('bth,eh->bte', x, router_W) + router_b
        logits = logits[..., active]
        prior = domain_prior[active]
        alpha = jax.nn.softmax(jnp.log(prior + EPS) + logits / GAMMA, axis=-1)
        return y + jnp.einsum('bteo,bte->bto', contribs, alpha)
    x = x + _L0_ffn_ref(_L0_cond_ref(x, cond_512, L0_cond_weights, L0_cond_biases, L0_cond_mod_w, L0_cond_mod_b), L0_ffn_identity)
    x = x + _L1_ffn_ref(_L1_cond_ref(x, cond_512, L1_cond_weights, L1_cond_biases, L1_cond_mod_w, L1_cond_mod_b), L1_ffn_W_base, L1_ffn_b_base, L1_ffn_lora_A, L1_ffn_lora_B, L1_ffn_router_W, L1_ffn_router_b, L1_ffn_domain_prior, L1_ffn_active)
    return x

_drawn_inputs = setup_inputs


def setup_inputs(seed=0):
    import zlib

    import numpy as np

    out = dict(_drawn_inputs(seed))
    spreads = {}
    factors = {'L1_ffn_b_base': 3.816,
     'L1_ffn_router_W': 3.771,
     'L1_ffn_router_b': 200.0,
     'L1_ffn_domain_prior': 200.0}
    for name, (base, spread) in spreads.items():
        noise = np.random.default_rng([zlib.crc32(name.encode()), seed]).standard_normal(out[name].shape)
        drawn = base * np.exp(spread * noise) if base else spread * noise
        out[name] = jnp.asarray(drawn.astype(out[name].dtype))
    for name, factor in factors.items():
        out[name] = (out[name] * factor).astype(out[name].dtype)
    return out
```

```python
from contextlib import ExitStack

import concourse.bass as bass
import numpy as np
from concourse import mybir

ALU = mybir.AluOpType
ACT = mybir.ActivationFunctionType
F32 = mybir.dt.float32
F32R = mybir.dt.float32r
I32 = mybir.dt.int32
AX_X = mybir.AxisListType.X

NB, C, L = 64, 64, 1024
P = 128
NPAIR = NB // 2
HL = L // 2
STYLE = 128
NL, K = 4, 3
PAD = 2
NSH = 2 * PAD + 1
MINI = 8
MH = MINI // 2
CHUNKS = L // P
SCALE = 1.0 / float(np.sqrt(C * K ** 2))
EPS = 1e-8
UP = (0.25, 0.75, 0.75, 0.25)
DOWN = (0.125, 0.375, 0.375, 0.125)
E_TOT, E_ACT, R = 16, 4, 8
ZR = E_ACT * R
LORA_SCALE = 16.0 / 8.0
PRIOR_EPS = 1e-12

Q_STEPS = [(t, [r for r in range(-2, 2) if -2 <= 2 * r - t <= 2 and not (t == -2 and r == 1)]) for t in (0, -2, -1, 1)]
T_EVEN = [(0, [-2, -1, 0, 1]), (2, [-2, -1, 0, 1]), (-2, [-1, 0, 1])]
T_ODD = [(1, [-2, -1, 0, 1]), (-1, [-2, -1, 0, 1])]


def half(p):
    return slice(C * p, C * p + C)


def ffn_outs(pairs):
    return 2 * pairs + 2


def stores(pairs):
    return 16 * pairs + 16


def build(nc, a):
    with ExitStack() as ctx:
        def sb(name, shape, dt=F32):
            return ctx.enter_context(nc.sbuf_tensor(name, shape, dt))

        def sem(name):
            return ctx.enter_context(nc.semaphore(name))

        bank = [ctx.enter_context(nc.psum_tensor(f"bank{i}", [P, 512], F32)) for i in range(8)]
        comp_ps, conv_ps, ffn_ps, lora_ps = bank[0:2], bank[2:4], bank[4:6], bank[6]

        x1 = nc.dram_tensor("x1_dram", [NB, C, L], F32, kind="Internal").ap()

        style_in = sb("style_in", [NB, STYLE])
        modb = sb("modb", [P, NL])
        bias = sb("bias", [P, NL])
        ident = sb("ident", [P, P])

        style_t = sb("style_t", [STYLE, NB])
        mw_t = sb("mw_t", [STYLE, NL, P])
        s_all = sb("s_all", [P, NL, NB])
        ssq = sb("ssq", [P, NL, NB])
        wsum = sb("wsum", [P, NL, C])
        dvar = sb("dvar", [P, NL, NB])
        dsq = sb("dsq", [P, NL, NB])
        d_all = sb("d_all", [P, NL, NB])
        lam1 = sb("lam1", [P, NB])
        lam2 = sb("lam2", [P, NB])
        lam3 = sb("lam3", [P, NB + 2])
        lam4 = sb("lam4", [P, NB])
        add1 = sb("add1", [P, NB])
        add2 = sb("add2", [P, NB])
        add2q = sb("add2q", [P, NB])
        add3 = sb("add3", [P, NB])
        beta = sb("beta", [P, NB])
        bc = [sb(f"bc{i}", [P, NB]) for i in range(3)]

        wk = sb("wk", [P, NL, K, 2, C])
        wt = sb("wt", [P, NL, K, C])
        up_n = sb("up_n", [P, 2, 3, C])
        up_t = sb("up_t", [P, 2, 3, C])
        down_t = sb("down_t", [P, 6, C])
        sta = sb("sta", [P, 14, 2, C])
        qst, tst, dmv = sta[:, 0:4], sta[:, 4:9], sta[:, 9:13].rearrange("p (g b) q c -> p g (b q) c", g=2)
        m1, m2, m3, m4 = sta[:, 0:3], sta[:, 3:7], sta[:, 7:10], sta[:, 10:14]
        pst = sb("pst", [P, 2, 2, C])
        qst_h, qst_l = sb("qst_h", [P, 4, P], F32R), sb("qst_l", [P, 4, P], F32R)
        tst_h, tst_l = sb("tst_h", [P, 5, P], F32R), sb("tst_l", [P, 5, P], F32R)
        dmv_h, dmv_l = sb("dmv_h", [P, 4, P], F32R), sb("dmv_l", [P, 4, P], F32R)

        ends = sb("ends", [P, NPAIR, 2, MINI])
        win = [sb(f"win{i}", [P, 2 * NB * (2 * MH + 2)]) for i in range(2)]
        x8, y8 = (w[:, 0:2 * NB * (MH + 2)].rearrange("p (e b m) -> p e b m", e=2, b=NB) for w in win)
        z16, u16 = (w[:, :].rearrange("p (e b m) -> p e b m", e=2, b=NB) for w in win)
        mtmp = sb("mtmp", [P, 512])
        wsum_t = mtmp[0:C, :].rearrange("i (l o) -> i l o", l=NL)
        dtmp = ssq
        edge = sb("edge", [P, NB, 2, 2])

        f_in = [sb(f"f_in{i}", [P, L]) for i in range(2)]
        fw_h = sb("fw_h", [P, CHUNKS, L], F32R)
        fw_l = sb("fw_l", [P, CHUNKS, L], F32R)

        xraw = sb("xraw", [P, 2, L])
        xres = sb("xres", [P, L])
        xout = sb("xout", [P, L])
        x_h = [sb(f"x_h{h}", [P, HL + 2 * PAD], F32R) for h in range(2)]
        x_l = [sb(f"x_l{h}", [P, HL + 2 * PAD], F32R) for h in range(2)]
        w3_h = [sb(f"w3_h{h}", [P, 2 * P], F32R) for h in range(2)]
        w3_l = [sb(f"w3_l{h}", [P, 2 * P], F32R) for h in range(2)]
        p_h = [sb(f"p_h{h}", [P, 5 * C], F32R) for h in range(2)]
        p_l = [sb(f"p_l{h}", [P, 5 * C], F32R) for h in range(2)]
        q_h = [sb(f"q_h{h}", [P, 4 * C], F32R) for h in range(2)]
        q_l = [sb(f"q_l{h}", [P, 4 * C], F32R) for h in range(2)]
        t_h = [sb(f"t_h{h}", [P, NSH, 2, C], F32R) for h in range(2)]
        t_l = [sb(f"t_l{h}", [P, NSH, 2, C], F32R) for h in range(2)]
        conv_buf = sb("conv_buf", [P, 2, HL])
        conv = [conv_buf[:, h, :] for h in range(2)]
        conv_flat = conv_buf[:, :, :].rearrange("p h m -> p (h m)")
        w_in = conv_flat[:, 0:NL * C * K].rearrange("p (l i k) -> p l i k", l=NL, k=K)
        wsq = xout[:, 0:NL * C * K].rearrange("p (l i k) -> p l i k", l=NL, k=K)
        ct_h = sb("ct_h", [P, CHUNKS, 2, C], F32R)
        ct_l = sb("ct_l", [P, CHUNKS, 2, C], F32R)

        act_i = sb("act_i", [P, E_ACT], I32)
        act_f = sb("act_f", [P, E_ACT])
        act_m = sb("act_m", [P, E_ACT])
        pidx_i = sb("pidx_i", [P, 2], I32)
        pidx = sb("pidx", [P, 3])
        rr_i = sb("rr_i", [P, E_ACT, R], I32)
        rr = sb("rr", [P, E_ACT, R])
        sel = sb("sel", [P, 3, E_ACT, R])
        sel_e = sb("sel_e", [P, E_ACT])
        sel16 = sb("sel16", [E_TOT, E_ACT])
        rb_in = sb("rb_in", [E_TOT, 1])
        pr_in = sb("pr_in", [E_TOT, 1])
        lnp = sb("lnp", [E_TOT, 1])
        lsum = sb("lsum", [E_TOT, P])
        const4 = sb("const4", [P, E_ACT])
        ar_h = sb("ar_h", [P, CHUNKS, 64], F32R)
        ar_l = sb("ar_l", [P, CHUNKS, 64], F32R)
        bb = sb("bb", [P, L], F32R)
        b_part = win[1][:, 0:L]
        b_pack = b_part.rearrange("p (g e r) -> p g e r", g=CHUNKS, e=E_TOT)
        a_in, r_in, bias_in = xres[:, :], xout[0:E_TOT, :], xout[96:97, :]
        b_in = xraw[:, 0, :].rearrange("p (e g r) -> p e g r", e=E_TOT, g=CHUNKS)
        b_t = xraw[:, 1, :]
        mw_in = xraw[:, 1, 0:NL * STYLE].rearrange("p (l s) -> p l s", l=NL)
        gate = sb("gate", [P, 16])
        za = sb("za", [P, ZR])
        zcat = sb("zcat", [P, P])
        zt = sb("zt", [P, P], F32R)

        layers = [
            dict(x=a["x"], out=x1, w=a["L0_cond_weights"], b=a["L0_cond_biases"],
                            mw=a["L0_cond_mod_w"], mb=a["L0_cond_mod_b"], f=a["L0_ffn_identity"], lora=False),
            dict(x=x1, out=a["out"], w=a["L1_cond_weights"], b=a["L1_cond_biases"],
                            mw=a["L1_cond_mod_w"], mb=a["L1_cond_mod_b"], f=a["L1_ffn_W_base"], lora=True),
        ]
        names = ("params ends f_load0 f_load1 modt_acc modt s_acc s_ready w2_acc w2_ready d_acc dvar_ready dsqrt "
                 "mod_ready wt_acc wt_ready stat_ready x8_ready m1_acc y8_ready m2_acc z16_ready m3_acc u16_ready "
                 "m4_acc edge_ready b2_acc b2_ready b3_acc b3_ready b4_acc beta_ready fw_acc fw_hi fw_ready chain "
                 "x_load res_load x_hi x_ready w3_hi w3_ready p_acc p_hi p_ready q_acc q_hi q_ready t_acc t_hi "
                 "t_ready conv_acc c_mid c_edge ct_acc ct_hi ct_ready ffn_acc ffn_out stored").split()
        for n, ly in enumerate(layers):
            ly["s"] = {k: sem(f"{k}_{n}") for k in names}
        zs = {k: sem(k) for k in (
            "lora_in ident_made iota_made bias_row_moved ln_in ln_ready sel_ready bt_acc bt_ready ar_acc c4_acc "
            "ar_ready bb_acc bb_ready z_acc logit_ready exp_ready zcat_ready zt_acc zt_ready zeroed").split()}

        block = ctx.enter_context(nc.Block())

        @block.sync
        def _(sp):
            for n, ly in enumerate(layers):
                s = ly["s"]
                x_pair = ly["x"].rearrange("(j h) c l -> j c h l", h=2)
                x_rows = ly["x"].rearrange("(j h) c l -> j (h c) l", h=2)
                o_rows = ly["out"].rearrange("(j h) c l -> j (h c) l", h=2)
                if n:
                    sp.wait_ge(layers[n - 1]["s"]["ffn_out"], ffn_outs(NPAIR))
                    sp.wait_ge(layers[n - 1]["s"]["stored"], stores(NPAIR))
                sp.sem_inc(s["stored"], 16)
                if not n:
                    sp.dma_start(style_in[:, :], a["cond_512"]).then_inc(s["params"], 16)
                for g in range(2):
                    sp.dma_start(mw_in[half(g)], ly["mw"].rearrange("l c s -> c l s")).then_inc(s["params"], 16)
                    sp.dma_start(w_in[half(g)], ly["w"].rearrange("l o i k -> o l i k")).then_inc(s["params"], 16)
                    sp.dma_start(modb[half(g)], ly["mb"].rearrange("l c -> c l"), allow_slow_non_contiguous=True).then_inc(s["params"], 16)
                    sp.dma_start(bias[half(g)], ly["b"].rearrange("l c -> c l"), allow_slow_non_contiguous=True).then_inc(s["params"], 16)
                for e in range(2):
                    sp.dma_start(ends[:, :, e, :], x_rows[:, :, e * (L - MINI):e * (L - MINI) + MINI]
                                 .rearrange("j r l -> r j l")).then_inc(s["ends"], 16)
                if ly["lora"]:
                    sp.wait_ge(s["w2_ready"], 1)
                    sp.dma_start(act_i[:, :], a["L1_ffn_active"].unsqueeze(0).broadcast_to([P, E_ACT])).then_inc(zs["lora_in"], 16)
                    sp.dma_start(a_in[:, :], a["L1_ffn_lora_A"].rearrange("e r h -> (e r) h")).then_inc(zs["lora_in"], 16)
                    sp.dma_start(r_in[:, :], a["L1_ffn_router_W"]).then_inc(zs["lora_in"], 16)
                    sp.dma_start(b_in[:, :, :, :], a["L1_ffn_lora_B"].rearrange("e (p g) r -> p e g r", g=CHUNKS)).then_inc(zs["lora_in"], 16)
                    sp.dma_start(rb_in[:, :], a["L1_ffn_router_b"].unsqueeze(1)).then_inc(zs["lora_in"], 16)
                    sp.dma_start(pr_in[:, :], a["L1_ffn_domain_prior"].unsqueeze(1)).then_inc(zs["lora_in"], 16)
                    sp.dma_start(bias_in, a["L1_ffn_b_base"].unsqueeze(0)).then_inc(zs["lora_in"], 16)
                for ec in range(CHUNKS):
                    if ec >= 2:
                        sp.wait_ge(s["fw_acc"], 2 * (ec - 1))
                    sp.dma_start(f_in[ec % 2][:, :], ly["f"][ec * P:(ec + 1) * P, :]).then_inc((s["f_load0"], s["f_load1"])[ec % 2], 16)

                def load_x(j):
                    sp.dma_start(xraw[half(0)], x_pair[j]).then_inc(s["x_load"], 16)
                    sp.dma_start(xraw[half(1), :, 0:L - 1], x_pair[j, :, :, 1:L]).then_inc(s["x_load"], 16)

                def load_res(j):
                    sp.dma_start(xres[:, :], x_rows[j]).then_inc(s["res_load"], 16)

                def store(j):
                    sp.dma_start(o_rows[j], xout[:, :]).then_inc(s["stored"], 16)

                if ly["lora"]:
                    sp.wait_ge(zs["bb_ready"], 1)
                    sp.dma_start(bb[97:98, :].bitcast(F32), b_part[96:97, :]).then_inc(zs["bias_row_moved"], 16)
                load_x(0)
                load_res(0)
                sp.wait_ge(s["x_ready"], 2)
                load_x(1)
                with sp.Fori(2, NPAIR) as j:
                    sp.wait_ge(s["x_ready"], 2 * j)
                    load_x(j)
                    sp.wait_ge(s["ffn_out"], ffn_outs(j - 1))
                    store(j - 2)
                    load_res(j - 1)
                sp.wait_ge(s["ffn_out"], ffn_outs(NPAIR - 1))
                store(NPAIR - 2)
                load_res(NPAIR - 1)
                sp.wait_ge(s["ffn_out"], ffn_outs(NPAIR))
                store(NPAIR - 1)
                sp.wait_ge(s["stored"], stores(NPAIR))

        @block.gpsimd
        def _(pool):
            nc.gpsimd.memset(ident[:, :], 0.0).then_inc(zs["ident_made"], 1)
            pool.wait_ge(zs["ident_made"], 1)
            nc.gpsimd.affine_select(out=ident[:, :], in_=ident[:, :], compare_op=ALU.not_equal, fill=1.0, base=0,
                                    pattern=[[-1, P]], channel_multiplier=1).then_inc(zs["ident_made"], 1)
            nc.gpsimd.iota(pidx_i[:, 0:1], [[0, 1]], base=0, channel_multiplier=1).then_inc(zs["iota_made"], 1)
            nc.gpsimd.iota(rr_i[:, :, :], [[0, E_ACT], [1, R]], base=0, channel_multiplier=0).then_inc(zs["iota_made"], 1)
            for h in range(2):
                for t in (x_h[h], x_l[h]):
                    nc.gpsimd.memset(t[:, 0:PAD].bitcast(F32), 0.0)
                    nc.gpsimd.memset(t[:, PAD + HL:2 * PAD + HL].bitcast(F32), 0.0)
            for ly in layers:
                s = ly["s"]

                def split_low(j, h):
                    src = xraw[:, h, :].rearrange("p (m q) -> p m q", q=2)[:, :, 0]
                    pool.wait_ge(s["x_hi"], 2 * j + h + 1)
                    nc.gpsimd.tensor_tensor(x_l[h][:, PAD:PAD + HL], src, x_h[h][:, PAD:PAD + HL].bitcast(F32),
                                            ALU.subtract).then_inc(s["x_ready"], 1)

                def put_edge(j, h):
                    dst = conv[h][:, :]
                    dst = bass.AP(dst.tensor, dst.offset, [list(dst.ap[0]), [HL - 2, 2], [1, 2]])
                    nc.gpsimd.tensor_copy(dst, edge[:, bass.ds(2 * j + h, 1), :, :].rearrange("p b g m -> p (b g) m")
                                          ).then_inc(s["c_edge"], 1)

                def body(j, first=False):
                    split_low(j, 0)
                    split_low(j, 1)
                    if first:
                        pool.wait_ge(s["edge_ready"], 1)
                    else:
                        pool.wait_ge(s["ct_acc"], 2 * j)
                    put_edge(j, 0)
                    put_edge(j, 1)

                if ly is not layers[0]:
                    pool.wait_ge(layers[0]["s"]["ffn_out"], ffn_outs(NPAIR))
                body(0, True)
                with pool.Fori(1, NPAIR) as j:
                    body(j)

        @block.scalar
        def _(act):
            for ly in layers:
                s = ly["s"]
                if ly is not layers[0]:
                    act.wait_ge(layers[0]["s"]["ffn_out"], ffn_outs(NPAIR))
                act.wait_ge(s["dvar_ready"], 1)
                nc.scalar.activation(dsq[:, :, :], dvar[:, :, :], ACT.Sqrt).then_inc(s["dsqrt"], 1)
                act.wait_ge(s["wt_acc"], 1)
                for g in range(2):
                    ev = nc.scalar.copy(wt[:, 2 * g:2 * g + 2, :, :],
                                        bank[5 + g][:, 0:2 * K * C].rearrange("p (l k o) -> p l k o", l=2, k=K))
                    ev.then_inc(s["wt_ready"], 1)
                if ly["lora"]:
                    act.wait_ge(zs["ln_in"], 1)
                    nc.scalar.activation(lnp[:, :], gate[0:E_TOT, 0:1], ACT.Ln).then_inc(zs["ln_ready"], 1)
                for g in range(2 * CHUNKS):
                    act.wait_ge(s["fw_acc"], g + 1)
                    dst = fw_h[:, 4 * (g % 2):4 * (g % 2) + 4, (g // 2) * P:(g // 2 + 1) * P]
                    nc.scalar.copy(dst, bank[g % 2][:, :].rearrange("p (k e) -> p k e", k=4)).then_inc(s["fw_hi"], 1)

                def w3_high(j, h):
                    nc.scalar.activation(w3_h[h][:, :], pst[:, :, :, :].rearrange("p a q c -> p (a q c)"), ACT.Copy,
                                         scale=lam3[:, bass.ds(2 * j + h, 1)]).then_inc(s["w3_hi"], 1)

                def x_high(j, first=False):
                    act.wait_ge(s["x_load"], 32 * j + 32)
                    if not first:
                        act.wait_ge(s["conv_acc"], 2 * j)
                    for h in range(2):
                        nc.scalar.copy(x_h[h][:, PAD:PAD + HL],
                                       xraw[:, h, :].rearrange("p (m q) -> p m q", q=2)[:, :, 0]).then_inc(s["x_hi"], 1)

                def compose_high(j, gated=False):
                    for h in range(2):
                        act.wait_ge(s["p_acc"], 2 * j + h + 1)
                        nc.scalar.activation(p_h[h][:, :], comp_ps[h][:, 0:5 * C], ACT.Copy,
                                             scale=lam2[:, bass.ds(2 * j + h, 1)]).then_inc(s["p_hi"], 1)
                    if gated:
                        gate_exp(j - 1)
                    for h in range(2):
                        act.wait_ge(s["q_acc"], 2 * j + h + 1)
                        nc.scalar.activation(q_h[h][:, :], comp_ps[h][:, 0:4 * C], ACT.Copy,
                                             scale=lam1[:, bass.ds(2 * j + h, 1)]).then_inc(s["q_hi"], 1)
                    for h in range(2):
                        w3_high(j + 1, h)
                    for h in range(2):
                        act.wait_ge(s["t_acc"], 2 * j + h + 1)
                        for q, ps in enumerate((comp_ps[h], conv_ps[h])):
                            nc.scalar.activation(t_h[h][:, :, q, :], ps[:, 0:NSH * C].rearrange("p (u c) -> p u c", c=C),
                                                 ACT.Copy, scale=s_all[:, 0, bass.ds(2 * j + h, 1)]).then_inc(s["t_hi"], 1)

                def conv_out(j, first=False):
                    for h in range(2):
                        act.wait_ge(s["conv_acc"], 2 * j + h + 1)
                        if not first:
                            act.wait_ge(s["ct_acc"], 2 * j)
                        nc.scalar.activation(conv[h][:, 2:HL - 2], conv_ps[h][:, 2:HL - 2], ACT.Identity,
                                             scale=lam4[:, bass.ds(2 * j + h, 1)],
                                             bias=beta[:, bass.ds(2 * j + h, 1)]).then_inc(s["c_mid"], 1)
                    for h in range(2):
                        act.wait_ge(s["ct_acc"], 2 * j + h + 1)
                        nc.scalar.copy(ct_h[:, :, h, :], conv_ps[h][:, :].rearrange("p (k o) -> p k o", o=C)
                                       ).then_inc(s["ct_hi"], 1)

                def gate_exp(j):
                    act.wait_ge(zs["logit_ready"], j + 1)
                    nc.scalar.activation(gate[:, 8:12], gate[:, 4:8], ACT.Exp).then_inc(zs["exp_ready"], 1)

                def zt_out(j):
                    act.wait_ge(zs["zt_acc"], j + 1)
                    nc.scalar.copy(zt[0:98, :], lora_ps[0:98, 64:64 + P]).then_inc(zs["zt_ready"], 1)

                act.wait_ge(s["stat_ready"], 1)
                for h in range(2):
                    w3_high(0, h)
                x_high(0, True)
                compose_high(0)
                act.wait_ge(s["beta_ready"], 1)
                conv_out(0, True)
                with act.Fori(1, NPAIR) as j:
                    x_high(j)
                    compose_high(j, ly["lora"])
                    if ly["lora"]:
                        zt_out(j - 1)
                    conv_out(j)
                if ly["lora"]:
                    gate_exp(NPAIR - 1)
                    zt_out(NPAIR - 1)

        @block.vector
        def _(dve):
            for n, ly in enumerate(layers):
                s = ly["s"]
                done = [0]

                def link(ins):
                    done[0] += 1
                    ins.then_inc(s["chain"], 1)
                    dve.wait_ge(s["chain"], done[0])

                v = nc.vector
                if n == 0:
                    for t in (pst[:, :, :, :], lam3[:, :], zcat[:, :]):
                        link(v.memset(t, 0.0))
                    v.memset(zcat[:, 96:98], 1.0)
                    for h in range(2):
                        v.memset(t_h[h][:, 0, 0, :].bitcast(F32), 0.0)
                    link(v.memset(bb[:, :].bitcast(F32), 0.0))
                dve.sem_inc(s["ffn_out"], 2)
                v.memset(sta[:, :, :, :], 0.0)
                for w in win:
                    link(v.memset(w[:, :], 0.0))
                dve.wait_ge(s["params"], 16 * (9 if n == 0 else 8))
                link(v.tensor_tensor(wsq[:, :, :, :], w_in[:, :, :, :], w_in[:, :, :, :], ALU.mult))
                v.tensor_reduce(wsum[:, :, :].rearrange("p l i -> p (l i)"),
                                wsq[:, :, :, :].rearrange("p l i k -> p (l i) k"), AX_X, ALU.add).then_inc(s["w2_ready"], 1)
                for l in range(NL):
                    for g in range(2):
                        last = v.tensor_copy(wk[:, l, :, g, :], w_in[:, l, :, :].rearrange("p i k -> p k i"))
                last.then_inc(s["w2_ready"], 1)
                dve.wait_ge(s["modt_acc"], 2)
                v.tensor_copy(style_t[:, :], bank[0][:, 0:NB])
                v.tensor_copy(mw_t[:, :, :], bank[1][:, :].rearrange("p (l c) -> p l c", l=NL)).then_inc(s["modt"], 1)
                dve.wait_ge(s["s_acc"], 1)
                link(v.tensor_tensor(s_all[:, :, :], bank[2][:, 0:NL * NB].rearrange("p (l b) -> p l b", l=NL),
                                     modb[:, :].unsqueeze(2).broadcast_to([P, NL, NB]), ALU.add))
                v.tensor_tensor(ssq[:, :, :], s_all[:, :, :], s_all[:, :, :], ALU.mult).then_inc(s["s_ready"], 1)
                dve.wait_ge(s["w2_acc"], 1)
                v.tensor_copy(wsum_t[:, :, :], bank[3][0:C, :].rearrange("p (l o) -> p l o", l=NL)).then_inc(s["s_ready"], 1)
                dve.wait_ge(s["d_acc"], 1)
                v.tensor_scalar(dvar[:, :, :], bank[4][:, 0:NL * NB].rearrange("p (l b) -> p l b", l=NL),
                                SCALE * SCALE, EPS, ALU.mult, ALU.add).then_inc(s["dvar_ready"], 1)
                dve.wait_ge(s["dsqrt"], 1)
                link(v.reciprocal(dsq[:, :, :], dsq[:, :, :]))
                link(v.tensor_tensor(dtmp[:, :, :], dsq[:, :, :], dsq[:, :, :], ALU.mult))
                link(v.tensor_tensor(dtmp[:, :, :], dtmp[:, :, :], dvar[:, :, :], ALU.mult))
                link(v.tensor_scalar(dtmp[:, :, :], dtmp[:, :, :], -0.5, 1.5, ALU.mult, ALU.add))
                link(v.tensor_tensor(d_all[:, :, :], dtmp[:, :, :], dsq[:, :, :], ALU.mult))
                stt = v.scalar_tensor_tensor
                stt(out=lam1[:, :], in0=d_all[:, 0, :], scalar=SCALE, in1=d_all[:, 1, :], op0=ALU.mult, op1=ALU.mult)
                stt(out=lam2[:, :], in0=s_all[:, 1, :], scalar=SCALE, in1=s_all[:, 2, :], op0=ALU.mult, op1=ALU.mult)
                stt(out=lam3[:, 0:NB], in0=d_all[:, 2, :], scalar=SCALE, in1=s_all[:, 3, :], op0=ALU.mult, op1=ALU.mult)
                v.tensor_scalar(lam4[:, :], d_all[:, 3, :], SCALE, None, ALU.mult)
                v.tensor_scalar(add1[:, :], d_all[:, 1, :], bias[:, 0:1], None, ALU.mult)
                v.tensor_scalar(add2[:, :], s_all[:, 2, :], bias[:, 1:2], 2.0, ALU.mult, ALU.mult)
                v.tensor_scalar(add2q[:, :], s_all[:, 2, :], bias[:, 1:2], 0.25, ALU.mult, ALU.mult)
                link(v.tensor_scalar(add3[:, :], s_all[:, 3, :], bias[:, 2:3], None, ALU.mult))
                dve.wait_ge(s["ends"], 32)
                for p in range(2):
                    for h in range(2):
                        for e in range(2):
                            last = v.tensor_tensor(
                                x8[half(p), e, h::2, 1:1 + MH], ends[half(h), :, e, p::2],
                                s_all[half(h), 0, h::2].unsqueeze(2).broadcast_to([C, NPAIR, MH]), ALU.mult)
                last.then_inc(s["x8_ready"], 1)

                dve.wait_ge(s["wt_ready"], 2)

                def mix(dst, srcs):
                    (c0, t0), rest = srcs[0], srcs[1:]
                    link(v.tensor_scalar(dst, t0, c0, None, ALU.mult))
                    for c, t in rest:
                        link(stt(out=dst, in0=t, scalar=c, in1=dst, op0=ALU.mult, op1=ALU.add))

                for dst, src in ((up_n, lambda k: wk[:, 1, k, 0, :]), (up_t, lambda k: wt[:, 1, k, :])):
                    for z in range(2):
                        for t in (-1, 0, 1):
                            terms = [(UP[2 * t + k + 1 - z], src(k)) for k in range(K) if 0 <= 2 * t + k + 1 - z < 4]
                            mix(dst[:, z, t + 1, :], terms)
                for e in range(6):
                    mix(down_t[:, e, :], [(DOWN[e - k], wt[:, 3, k, :]) for k in range(K) if 0 <= e - k < 4])

                for p in range(2):
                    for ab in range(2):
                        for q in range(2):
                            k = -2 + ab + 2 * p + q + 1
                            if 0 <= k < K:
                                v.tensor_copy(pst[half(p), ab, q, :], wk[half(p), 2, k, 0, :])
                        for i in range(3):
                            v.tensor_copy(dmv[half(p), ab, i + p, :], down_t[half(p), 2 * i + ab, :])
                    for t in range(-2, 2):
                        for h in range(2):
                            if -1 <= t + h <= 1:
                                v.tensor_copy(qst[half(p), t + 2, h, :], up_t[half(p), p, t + h + 1, :])
                    for d in range(-2, 3):
                        for q in range(2):
                            k = d + q - p + 1
                            if 0 <= k < K:
                                last = v.tensor_copy(tst[half(p), d + 2, q, :], wk[half(p), 0, k, 0, :])
                link(last)
                for src, hi, lo in ((0, qst_h, qst_l), (4, tst_h, tst_l), (9, dmv_h, dmv_l)):
                    flat = sta[:, src:src + hi.shape[1]].rearrange("p a q c -> p a (q c)")
                    link(v.tensor_copy(hi[:, :, :], flat))
                    link(v.tensor_tensor(lo[:, :, :], flat, hi[:, :, :].bitcast(F32), ALU.subtract))
                link(v.memset(sta[:, :, :, :], 0.0))

                for p in range(2):
                    for sh in (-1, 0, 1):
                        for q in range(2):
                            k = 2 * sh + p - q + 1
                            if 0 <= k < K:
                                v.tensor_copy(m1[half(p), sh + 1, q, :], wt[half(p), 0, k, :])
                                v.tensor_copy(m3[half(p), sh + 1, q, :], wt[half(p), 2, k, :])
                    for i, (q, sh) in enumerate(((0, -1), (0, 0), (1, 0), (1, 1))):
                        t = 2 * sh + p - q
                        if -1 <= t <= 1:
                            v.tensor_copy(m2[half(p), i, :, :], up_n[half(p), :, t + 1, :])
                    for i in range(4):
                        for q in range(2):
                            e = 2 * (i - 1 - q) + p + 2
                            if 0 <= e < 6:
                                last = v.tensor_copy(m4[half(p), i, q, :], down_t[half(p), e, :])
                last.then_inc(s["stat_ready"], 1)

                def scaled(dst, ps, lam, add, shape, tmp):
                    link(v.tensor_tensor(tmp, ps, lam.broadcast_to(shape), ALU.mult))
                    return v.tensor_tensor(dst, tmp, add.broadcast_to(shape), ALU.add)

                tm = mtmp[:, :]
                dve.wait_ge(s["m1_acc"], 1)
                for e in range(2):
                    last = scaled(y8[:, e, :, 1:1 + MH], bank[0][:, e * 256:e * 256 + 256].rearrange("p (b m) -> p b m", m=MH),
                                  lam1[:, :].unsqueeze(2), add1[:, :].unsqueeze(2), [P, NB, MH],
                                  tm[:, e * 256:e * 256 + 256].rearrange("p (b m) -> p b m", m=MH))
                last.then_inc(s["y8_ready"], 1)
                link(v.memset(win[0][:, :], 0.0))
                dve.wait_ge(s["m2_acc"], 1)
                for q in range(2):
                    for e in range(2):
                        link(scaled(z16[:, e, :, 1 + q:1 + 2 * MH:2],
                                    bank[1 + q][:, e * 256:e * 256 + 256].rearrange("p (b m) -> p b m", m=MH),
                                    lam2[:, :].unsqueeze(2), add2[:, :].unsqueeze(2), [P, NB, MH],
                                    tm[:, e * 256:e * 256 + 256].rearrange("p (b m) -> p b m", m=MH)))
                v.tensor_tensor(z16[half(0), 0, :, 1], z16[half(0), 0, :, 1], add2q[half(0), :], ALU.subtract)
                v.tensor_tensor(z16[half(1), 1, :, 2 * MH], z16[half(1), 1, :, 2 * MH], add2q[half(1), :],
                                ALU.subtract).then_inc(s["z16_ready"], 1)
                link(v.memset(win[1][:, :], 0.0))
                dve.wait_ge(s["m3_acc"], 1)
                for e in range(2):
                    last = scaled(u16[:, e, :, 1:1 + 2 * MH], bank[3 + e][:, :].rearrange("p (b m) -> p b m", m=2 * MH),
                                  lam3[:, 0:NB].unsqueeze(2), add3[:, :].unsqueeze(2), [P, NB, 2 * MH],
                                  tm.rearrange("p (b m) -> p b m", m=2 * MH))
                    if e == 0:
                        link(last)
                last.then_inc(s["u16_ready"], 1)
                dve.wait_ge(s["m4_acc"], 1)
                link(v.tensor_tensor(tm[:, 0:256].rearrange("p (b m) -> p b m", m=4),
                                     bank[0][:, 0:256].rearrange("p (b m) -> p b m", m=4),
                                     lam4[:, :].unsqueeze(2).broadcast_to([P, NB, 4]), ALU.mult))
                v.tensor_scalar(edge[:, :, :, :].rearrange("p b g m -> p (b g m)"), tm[:, 0:256], bias[:, 3:4], None,
                                ALU.add).then_inc(s["edge_ready"], 1)
                for src, lam, add, acc, ready, bk in ((bc[0], lam2[:, :], add2[:, :], s["b2_acc"], s["b2_ready"], 1),
                                                      (bc[1], lam3[:, 0:NB], add3[:, :], s["b3_acc"], s["b3_ready"], 2)):
                    dve.wait_ge(acc, 1)
                    link(v.tensor_tensor(src[:, :], bank[bk][:, 0:NB], lam, ALU.mult))
                    v.tensor_tensor(src[:, :], src[:, :], add, ALU.add).then_inc(ready, 1)
                dve.wait_ge(s["b4_acc"], 1)
                link(v.tensor_tensor(bc[2][:, :], bank[3][:, 0:NB], lam4[:, :], ALU.mult))
                v.tensor_scalar(beta[:, :], bc[2][:, :], bias[:, 3:4], None, ALU.add).then_inc(s["beta_ready"], 1)

                if ly["lora"]:
                    dve.wait_ge(zs["lora_in"], 16 * 7)
                    dve.wait_ge(zs["iota_made"], 2)
                    link(v.tensor_copy(act_f[:, :], act_i[:, :]))
                    link(v.tensor_scalar(act_m[:, :], act_f[:, :], 0.0, float(E_TOT), ALU.is_lt, ALU.mult))
                    link(v.tensor_tensor(act_f[:, :], act_f[:, :], act_m[:, :], ALU.add))
                    link(v.tensor_scalar(act_f[:, :], act_f[:, :], 0.0, float(E_TOT - 1), ALU.max, ALU.min))
                    link(v.tensor_scalar(pidx_i[:, 1:2], pidx_i[:, 0:1], 3, None, ALU.logical_shift_right))
                    link(v.tensor_copy(pidx[:, 0:2], pidx_i[:, 0:2]))
                    link(stt(out=pidx[:, 2:3], in0=pidx[:, 1:2], scalar=-float(R), in1=pidx[:, 0:1], op0=ALU.mult, op1=ALU.add))
                    link(v.tensor_copy(rr[:, :, :], rr_i[:, :, :]))
                    link(v.tensor_scalar(sel_e[:, :], act_f[:, :], pidx[:, 1:2], None, ALU.is_equal))
                    v.tensor_scalar(sel16[:, :], act_f[0:E_TOT, :], pidx[0:E_TOT, 0:1], None, ALU.is_equal)
                    for g in range(3):
                        stt(out=sel[:, g, :, :], in0=rr[:, :, :], scalar=pidx[:, 2:3],
                            in1=sel_e[:, :].unsqueeze(2).broadcast_to([P, E_ACT, R]), op0=ALU.is_equal, op1=ALU.mult)
                    link(v.tensor_scalar(gate[0:E_TOT, 0:1], pr_in[:, :], PRIOR_EPS, None, ALU.add))
                    v.tensor_copy(gate[0:E_TOT, 1:2], gate[0:E_TOT, 0:1]).then_inc(zs["ln_in"], 1)
                    dve.wait_ge(zs["ln_ready"], 1)
                    link(v.tensor_tensor(lnp[:, :], lnp[:, :], rb_in[:, :], ALU.add))
                    link(v.tensor_copy(b_pack, b_in.rearrange("p e g r -> p g e r")))
                    v.tensor_copy(lsum[:, :], lnp[:, :].broadcast_to([E_TOT, P])).then_inc(zs["sel_ready"], 1)
                    dve.wait_ge(zs["bt_acc"], 1)
                    for g in range(2):
                        last = v.tensor_copy(b_t[:, :].rearrange("e (p g) -> e g p", g=CHUNKS)[:, 4 * g:4 * g + 4, :],
                                             bank[g][:, :].rearrange("e (g p) -> e g p", g=4))
                    last.then_inc(zs["bt_ready"], 1)
                    dve.wait_ge(zs["ar_acc"], 1)
                    ar = bank[2][:, :].rearrange("p (k n) -> p k n", k=CHUNKS)[:, :, 0:ZR + E_ACT]
                    link(v.tensor_copy(ar_h[:, :, 0:ZR + E_ACT], ar))
                    v.tensor_tensor(ar_l[:, :, 0:ZR + E_ACT], ar, ar_h[:, :, 0:ZR + E_ACT].bitcast(F32), ALU.subtract)
                    v.tensor_copy(const4[:, :], bank[3][:, 0:E_ACT]).then_inc(zs["ar_ready"], 1)
                    dve.wait_ge(zs["bb_acc"], 1)
                    for g in range(2):
                        cols = slice(512 * g, 512 * g + 512)
                        v.tensor_copy(bb[0:64, cols], bank[4 + g][0:64, :])
                        link(v.tensor_copy(b_part[64:96, cols].bitcast(F32R), bank[4 + g][64:96, :]))
                        v.tensor_tensor(bb[64:96, cols], bank[4 + g][64:96, :], b_part[64:96, cols], ALU.subtract)
                    link(v.tensor_copy(bb[96:97, :], bias_in))
                    v.tensor_tensor(b_part[96:97, :], bias_in, bb[96:97, :].bitcast(F32), ALU.subtract).then_inc(zs["bb_ready"], 1)

                for g in range(2 * CHUNKS):
                    dve.wait_ge(s["fw_hi"], g + 1)
                    at = (slice(None), slice(4 * (g % 2), 4 * (g % 2) + 4), slice((g // 2) * P, (g // 2 + 1) * P))
                    v.tensor_tensor(fw_l[at], bank[g % 2][:, :].rearrange("p (k e) -> p k e", k=4), fw_h[at].bitcast(F32),
                                    ALU.subtract).then_inc(s["fw_ready"], 1)

                def low(dst, ps, lam, high):
                    return stt(out=dst, in0=ps, scalar=lam, in1=high.bitcast(F32), op0=ALU.mult, op1=ALU.subtract)

                def w3_low(j, h):
                    dve.wait_ge(s["w3_hi"], 2 * j + h + 1)
                    low(w3_l[h][:, :], pst[:, :, :, :].rearrange("p a q c -> p (a q c)"), lam3[:, bass.ds(2 * j + h, 1)],
                        w3_h[h][:, :]).then_inc(s["w3_ready"], 1)

                def compose_low(j, lora=False):
                    for h in range(2):
                        dve.wait_ge(s["p_hi"], 2 * j + h + 1)
                        low(p_l[h][:, :], comp_ps[h][:, 0:5 * C], lam2[:, bass.ds(2 * j + h, 1)], p_h[h][:, :]).then_inc(s["p_ready"], 1)
                    if lora:
                        gates(j - 1)
                    for h in range(2):
                        dve.wait_ge(s["q_hi"], 2 * j + h + 1)
                        low(q_l[h][:, :], comp_ps[h][:, 0:4 * C], lam1[:, bass.ds(2 * j + h, 1)], q_h[h][:, :]).then_inc(s["q_ready"], 1)
                    for h in range(2):
                        w3_low(j + 1, h)
                    for h in range(2):
                        for q, ps in enumerate((comp_ps[h], conv_ps[h])):
                            dve.wait_ge(s["t_hi"], 4 * j + 2 * h + q + 1)
                            low(t_l[h][:, :, q, :], ps[:, 0:NSH * C].rearrange("p (u c) -> p u c", c=C),
                                s_all[:, 0, bass.ds(2 * j + h, 1)], t_h[h][:, :, q, :]).then_inc(s["t_ready"], 1)

                def ffn_result(j):
                    dve.wait_ge(s["ffn_acc"], j + 1)
                    dve.wait_ge(s["res_load"], 16 * j + 16)
                    dve.wait_ge(s["stored"], stores(j))
                    for e in range(2):
                        v.tensor_tensor(xout[:, 512 * e:512 * e + 512], ffn_ps[e][:, :], xres[:, 512 * e:512 * e + 512],
                                        ALU.add).then_inc(s["ffn_out"], 1)

                def turned_low(j):
                    for h in range(2):
                        dve.wait_ge(s["ct_hi"], 2 * j + h + 1)
                        v.tensor_tensor(ct_l[:, :, h, :], conv_ps[h][:, :].rearrange("p (k o) -> p k o", o=C),
                                        ct_h[:, :, h, :].bitcast(F32), ALU.subtract).then_inc(s["ct_ready"], 1)

                gdone = [0]
                GSTEPS = 7

                def gates(j):
                    def glink(ins, i):
                        ins.then_inc(zs["zeroed"], 1)
                        dve.wait_ge(zs["zeroed"], GSTEPS * j + i)
                    dve.wait_ge(zs["z_acc"], j + 1)
                    glink(v.tensor_tensor(gate[:, 0:4], lora_ps[:, ZR:ZR + E_ACT], const4[:, :], ALU.add), 1)
                    glink(v.tensor_reduce(gate[:, 12:13], gate[:, 0:4], AX_X, ALU.max), 2)
                    v.tensor_scalar(gate[:, 4:8], gate[:, 0:4], gate[:, 12:13], None, ALU.subtract).then_inc(zs["logit_ready"], 1)
                    dve.wait_ge(zs["exp_ready"], j + 1)
                    glink(v.tensor_reduce(gate[:, 13:14], gate[:, 8:12], AX_X, ALU.add), 3)
                    glink(v.reciprocal(gate[:, 14:15], gate[:, 13:14]), 4)
                    glink(v.tensor_scalar(gate[:, 0:4], gate[:, 8:12], gate[:, 14:15], LORA_SCALE, ALU.mult, ALU.mult), 5)
                    glink(v.tensor_tensor(za[:, :].rearrange("p (e r) -> p e r", r=R),
                                          lora_ps[:, 0:ZR].rearrange("p (e r) -> p e r", r=R),
                                          gate[:, 0:4].unsqueeze(2).broadcast_to([P, E_ACT, R]), ALU.mult), 6)
                    v.tensor_copy(zcat[:, 2 * ZR:3 * ZR].bitcast(F32R), za[:, :])
                    glink(v.tensor_copy(zcat[:, 0:ZR].bitcast(F32R), za[:, :]), 7)
                    v.tensor_tensor(zcat[:, ZR:2 * ZR], za[:, :], zcat[:, 0:ZR], ALU.subtract).then_inc(zs["zcat_ready"], 1)

                for h in range(2):
                    w3_low(0, h)
                compose_low(0)
                turned_low(0)
                with dve.Fori(1, NPAIR) as j:
                    compose_low(j, ly["lora"])
                    ffn_result(j - 1)
                    turned_low(j)
                if ly["lora"]:
                    gates(NPAIR - 1)
                ffn_result(NPAIR - 1)

        @block.tensor
        def _(pe):
            mm = nc.tensor.matmul

            def three(out, wh, wl, xh, xl, start, stop):
                mm(out, wh, xh, start=start, stop=False, skip_group_check=True)
                mm(out, wh, xl, start=False, stop=False, skip_group_check=True)
                return mm(out, wl, xh, start=False, stop=stop, skip_group_check=True)

            for n, ly in enumerate(layers):
                s = ly["s"]
                if n == 0:
                    pe.wait_ge(zs["ident_made"], 2)
                else:
                    pe.wait_ge(layers[0]["s"]["ffn_out"], ffn_outs(NPAIR))
                pe.wait_ge(s["params"], 16 * (9 if n == 0 else 8))
                nc.tensor.transpose(bank[0][:, 0:NB], style_in[:, :], ident[0:NB, 0:NB]).then_inc(s["modt_acc"], 1)
                for l in range(NL):
                    last = nc.tensor.transpose(bank[1][:, l * P:(l + 1) * P], mw_in[:, l, :], ident[:, :])
                last.then_inc(s["modt_acc"], 1)
                pe.wait_ge(s["w2_ready"], 1)
                for l in range(NL):
                    last = mm(bank[3][0:C, l * P:(l + 1) * P], wsum[:, l, :], ident[:, :], start=True, stop=True)
                last.then_inc(s["w2_acc"], 1)
                pe.wait_ge(s["w2_ready"], 2)
                for l in range(NL):
                    for k in range(K):
                        at = ((l % 2) * K + k) * C
                        last = nc.tensor.transpose(bank[5 + l // 2][:, at:at + C],
                                                   wk[half(0), l, k, :, :].rearrange("p g i -> p (g i)"), ident[0:C, 0:C])
                last.then_inc(s["wt_acc"], 1)
                pe.wait_ge(s["modt"], 1)
                for l in range(NL):
                    last = mm(bank[2][:, l * NB:(l + 1) * NB], mw_t[:, l, :], style_t[:, :], start=True, stop=True)
                last.then_inc(s["s_acc"], 1)
                pe.wait_ge(s["s_ready"], 2)
                for l in range(NL):
                    last = mm(bank[4][:, l * NB:(l + 1) * NB], wsum_t[:, l, :], ssq[half(0), l, :], start=True, stop=True)
                last.then_inc(s["d_acc"], 1)

                pe.wait_ge(s["x8_ready"], 1)
                pe.wait_ge(s["stat_ready"], 1)
                flat = lambda t: t.rearrange("p q c -> p (q c)")
                for sh in range(3):
                    last = mm(bank[0][:, :], flat(m1[:, sh, :, :]), x8[:, :, :, sh:sh + MH].rearrange("p e b m -> p (e b) m"),
                              start=(sh == 0), stop=(sh == 2))
                last.then_inc(s["m1_acc"], 1)
                pe.wait_ge(s["y8_ready"], 1)
                for i, (q, sh) in enumerate(((0, -1), (0, 0), (1, 0), (1, 1))):
                    last = mm(bank[1 + q][:, :], flat(m2[:, i, :, :]),
                              y8[:, :, :, 1 + sh:1 + sh + MH].rearrange("p e b m -> p (e b) m"),
                              start=(i % 2 == 0), stop=(i % 2 == 1))
                last.then_inc(s["m2_acc"], 1)
                pe.wait_ge(s["z16_ready"], 1)
                for e in range(2):
                    for sh in range(3):
                        last = mm(bank[3 + e][:, :], flat(m3[:, sh, :, :]), z16[:, e, :, sh:sh + 2 * MH],
                                  start=(sh == 0), stop=(sh == 2))
                last.then_inc(s["m3_acc"], 1)
                pe.wait_ge(s["u16_ready"], 1)
                out4 = bank[0][:, 0:4 * NB].rearrange("p (b e m) -> p b e m", e=2, m=2)
                for e in range(2):
                    for i in range(4):
                        last = mm(out4[:, :, e, :], flat(m4[:, i, :, :]), u16[:, e, :, MH * e + i:MH * e + i + 3:2],
                                  start=(e == 0 and i == 0), stop=(i == 3), skip_group_check=True)
                last.then_inc(s["m4_acc"], 1)
                for i in range(2):
                    last = mm(bank[1][:, 0:NB], flat(m2[:, i, :, :]), add1[:, :], start=(i == 0), stop=(i == 1))
                last.then_inc(s["b2_acc"], 1)
                pe.wait_ge(s["b2_ready"], 1)
                for sh in range(3):
                    last = mm(bank[2][:, 0:NB], flat(m3[:, sh, :, :]), bc[0][:, :], start=(sh == 0), stop=(sh == 2))
                last.then_inc(s["b3_acc"], 1)
                pe.wait_ge(s["b3_ready"], 1)
                for i in range(4):
                    last = mm(bank[3][:, 0:NB], flat(m4[:, i, :, :]), bc[1][:, :], start=(i == 0), stop=(i == 3))
                last.then_inc(s["b4_acc"], 1)

                if ly["lora"]:
                    pe.wait_ge(s["beta_ready"], 1)
                    pe.wait_ge(zs["sel_ready"], 1)
                    for g in range(CHUNKS):
                        last = nc.tensor.transpose(bank[g // 4][:, (g % 4) * P:(g % 4 + 1) * P],
                                                   b_part[:, g * P:(g + 1) * P], ident[:, :])
                    last.then_inc(zs["bt_acc"], 1)
                    mm(bank[3][:, 0:E_ACT], lsum[:, :], sel16[:, :], start=True, stop=True)
                    for k in range(CHUNKS):
                        pos = slice(256 * (k // 2) + k % 2, 256 * (k // 2) + 256, 2)
                        mm(bank[2][:, 64 * k:64 * k + ZR], a_in[:, pos], sel[:, 0, :, :].rearrange("p e r -> p (e r)"),
                           start=(k == 0), stop=True, skip_group_check=True)
                        last = mm(bank[2][:, 64 * k + ZR:64 * k + ZR + E_ACT], r_in[:, pos], sel16[:, :],
                                  start=False, stop=True, skip_group_check=True)
                    last.then_inc(zs["ar_acc"], 1)
                    pe.wait_ge(zs["bt_ready"], 1)
                    for g in range(2):
                        last = mm(bank[4 + g][0:96, :], sel[:, :, :, :].rearrange("p g e r -> p (g e r)"),
                                  b_t[:, 512 * g:512 * g + 512], start=True, stop=True)
                    last.then_inc(zs["bb_acc"], 1)
                    pe.wait_ge(zs["ar_ready"], 1)
                    pe.wait_ge(zs["bb_ready"], 1)
                else:
                    pe.wait_ge(s["beta_ready"], 1)

                for g in range(2 * CHUNKS):
                    ec = g // 2
                    pe.wait_ge((s["f_load0"], s["f_load1"])[ec % 2], 16 * (ec // 2 + 1))
                    if g >= 2:
                        pe.wait_ge(s["fw_ready"], g - 1)
                    for k in range(4):
                        ck = 4 * (g % 2) + k
                        last = nc.tensor.transpose(bank[g % 2][:, k * P:(k + 1) * P],
                                                   f_in[ec % 2][:, 256 * (ck // 2) + ck % 2:256 * (ck // 2) + 256:2], ident[:, :])
                    last.then_inc(s["fw_acc"], 1)
                pe.wait_ge(s["fw_ready"], 2 * CHUNKS)

                flat2 = lambda t, g: t[:, 2 * g:2 * g + 2, :].rearrange("p b n -> p (b n)")

                def stage_p(j):
                    for h in range(2):
                        pe.wait_ge(s["w3_ready"], 2 * j + h + 1)
                        for g in range(2):
                            last = three(comp_ps[h][:, g * C:(g + 4) * C], w3_h[h][:, g * P:(g + 1) * P],
                                         w3_l[h][:, g * P:(g + 1) * P], flat2(dmv_h, g), flat2(dmv_l, g), g == 0, g == 1)
                        last.then_inc(s["p_acc"], 1)

                def stage_q(j):
                    for h in range(2):
                        pe.wait_ge(s["p_ready"], 2 * j + h + 1)
                        out = comp_ps[h][:, 0:4 * C].rearrange("p (r c) -> p r c", c=C)
                        ph = p_h[h][:, :].rearrange("p (a c) -> p a c", c=C)
                        pl = p_l[h][:, :].rearrange("p (a c) -> p a c", c=C)
                        for i, (t, rs) in enumerate(Q_STEPS):
                            a0, cnt = 2 * rs[0] - t + 2, len(rs)
                            src = slice(a0, a0 + 2 * cnt - 1, 2)
                            last = three(out[:, rs[0] + 2:rs[0] + 2 + cnt, :], qst_h[:, t + 2, :], qst_l[:, t + 2, :],
                                         ph[:, src, :], pl[:, src, :], i == 0, i == 3)
                        last.then_inc(s["q_acc"], 1)

                def stage_t(j, first=False):
                    for h in range(2):
                        pe.wait_ge(s["q_ready"], 2 * j + h + 1)
                        if not first:
                            pe.wait_ge(s["ct_ready"], 2 * j)
                        for ps, steps, odd in ((comp_ps[h], T_EVEN, 0), (conv_ps[h], T_ODD, 1)):
                            for i, (d, rs) in enumerate(steps):
                                u0 = (d + 2 * rs[0] + odd) // 2 + 2
                                cnt = len(rs)
                                src = slice((rs[0] + 2) * C, (rs[0] + 2 + cnt) * C)
                                last = three(ps[:, u0 * C:(u0 + cnt) * C], tst_h[:, d + 2, :], tst_l[:, d + 2, :],
                                             q_h[h][:, src], q_l[h][:, src], i == 0, i == len(steps) - 1)
                        last.then_inc(s["t_acc"], 1)

                def stage_conv(j, h):
                    pe.wait_ge(s["t_ready"], 4 * j + 2 * h + 2)
                    pe.wait_ge(s["x_ready"], 2 * j + h + 1)
                    for u in range(NSH):
                        last = three(conv_ps[h][:, :], flat(t_h[h][:, u, :, :]), flat(t_l[h][:, u, :, :]),
                                     x_h[h][:, u:u + HL], x_l[h][:, u:u + HL], u == 0, u == NSH - 1)
                    last.then_inc(s["conv_acc"], 1)

                def stage_turn(j):
                    for h in range(2):
                        pe.wait_ge(s["c_mid"], 2 * j + h + 1)
                        pe.wait_ge(s["c_edge"], 2 * j + h + 1)
                        for k in range(HL // P):
                            last = nc.tensor.transpose(conv_ps[h][:, k * P:(k + 1) * P], conv[h][:, k * P:(k + 1) * P], ident[:, :])
                        last.then_inc(s["ct_acc"], 1)

                ctf = lambda t, k: t[:, k, :, :].rearrange("p h o -> p (h o)")

                def ffn_chunk(j, k, last_one=False):
                    for e in range(2):
                        cols = slice(512 * e, 512 * e + 512)
                        last = three(ffn_ps[e][:, :], ctf(ct_h, k), ctf(ct_l, k), fw_h[:, k, cols], fw_l[:, k, cols],
                                     k == 0, k == CHUNKS - 1 and not ly["lora"])
                    if last_one and not ly["lora"]:
                        last.then_inc(s["ffn_acc"], 1)

                def ffn_begin(j):
                    pe.wait_ge(s["ct_ready"], 2 * j + 2)
                    pe.wait_ge(s["ffn_out"], ffn_outs(j))
                    if ly["lora"]:
                        nz = ZR + E_ACT
                        for k in range(CHUNKS):
                            last = three(lora_ps[:, 0:nz], ctf(ct_h, k), ctf(ct_l, k), ar_h[:, k, 0:nz], ar_l[:, k, 0:nz],
                                         k == 0, k == CHUNKS - 1)
                        last.then_inc(zs["z_acc"], 1)

                def turn_z(j):
                    if ly["lora"]:
                        pe.wait_ge(zs["zcat_ready"], j + 1)
                        nc.tensor.transpose(lora_ps[:, 64:64 + P], zcat[:, :], ident[:, :]).then_inc(zs["zt_acc"], 1)

                def ffn_end(j):
                    if ly["lora"]:
                        pe.wait_ge(zs["zt_ready"], j + 1)
                        for e in range(2):
                            last = mm(ffn_ps[e][:, :], zt[0:98, :], bb[0:98, 512 * e:512 * e + 512], start=False, stop=True,
                                      skip_group_check=True)
                        last.then_inc(s["ffn_acc"], 1)

                if ly["lora"]:
                    pe.wait_ge(zs["bias_row_moved"], 16)
                stage_p(0)
                stage_q(0)
                stage_t(0, True)
                for h in range(2):
                    stage_conv(0, h)
                stage_turn(0)
                with pe.Fori(1, NPAIR) as j:
                    stage_p(j)
                    ffn_begin(j - 1)
                    ffn_chunk(j - 1, 0)
                    stage_q(j)
                    for k in (1, 2):
                        ffn_chunk(j - 1, k)
                    stage_t(j)
                    turn_z(j - 1)
                    for k in (3, 4):
                        ffn_chunk(j - 1, k)
                    stage_conv(j, 0)
                    stage_conv(j, 1)
                    for k in (5, 6, 7):
                        ffn_chunk(j - 1, k, k == 7)
                    ffn_end(j - 1)
                    stage_turn(j)
                ffn_begin(NPAIR - 1)
                for k in range(CHUNKS):
                    ffn_chunk(NPAIR - 1, k, k == 7)
                turn_z(NPAIR - 1)
                ffn_end(NPAIR - 1)


_INS = ['x', 'cond_512', 'L0_cond_weights', 'L0_cond_biases', 'L0_cond_mod_w', 'L0_cond_mod_b', 'L0_ffn_identity',
        'L1_cond_weights', 'L1_cond_biases', 'L1_cond_mod_w', 'L1_cond_mod_b', 'L1_ffn_W_base', 'L1_ffn_b_base',
        'L1_ffn_lora_A', 'L1_ffn_lora_B', 'L1_ffn_router_W', 'L1_ffn_router_b', 'L1_ffn_domain_prior', 'L1_ffn_active']


def kernel(**inputs):
    import concourse.bacc as _bacc
    from concourse import mybir as _mybir
    from concourse.bass_utils import run_bass_kernel_spmd as _run

    nc = _bacc.Bacc("TRN2", target_bir_lowering=False, num_devices=1)
    arrays, aps = {}, {}
    for name in _INS:
        arr = np.ascontiguousarray(inputs[name])
        arrays[f"in_{name}_dram"] = arr
        aps[name] = nc.dram_tensor(f"in_{name}_dram", arr.shape, _mybir.dt.from_np(arr.dtype), kind="ExternalInput").ap()
    aps["out"] = nc.dram_tensor("out_dram", (NB, C, L), F32, kind="ExternalOutput").ap()
    build(nc, aps)
    r = _run(nc, [arrays], core_ids=[0])
    return r.results[0]["out_dram"]
```

```python
from contextlib import ExitStack

import concourse.bass as bass
import numpy as np
from concourse import mybir

ALU = mybir.AluOpType
ACT = mybir.ActivationFunctionType
F32 = mybir.dt.float32
F32R = mybir.dt.float32r
I32 = mybir.dt.int32
AX_X = mybir.AxisListType.X

NB, C, L = 64, 64, 1024
P = 128
NPAIR = NB // 2
HL = L // 2
STYLE = 128
NL, K = 4, 3
PAD = 2
NSH = 2 * PAD + 1
MINI = 8
MH = MINI // 2
CHUNKS = L // P
SCALE = 1.0 / float(np.sqrt(C * K ** 2))
EPS = 1e-8
BLUR = (0.25, 0.75)
E_TOT, E_ACT, R = 16, 4, 8
ZR = E_ACT * R
NZ = ZR + E_ACT
LORA_SCALE = 16.0 / 8.0
PRIOR_EPS = 1e-12

Q_STEPS = [(t, [r for r in range(-2, 2) if -2 <= 2 * r - t <= 2 and not (t == -2 and r == 1)]) for t in (0, -2, -1, 1)]
T_STEPS = [(0, [-2, -1, 0, 1]), (2, [-2, -1, 0, 1]), (-2, [-1, 0, 1])]


SCALES = ("s_all", "lam1", "lam2", "lam3", "lam4", "beta")
PREP, PREPS = 3, 7


def half(p):
    return slice(C * p, C * p + C)


def ffn_outs(pairs):
    return 2 * pairs + 2


def stores(pairs):
    return 16 * pairs + 16


def build(nc, a):
    with ExitStack() as ctx:
        def sb(name, shape, dt=F32):
            return ctx.enter_context(nc.sbuf_tensor(name, shape, dt))

        def sem(name):
            return ctx.enter_context(nc.semaphore(name))

        bank = [ctx.enter_context(nc.psum_tensor(f"bank{i}", [P, 512], F32)) for i in range(8)]
        comp_ps, conv_ps, ffn_ps, lora_ps = bank[0:2], bank[2:4], bank[4:6], bank[6]

        x1 = nc.dram_tensor("x1_dram", [NB, C, L], F32, kind="Internal").ap()

        modb = sb("modb", [P, NL])
        bias = sb("bias", [P, NL])
        ident = sb("ident", [P, P])

        style_t = sb("style_t", [STYLE, NB])
        ssq = sb("ssq", [P, NL, NB])
        wsum = sb("wsum", [P, NL, C])
        d_all = sb("d_all", [P, NL, NB])
        add1 = sb("add1", [P, NB])
        add2 = sb("add2", [P, NB])
        add2q = sb("add2q", [P, NB])
        add3 = sb("add3", [P, NB])
        bc = [sb(f"bc{i}", [P, NB]) for i in range(3)]

        wk = sb("wk", [P, NL, K, 2, C])
        wt = sb("wt", [P, NL, K, C])
        blur_n = sb("blur_n", [P, 6, C])
        blur_t = sb("blur_t", [P, 2, 6, C])
        sta = sb("sta", [P, 13, 2, C])
        qst, tst, dmv = sta[:, 0:4], sta[:, 4:9], sta[:, 9:13].rearrange("p (g b) q c -> p g (b q) c", g=2)
        mst = sb("mst", [P, 14, 2, C])
        m1, m2, m3, m4 = mst[:, 0:3], mst[:, 3:7], mst[:, 7:10], mst[:, 10:14]
        pst = sb("pst", [P, 2, 2, C])
        qst_h, qst_l = sb("qst_h", [P, 4, P], F32R), sb("qst_l", [P, 4, P], F32R)
        tst_h, tst_l = sb("tst_h", [P, 5, P], F32R), sb("tst_l", [P, 5, P], F32R)
        dmv_h, dmv_l = sb("dmv_h", [P, 4, P], F32R), sb("dmv_l", [P, 4, P], F32R)

        ends = sb("ends", [P, NPAIR, 2, MINI])
        win = [sb(f"win{i}", [P, 2 * NB * (2 * MH + 2)]) for i in range(2)]
        x8, y8 = (w[:, 0:2 * NB * (MH + 2)].rearrange("p (e b m) -> p e b m", e=2, b=NB) for w in win)
        z16, u16 = (w[:, :].rearrange("p (e b m) -> p e b m", e=2, b=NB) for w in win)
        mtmp = sb("mtmp", [P, 512])
        wsum_t = mtmp[0:C, :].rearrange("i (l o) -> i l o", l=NL)
        dtmp = ssq
        dvar = wsum
        dsq = mtmp[:, 0:NL * NB].rearrange("p (l b) -> p l b", l=NL)
        style_in = mtmp[0:NB, 0:STYLE]
        edge = sb("edge", [P, NB, 2, 2])

        f_in = [sb(f"f_in{i}", [P, L]) for i in range(2)]
        fw_h = sb("fw_h", [P, CHUNKS, L], F32R)
        fw_l = sb("fw_l", [P, CHUNKS, L], F32R)

        xraw = sb("xraw", [P, 2, L])
        xres = sb("xres", [P, L])
        xout = sb("xout", [P, L])
        x_h = [sb(f"x_h{h}", [P, HL + 2 * PAD], F32R) for h in range(2)]
        x_l = [sb(f"x_l{h}", [P, HL + 2 * PAD], F32R) for h in range(2)]
        w3_h = [sb(f"w3_h{h}", [P, 2 * P], F32R) for h in range(2)]
        w3_l = [sb(f"w3_l{h}", [P, 2 * P], F32R) for h in range(2)]
        p_h, p_l = sb("p_h", [P, 2, 5, C], F32R), sb("p_l", [P, 2, 5, C], F32R)
        q_h, q_l = sb("q_h", [P, 2, 4 * C], F32R), sb("q_l", [P, 2, 4 * C], F32R)
        tw = [sb(f"tw{h}", [P, 2, NSH, 2, C], F32R) for h in range(2)]
        conv_buf = sb("conv_buf", [P, 2, HL])
        conv = [conv_buf[:, h, :] for h in range(2)]
        w_in = win[0][:, 0:NL * C * K].rearrange("p (l i k) -> p l i k", l=NL, k=K)
        mw_in = win[0][:, NL * C * K:NL * C * K + NL * STYLE].rearrange("p (l s) -> p l s", l=NL)
        wsq = win[1][:, 0:NL * C * K].rearrange("p (l i k) -> p l i k", l=NL, k=K)
        mw_t = win[1][:, NL * C * K:NL * C * K + NL * P].rearrange("p (l c) -> p l c", l=NL)
        ct_h = sb("ct_h", [P, CHUNKS, 2, C], F32R)
        ct_l = sb("ct_l", [P, CHUNKS, 2, C], F32R)

        act_i = sb("act_i", [P, E_ACT], I32)
        act_f = sb("act_f", [P, E_ACT])
        act_m = sb("act_m", [P, E_ACT])
        pidx_i = sb("pidx_i", [P, 2], I32)
        pidx = sb("pidx", [P, 3])
        rr_i = sb("rr_i", [P, E_ACT, R], I32)
        rr = sb("rr", [P, E_ACT, R])
        sel = sb("sel", [P, 3, E_ACT, R])
        sel_e = sb("sel_e", [P, E_ACT])
        sel16 = sb("sel16", [E_TOT, E_ACT])
        rb_in = sb("rb_in", [E_TOT, 1])
        pr_in = sb("pr_in", [E_TOT, 1])
        lnp = sb("lnp", [E_TOT, 1])
        lsum = sb("lsum", [E_TOT, P])
        const4 = sb("const4", [P, E_ACT])
        ar = sb("ar", [P, CHUNKS, 2 * NZ], F32R)
        fold = sb("fold", [2 * NZ, NZ])
        z_sum = sb("z_sum", [2 * NZ, P])
        bb = sb("bb", [P, L], F32R)
        b_part = win[1][:, 0:L]
        b_pack = b_part.rearrange("p (g e r) -> p g e r", g=CHUNKS, e=E_TOT)
        a_in, r_in, bias_in = f_in[0][:, :], win[0][0:E_TOT, 0:L], win[0][96:97, 0:L]
        b_in = f_in[1][:, :].rearrange("p (e g r) -> p e g r", e=E_TOT, g=CHUNKS)
        b_t = f_in[1]
        gate = sb("gate", [P, 16])
        za = sb("za", [P, ZR])
        zcat = sb("zcat", [P, P])
        zt = sb("zt", [P, P], F32R)

        layers = [
            dict(x=a["x"], out=x1, w=a["L0_cond_weights"], b=a["L0_cond_biases"],
                            mw=a["L0_cond_mod_w"], mb=a["L0_cond_mod_b"], f=a["L0_ffn_identity"], lora=False),
            dict(x=x1, out=a["out"], w=a["L1_cond_weights"], b=a["L1_cond_biases"],
                            mw=a["L1_cond_mod_w"], mb=a["L1_cond_mod_b"], f=a["L1_ffn_W_base"], lora=True),
        ]
        names = ("params ends f_load0 f_load1 modt_acc modt s_acc s_ready w2_acc w2_ready d_acc dvar_ready dsqrt "
                 "wt_acc wt_ready x8_ready m1_acc y8_ready m2_acc z16_ready m3_acc u16_ready "
                 "m4_acc edge_ready bias_acc bias_ready fw_acc fw_hi fw_ready chain "
                 "x_load res_load x_hi x_ready w3_hi w3_ready p_acc p_hi p_ready q_acc q_hi q_ready t_acc t_hi "
                 "t_ready blur_ready mst_ready split_hi split_ready t_lo conv_acc c_mid c_edge ct_acc ct_hi ct_ready ffn_acc ffn_out stored").split()
        for n, ly in enumerate(layers):
            ly["s"] = {k: sem(f"{k}_{n}") for k in names}
            ly["s_all"] = sb(f"s_all{n}", [P, NL, NB])
            for k, width in (("lam1", NB), ("lam2", NB), ("lam3", NB + 2), ("lam4", NB), ("beta", NB)):
                ly[k] = sb(f"{k}_{n}", [P, width])
        zs = {k: sem(k) for k in (
            "style_acc pack_ready lora_in ident_made iota_made bias_row_moved ln_in ln_ready sel_ready bt_acc bt_ready ar_acc "
            "lora_late ar_ready bb_acc bb_ready z_acc logit_ready exp_ready zcat_ready zt_acc zt_ready zeroed sta_zero fold_made z_out fold_acc").split()}

        block = ctx.enter_context(nc.Block())

        @block.sync
        def _(sp):
            def load_params(ly):
                s = ly["s"]
                for g in range(2):
                    sp.dma_start(w_in[half(g)], ly["w"].rearrange("l o i k -> o l i k")).then_inc(s["params"], 16)
                    sp.dma_start(mw_in[half(g)], ly["mw"].rearrange("l c s -> c l s")).then_inc(s["params"], 16)
                    sp.dma_start(modb[half(g)], ly["mb"].rearrange("l c -> c l"), allow_slow_non_contiguous=True).then_inc(s["params"], 16)
                    sp.dma_start(bias[half(g)], ly["b"].rearrange("l c -> c l"), allow_slow_non_contiguous=True).then_inc(s["params"], 16)

            def load_lora():
                for dst, src in ((act_i[:, :], a["L1_ffn_active"].unsqueeze(0).broadcast_to([P, E_ACT])),
                                 (a_in, a["L1_ffn_lora_A"].rearrange("e r h -> (e r) h")),
                                 (b_in, a["L1_ffn_lora_B"].rearrange("e (p g) r -> p e g r", g=CHUNKS)),
                                 (rb_in[:, :], a["L1_ffn_router_b"].unsqueeze(1)),
                                 (pr_in[:, :], a["L1_ffn_domain_prior"].unsqueeze(1))):
                    sp.dma_start(dst, src).then_inc(zs["lora_in"], 16)

            def load_f(ly, ec):
                sp.dma_start(f_in[ec % 2][:, :], ly["f"][ec * P:(ec + 1) * P, :]
                             ).then_inc((ly["s"]["f_load0"], ly["s"]["f_load1"])[ec % 2], 16)

            def load_x(ly, j):
                x_pair = ly["x"].rearrange("(j h) c l -> j c h l", h=2)
                sp.dma_start(xraw[half(0)], x_pair[j]).then_inc(ly["s"]["x_load"], 16)
                sp.dma_start(xraw[half(1), :, 0:L - 1], x_pair[j, :, :, 1:L]).then_inc(ly["s"]["x_load"], 16)

            def rows(t):
                return t.rearrange("(j h) c l -> j (h c) l", h=2)

            def load_res(ly, j):
                sp.dma_start(xres[:, :], rows(ly["x"])[j]).then_inc(ly["s"]["res_load"], 16)

            def store(ly, j):
                sp.dma_start(rows(ly["out"])[j], xout[:, :]).then_inc(ly["s"]["stored"], 16)

            first, second = layers
            sp.dma_start(style_in, a["cond_512"]).then_inc(first["s"]["params"], 16)
            load_params(first)
            for n, ly in enumerate(layers):
                s = ly["s"]
                sp.sem_inc(s["stored"], 16)
                if n:
                    sp.wait_ge(first["s"]["stored"], stores(NPAIR))
                for e in range(2):
                    sp.dma_start(ends[:, :, e, :], rows(ly["x"])[:, :, e * (L - MINI):e * (L - MINI) + MINI]
                                 .rearrange("j r l -> r j l")).then_inc(s["ends"], 16)
                if not n:
                    for ec in range(2):
                        load_f(ly, ec)
                    load_x(ly, 0)
                for ec in range(2, CHUNKS):
                    sp.wait_ge(s["fw_acc"], 2 * (ec - 1))
                    load_f(ly, ec)
                    if ec == 3:
                        sp.wait_ge(s["x_ready"], 2)
                        load_x(ly, 1)
                        load_res(ly, 0)
                if not n:
                    sp.wait_ge(s["edge_ready"], 1)
                    load_params(second)
                    sp.wait_ge(s["fw_acc"], 2 * CHUNKS)
                    load_lora()
                with sp.Fori(2, NPAIR) as j:
                    sp.wait_ge(s["x_ready"], 2 * j)
                    load_x(ly, j)
                    sp.wait_ge(s["ffn_out"], ffn_outs(j - 1))
                    store(ly, j - 2)
                    load_res(ly, j - 1)
                sp.wait_ge(s["ffn_out"], ffn_outs(NPAIR - 1))
                store(ly, NPAIR - 2)
                load_res(ly, NPAIR - 1)
                if not n:
                    sp.wait_ge(s["x_ready"], 2 * NPAIR)
                    sp.wait_ge(s["stored"], stores(1))
                    load_x(second, 0)
                    sp.wait_ge(zs["bb_ready"], 1)
                    sp.dma_start(bb[97:98, :].bitcast(F32), b_part[96:97, :]).then_inc(zs["bias_row_moved"], 16)
                    for ec in range(2):
                        load_f(second, ec)
                sp.wait_ge(s["ffn_out"], ffn_outs(NPAIR))
                store(ly, NPAIR - 1)
            sp.wait_ge(s["stored"], stores(NPAIR))

        @block.gpsimd
        def _(pool):
            nc.gpsimd.memset(ident[:, :], 0.0).then_inc(zs["ident_made"], 1)
            pool.wait_ge(zs["ident_made"], 1)
            nc.gpsimd.affine_select(out=ident[:, :], in_=ident[:, :], compare_op=ALU.not_equal, fill=1.0, base=0,
                                    pattern=[[-1, P]], channel_multiplier=1).then_inc(zs["ident_made"], 1)
            nc.gpsimd.iota(pidx_i[:, 0:1], [[0, 1]], base=0, channel_multiplier=1).then_inc(zs["iota_made"], 1)
            nc.gpsimd.iota(rr_i[:, :, :], [[0, E_ACT], [1, R]], base=0, channel_multiplier=0).then_inc(zs["iota_made"], 1)
            for h in range(2):
                for t in (x_h[h], x_l[h]):
                    nc.gpsimd.memset(t[:, 0:PAD].bitcast(F32), 0.0)
                    nc.gpsimd.memset(t[:, PAD + HL:2 * PAD + HL].bitcast(F32), 0.0)
            nc.gpsimd.memset(sta[:, :, :, :], 0.0).then_inc(zs["sta_zero"], 1)
            nc.gpsimd.memset(mst[:, :, :, :], 0.0).then_inc(zs["sta_zero"], 1)
            nc.gpsimd.memset(fold[:, :], 0.0).then_inc(zs["fold_made"], 1)
            for g in range(2):
                pool.wait_ge(zs["fold_made"], g + 1)
                nc.gpsimd.affine_select(out=fold[:, :], in_=fold[:, :], compare_op=ALU.not_equal, fill=1.0, base=-NZ * g,
                                        pattern=[[-1, NZ]], channel_multiplier=1).then_inc(zs["fold_made"], 1)
            for ly in layers:
                s = ly["s"]

                def split_low(j, h):
                    src = xraw[:, h, :].rearrange("p (m q) -> p m q", q=2)[:, :, 0]
                    pool.wait_ge(s["x_hi"], 2 * j + h + 1)
                    nc.gpsimd.tensor_tensor(x_l[h][:, PAD:PAD + HL], src, x_h[h][:, PAD:PAD + HL].bitcast(F32),
                                            ALU.subtract).then_inc(s["x_ready"], 1)

                def put_edge(j, h):
                    dst = conv[h][:, :]
                    dst = bass.AP(dst.tensor, dst.offset, [list(dst.ap[0]), [HL - 2, 2], [1, 2]])
                    nc.gpsimd.tensor_copy(dst, edge[:, bass.ds(2 * j + h, 1), :, :].rearrange("p b g m -> p (b g) m")
                                          ).then_inc(s["c_edge"], 1)

                def body(j, first=False):
                    split_low(j, 0)
                    split_low(j, 1)
                    if first:
                        pool.wait_ge(s["edge_ready"], 1)
                        if ly is not layers[0]:
                            pool.wait_ge(layers[0]["s"]["ct_acc"], 2 * NPAIR)
                    else:
                        pool.wait_ge(s["ct_acc"], 2 * j)
                    put_edge(j, 0)
                    put_edge(j, 1)

                for i, (at, hi, lo) in enumerate(((9, dmv_h, dmv_l), (0, qst_h, qst_l), (4, tst_h, tst_l))):
                    pool.wait_ge(s["split_hi"], i + 1)
                    nc.gpsimd.tensor_tensor(lo[:, :, :], sta[:, at:at + hi.shape[1]].rearrange("p a q c -> p a (q c)"),
                                            hi[:, :, :].bitcast(F32), ALU.subtract).then_inc(s["split_ready"], 1)
                body(0, True)
                with pool.Fori(1, NPAIR) as j:
                    body(j)

        @block.scalar
        def _(act):
            def prep_wt(ly, g):
                act.wait_ge(ly["s"]["wt_acc"], g + 1)
                nc.scalar.copy(wt[:, 2 * g:2 * g + 2, :, :], bank[7][:, 0:2 * K * C].rearrange("p (l k o) -> p l k o", l=2, k=K)
                               ).then_inc(ly["s"]["wt_ready"], 1)

            def prep_sqrt(ly):
                act.wait_ge(ly["s"]["dvar_ready"], 1)
                nc.scalar.activation(dsq, dvar[:, :, :], ACT.Sqrt).then_inc(ly["s"]["dsqrt"], 1)
                prep_wt(ly, 1)

            def prep_mst(ly):
                act.wait_ge(zs["sta_zero"], 2)
                act.wait_ge(ly["s"]["wt_ready"], 2)
                m13 = mst[:, :, :, :].rearrange("p (g i) q c -> p g i q c", g=2)[:, :, 0:3]
                for p in range(2):
                    nc.scalar.copy(m13[half(p), :, 1, p, :], wt[half(p), 0::2, 1, :])
                    nc.scalar.copy(m13[half(p), :, 1 - p:3 - p, 1 - p, :], wt[half(p), 0::2, 0::2, :])
                act.wait_ge(ly["s"]["blur_ready"], 2)
                for p in range(2):
                    nc.scalar.copy(m2[half(p), p:p + 3, :, :].rearrange("p i z c -> p (i z c)"),
                                   blur_n[half(p), :, :].rearrange("p n c -> p (n c)"))
                    for q in range(2):
                        last = nc.scalar.copy(m4[half(p), q:q + 3, q, :], blur_t[half(p), 1, p::2, :])
                last.then_inc(ly["s"]["mst_ready"], 1)

            def prep_prior():
                act.wait_ge(zs["ln_in"], 1)
                nc.scalar.activation(lnp[:, :], gate[0:E_TOT, 0:1], ACT.Ln).then_inc(zs["ln_ready"], 1)
                nc.scalar.activation(gate[0:E_TOT, 2:3], gate[0:E_TOT, 1:2], ACT.Exp, scale=0.0)

            def prep_late_loads(ly):
                act.wait_ge(ly["s"]["w2_ready"], 2)
                act.wait_ge(ly["s"]["modt_acc"], 1)
                nc.scalar.dma_start(r_in, a["L1_ffn_router_W"]).then_inc(zs["lora_late"], 16)
                nc.scalar.dma_start(bias_in, a["L1_ffn_b_base"].unsqueeze(0)).then_inc(zs["lora_late"], 16)

            def prep(i):
                ly = layers[1]
                if i == 1:
                    prep_late_loads(ly)
                    prep_wt(ly, 0)
                elif i == 2:
                    prep_sqrt(ly)
                elif i == 4:
                    prep_mst(ly)
                elif i == 5:
                    prep_prior()

            for n, ly in enumerate(layers):
                s = ly["s"]
                s_all, lam1, lam2, lam3, lam4, beta = (ly[k] for k in SCALES)
                if n == 0:
                    prep_wt(ly, 0)
                    prep_sqrt(ly)
                    prep_mst(ly)

                def fw_high(g0, g1):
                    for g in range(g0, g1):
                        act.wait_ge(s["fw_acc"], g + 1)
                        dst = fw_h[:, 4 * (g % 2):4 * (g % 2) + 4, (g // 2) * P:(g // 2 + 1) * P]
                        nc.scalar.copy(dst, bank[6 + g % 2][:, :].rearrange("p (k e) -> p k e", k=4)).then_inc(s["fw_hi"], 1)

                def w3_high(j, h):
                    nc.scalar.activation(w3_h[h][:, :], pst[:, :, :, :].rearrange("p a q c -> p (a q c)"), ACT.Copy,
                                         scale=lam3[:, bass.ds(2 * j + h, 1)]).then_inc(s["w3_hi"], 1)

                def x_high(j, first=False):
                    act.wait_ge(s["x_load"], 32 * j + 32)
                    if not first:
                        act.wait_ge(s["conv_acc"], 2 * j)
                    for h in range(2):
                        nc.scalar.copy(x_h[h][:, PAD:PAD + HL],
                                       xraw[:, h, :].rearrange("p (m q) -> p m q", q=2)[:, :, 0]).then_inc(s["x_hi"], 1)

                def compose_high(j, first=False, lora=False):
                    for h in range(2):
                        act.wait_ge(s["p_acc"], 2 * j + h + 1)
                        nc.scalar.activation(p_h[:, h, :, :].rearrange("p a c -> p (a c)"), comp_ps[h][:, 0:5 * C], ACT.Copy,
                                             scale=lam2[:, bass.ds(2 * j + h, 1)]).then_inc(s["p_hi"], 1)
                    if first:
                        fw_high(0, 2)
                    if lora:
                        act.wait_ge(zs["z_acc"], j)
                        nc.scalar.copy(z_sum[:, :], lora_ps[0:2 * NZ, 0:P]).then_inc(zs["z_out"], 1)
                    act.wait_ge(s["q_acc"], j + 1)
                    for h in range(2):
                        nc.scalar.activation(q_h[:, h, :], comp_ps[0][:, 4 * C * h:4 * C * (h + 1)], ACT.Copy,
                                             scale=lam1[:, bass.ds(2 * j + h, 1)]).then_inc(s["q_hi"], 1)
                    if first:
                        fw_high(2, 4)
                    if lora:
                        gate_exp(j - 1)
                    for h in range(2):
                        w3_high(j + 1, h)
                    x_high(j, first)
                    for h in range(2):
                        act.wait_ge(s["t_acc"], 2 * j + h + 1)
                        nc.scalar.activation(tw[h][:, 0, :, 0, :], comp_ps[h][:, 0:NSH * C].rearrange("p (u c) -> p u c", c=C),
                                             ACT.Copy, scale=s_all[:, 0, bass.ds(2 * j + h, 1)]).then_inc(s["t_hi"], 1)
                    if lora:
                        zt_out(j - 1)

                def conv_out(j, first=False, step=None):
                    for h in range(2):
                        act.wait_ge(s["conv_acc"], 2 * j + h + 1)
                        nc.scalar.activation(conv[h][:, 2:HL - 2], conv_ps[h][:, 2:HL - 2], ACT.Identity,
                                             scale=lam4[:, bass.ds(2 * j + h, 1)],
                                             bias=beta[:, bass.ds(2 * j + h, 1)]).then_inc(s["c_mid"], 1)
                        if not h and step is not None:
                            prep(step)
                    if first:
                        fw_high(4, 2 * CHUNKS)
                    for part, ks in enumerate((slice(0, 6), slice(6, 8))):
                        if part and not first:
                            act.wait_ge(s["ffn_acc"], 2 * j)
                        for h in range(2):
                            if part:
                                act.wait_ge(s["ct_ready"], 4 * j + h + 1)
                            else:
                                act.wait_ge(s["ct_acc"], 2 * j + h + 1)
                            nc.scalar.copy(ct_h[:, ks, h, :],
                                           conv_ps[h][:, :].rearrange("p (k o) -> p k o", o=C)[:, ks, :]).then_inc(s["ct_hi"], 1)

                def gate_exp(j):
                    act.wait_ge(zs["logit_ready"], j + 1)
                    nc.scalar.activation(gate[:, 8:12], gate[:, 4:8], ACT.Exp).then_inc(zs["exp_ready"], 1)

                def zt_out(j):
                    act.wait_ge(zs["zt_acc"], j + 1)
                    nc.scalar.copy(zt[0:98, :], lora_ps[0:98, 256:256 + P]).then_inc(zs["zt_ready"], 1)

                act.wait_ge(s["split_hi"], 1)
                for h in range(2):
                    w3_high(0, h)
                compose_high(0, True)
                act.wait_ge(s["bias_ready"], 3)
                conv_out(0, True)
                if n == 0:
                    with act.Fori(1, PREP) as j:
                        compose_high(j)
                        conv_out(j)
                    for step in range(PREPS):
                        compose_high(PREP + step)
                        conv_out(PREP + step, False, step)
                with act.Fori(1 if n else PREP + PREPS, NPAIR) as j:
                    compose_high(j, False, ly["lora"])
                    conv_out(j)
                if ly["lora"]:
                    act.wait_ge(zs["z_acc"], NPAIR)
                    nc.scalar.copy(z_sum[:, :], lora_ps[0:2 * NZ, 0:P]).then_inc(zs["z_out"], 1)
                    gate_exp(NPAIR - 1)
                    zt_out(NPAIR - 1)

        @block.vector
        def _(dve):
            v = nc.vector
            stt = v.scalar_tensor_tensor
            steps_done = [0, 0]

            def linker(n):
                def link(ins):
                    steps_done[n] += 1
                    ins.then_inc(layers[n]["s"]["chain"], 1)
                    dve.wait_ge(layers[n]["s"]["chain"], steps_done[n])
                return link

            def prep_squares(ly, link):
                s = ly["s"]
                dve.wait_ge(s["params"], 16 * (8 if ly["lora"] else 9))
                link(v.tensor_tensor(wsq[:, :, :, :], w_in[:, :, :, :], w_in[:, :, :, :], ALU.mult))
                v.tensor_reduce(wsum[:, :, :].rearrange("p l i -> p (l i)"),
                                wsq[:, :, :, :].rearrange("p l i k -> p (l i) k"), AX_X, ALU.add).then_inc(s["w2_ready"], 1)
                for l in range(NL):
                    for g in range(2):
                        last = v.tensor_copy(wk[:, l, :, g, :], w_in[:, l, :, :].rearrange("p i k -> p k i"))
                last.then_inc(s["w2_ready"], 1)

            def prep_turned(ly, link):
                s = ly["s"]
                if not ly["lora"]:
                    dve.wait_ge(zs["style_acc"], 1)
                    v.tensor_copy(style_t[:, :], bank[5][:, 0:NB])
                dve.wait_ge(s["modt_acc"], 1)
                v.tensor_copy(mw_t, bank[6][:, :].rearrange("p (l c) -> p l c", l=NL)).then_inc(s["modt"], 1)
                dve.wait_ge(s["w2_acc"], 1)
                v.tensor_copy(wsum_t[:, :, :], bank[7][0:C, :].rearrange("p (l o) -> p l o", l=NL)).then_inc(s["modt"], 1)

            def prep_styles(ly, link):
                s, s_all = ly["s"], ly["s_all"]
                dve.wait_ge(s["s_acc"], 1)
                link(v.tensor_tensor(s_all[:, :, :], bank[6][:, 0:NL * NB].rearrange("p (l b) -> p l b", l=NL),
                                     modb[:, :].unsqueeze(2).broadcast_to([P, NL, NB]), ALU.add))
                v.tensor_tensor(ssq[:, :, :], s_all[:, :, :], s_all[:, :, :], ALU.mult).then_inc(s["s_ready"], 1)

            def prep_scales(ly, link):
                s = ly["s"]
                s_all, lam1, lam2, lam3, lam4, beta = (ly[k] for k in SCALES)
                dve.wait_ge(s["d_acc"], 1)
                v.tensor_scalar(dvar[:, :, :], bank[6][:, 0:NL * NB].rearrange("p (l b) -> p l b", l=NL),
                                SCALE * SCALE, EPS, ALU.mult, ALU.add).then_inc(s["dvar_ready"], 1)
                dve.wait_ge(s["dsqrt"], 1)
                link(v.reciprocal(dsq, dsq))
                link(v.tensor_tensor(dtmp[:, :, :], dsq, dsq, ALU.mult))
                link(v.tensor_tensor(dtmp[:, :, :], dtmp[:, :, :], dvar[:, :, :], ALU.mult))
                link(v.tensor_scalar(dtmp[:, :, :], dtmp[:, :, :], -0.5, 1.5, ALU.mult, ALU.add))
                link(v.tensor_tensor(d_all[:, :, :], dtmp[:, :, :], dsq, ALU.mult))
                stt(out=lam1[:, :], in0=d_all[:, 0, :], scalar=SCALE, in1=d_all[:, 1, :], op0=ALU.mult, op1=ALU.mult)
                stt(out=lam2[:, :], in0=s_all[:, 1, :], scalar=SCALE, in1=s_all[:, 2, :], op0=ALU.mult, op1=ALU.mult)
                stt(out=lam3[:, 0:NB], in0=d_all[:, 2, :], scalar=SCALE, in1=s_all[:, 3, :], op0=ALU.mult, op1=ALU.mult)
                v.tensor_scalar(lam4[:, :], d_all[:, 3, :], 0.5 * SCALE, None, ALU.mult)
                v.tensor_scalar(add1[:, :], d_all[:, 1, :], bias[:, 0:1], None, ALU.mult)
                v.tensor_scalar(add2[:, :], s_all[:, 2, :], bias[:, 1:2], 2.0, ALU.mult, ALU.mult)
                v.tensor_scalar(add2q[:, :], s_all[:, 2, :], bias[:, 1:2], 0.25, ALU.mult, ALU.mult)
                link(v.tensor_scalar(add3[:, :], s_all[:, 3, :], bias[:, 2:3], None, ALU.mult))

            def prep_stationaries(ly, link):
                s = ly["s"]
                taps_n = lambda a, b: blur_n[:, a:b, :]
                taps_t = lambda a, b: (blur_t[:, :, a:b, :].rearrange("p l (j n) c -> p l j (n c)", j=2) if b - a == 6
                                       else blur_t[:, :, a:b, :].rearrange("p l n c -> p l (n c)"))
                dve.wait_ge(s["wt_ready"], 2)
                w13 = wt[:, 1::2, :, :].rearrange("p l k c -> p l (k c)")
                link(v.tensor_scalar(taps_t(0, 6), w13.unsqueeze(2).broadcast_to([P, 2, 2, K * C]), BLUR[0], None, ALU.mult))
                link(stt(out=taps_t(1, 4), in0=w13, scalar=BLUR[1], in1=taps_t(1, 4), op0=ALU.mult, op1=ALU.add))
                stt(out=taps_t(2, 5), in0=w13, scalar=BLUR[1], in1=taps_t(2, 5), op0=ALU.mult, op1=ALU.add
                    ).then_inc(s["blur_ready"], 1)
                w1n = wk[:, 1, :, 0, :]
                for g in range(2):
                    last = v.tensor_scalar(blur_n[:, 3 * g:3 * g + 3, :], w1n, BLUR[0], None, ALU.mult)
                link(last)
                link(stt(out=taps_n(1, 4), in0=w1n, scalar=BLUR[1], in1=taps_n(1, 4), op0=ALU.mult, op1=ALU.add))
                stt(out=taps_n(2, 5), in0=w1n, scalar=BLUR[1], in1=taps_n(2, 5), op0=ALU.mult, op1=ALU.add
                    ).then_inc(s["blur_ready"], 1)
                dve.wait_ge(s["blur_ready"], 2)
                dve.wait_ge(zs["sta_zero"], 1)
                if ly["lora"]:
                    dve.wait_ge(layers[0]["s"]["split_ready"], 3)
                for p in range(2):
                    v.tensor_copy(dmv[half(p), :, p:p + 3, :], blur_t[half(p), 1, :, :].rearrange("p (i a) c -> p a i c", a=2))
                    for h in range(2):
                        v.tensor_copy(qst[half(p), h:h + 3, h, :], blur_t[half(p), 0, p::2, :])
                    for q in range(2):
                        last = v.tensor_copy(tst[half(p), 1 + p - q:4 + p - q, q, :], wk[half(p), 0, :, 0, :])
                link(last)

            def prep_split(ly, link):
                for p in range(2):
                    v.tensor_copy(pst[half(p), 1 - p, :, :], wk[half(p), 2, p:p + 2, 0, :])
                    last = v.tensor_copy(pst[half(p), p, 1 - p, :], wk[half(p), 2, 2 * p, 0, :])
                link(last)
                for at, hi in ((9, dmv_h), (0, qst_h), (4, tst_h)):
                    v.tensor_copy(hi[:, :, :], sta[:, at:at + hi.shape[1]].rearrange("p a q c -> p a (q c)")
                                  ).then_inc(ly["s"]["split_hi"], 1)

            def prep_bias(ly, link, i):
                s = ly["s"]
                dve.wait_ge(s["bias_acc"], i + 1)
                lam, add, dst = ((ly["lam2"][:, :], add2[:, :], bc[0]), (ly["lam3"][:, 0:NB], add3[:, :], bc[1]),
                                 (ly["lam4"][:, :], bias[:, 3:4].broadcast_to([P, NB]), ly["beta"]))[i]
                link(v.tensor_tensor(bc[2][:, :], bank[6][:, 0:NB], lam, ALU.mult))
                v.tensor_tensor(dst[:, :], bc[2][:, :], add, ALU.add).then_inc(s["bias_ready"], 1)

            def prep_chosen(link):
                dve.wait_ge(zs["lora_in"], 16 * 5)
                dve.wait_ge(zs["iota_made"], 2)
                v.tensor_copy(b_pack, b_in.rearrange("p e g r -> p g e r")).then_inc(zs["pack_ready"], 1)
                link(v.tensor_copy(act_f[:, :], act_i[:, :]))
                link(v.tensor_scalar(act_m[:, :], act_f[:, :], 0.0, float(E_TOT), ALU.is_lt, ALU.mult))
                link(v.tensor_tensor(act_f[:, :], act_f[:, :], act_m[:, :], ALU.add))
                link(v.tensor_scalar(act_f[:, :], act_f[:, :], 0.0, float(E_TOT - 1), ALU.max, ALU.min))
                link(v.tensor_scalar(pidx_i[:, 1:2], pidx_i[:, 0:1], 3, None, ALU.logical_shift_right))
                link(v.tensor_copy(pidx[:, 0:2], pidx_i[:, 0:2]))
                link(stt(out=pidx[:, 2:3], in0=pidx[:, 1:2], scalar=-float(R), in1=pidx[:, 0:1], op0=ALU.mult, op1=ALU.add))
                link(v.tensor_copy(rr[:, :, :], rr_i[:, :, :]))
                link(v.tensor_scalar(sel_e[:, :], act_f[:, :], pidx[:, 1:2], None, ALU.is_equal))
                v.tensor_scalar(sel16[:, :], act_f[0:E_TOT, :], pidx[0:E_TOT, 0:1], None, ALU.is_equal)
                for g in range(3):
                    stt(out=sel[:, g, :, :], in0=rr[:, :, :], scalar=pidx[:, 2:3],
                        in1=sel_e[:, :].unsqueeze(2).broadcast_to([P, E_ACT, R]), op0=ALU.is_equal, op1=ALU.mult)
                link(v.tensor_scalar(gate[0:E_TOT, 0:1], pr_in[:, :], PRIOR_EPS, None, ALU.add))
                v.tensor_copy(gate[0:E_TOT, 1:2], gate[0:E_TOT, 0:1]).then_inc(zs["ln_in"], 1)

            def prep_b_turned(g):
                dve.wait_ge(zs["bt_acc"], g + 1)
                v.tensor_copy(b_t[:, :].rearrange("e (p g) -> e g p", g=CHUNKS)[:, 4 * g:4 * g + 4, :],
                              bank[7][:, :].rearrange("e (g p) -> e g p", g=4)).then_inc(zs["bt_ready"], 1)

            def prep_prior(link):
                dve.wait_ge(zs["ln_ready"], 1)
                link(v.tensor_tensor(lnp[:, :], lnp[:, :], rb_in[:, :], ALU.add))
                v.tensor_copy(lsum[:, :], lnp[:, :].broadcast_to([E_TOT, P])).then_inc(zs["sel_ready"], 1)

            def prep_rows(link):
                dve.wait_ge(zs["ar_acc"], 1)
                ar_ps = bank[7][:, :].rearrange("p (k n) -> p k n", k=CHUNKS)[:, :, 0:NZ]
                link(v.tensor_copy(ar[:, :, 0:NZ], ar_ps))
                v.tensor_tensor(ar[:, :, NZ:2 * NZ], ar_ps, ar[:, :, 0:NZ].bitcast(F32), ALU.subtract)
                v.tensor_copy(const4[:, :], bank[6][:, 256:256 + E_ACT]).then_inc(zs["ar_ready"], 1)

            def prep_b_rows(link):
                dve.wait_ge(zs["bb_acc"], 1)
                for g in range(2):
                    cols = slice(512 * g, 512 * g + 512)
                    v.tensor_copy(bb[0:64, cols], bank[6 + g][0:64, :])
                    link(v.tensor_copy(b_part[64:96, cols].bitcast(F32R), bank[6 + g][64:96, :]))
                    v.tensor_tensor(bb[64:96, cols], bank[6 + g][64:96, :], b_part[64:96, cols], ALU.subtract)
                dve.wait_ge(zs["lora_late"], 32)
                link(v.tensor_copy(bb[96:97, :], bias_in))
                v.tensor_tensor(b_part[96:97, :], bias_in, bb[96:97, :].bitcast(F32), ALU.subtract).then_inc(zs["bb_ready"], 1)

            def prep(i):
                ly, link = layers[1], linker(1)
                if i == 0:
                    prep_squares(ly, link)
                elif i == 1:
                    prep_turned(ly, link)
                    prep_styles(ly, link)
                elif i == 2:
                    prep_scales(ly, link)
                elif i == 3:
                    prep_stationaries(ly, link)
                elif i == 4:
                    prep_chosen(link)
                elif i == 5:
                    prep_bias(ly, link, 0)
                    prep_b_turned(0)
                    prep_bias(ly, link, 1)
                    prep_b_turned(1)
                    prep_prior(link)
                elif i == 6:
                    prep_bias(ly, link, 2)
                    prep_rows(link)
                    prep_b_rows(link)

            for n, ly in enumerate(layers):
                s = ly["s"]
                s_all, lam1, lam2, lam3, lam4, beta = (ly[k] for k in SCALES)
                link = linker(n)
                dve.sem_inc(s["ffn_out"], 2)
                if n == 0:
                    for t in (pst[:, :, :, :], layers[0]["lam3"][:, :], layers[1]["lam3"][:, :], zcat[:, :]):
                        link(v.memset(t, 0.0))
                    v.memset(zcat[:, 96:98], 1.0)
                    for h in range(2):
                        v.memset(tw[h][half(0), :, 0, 1, :].bitcast(F32), 0.0)
                    link(v.memset(bb[:, :].bitcast(F32), 0.0))
                    prep_squares(ly, link)
                    prep_turned(ly, link)
                    prep_styles(ly, link)
                    prep_scales(ly, link)
                    prep_stationaries(ly, link)
                    prep_split(ly, link)
                    prep_bias(ly, link, 0)

                def fw_low(g0, g1):
                    for g in range(g0, g1):
                        dve.wait_ge(s["fw_hi"], g + 1)
                        at = (slice(None), slice(4 * (g % 2), 4 * (g % 2) + 4), slice((g // 2) * P, (g // 2 + 1) * P))
                        v.tensor_tensor(fw_l[at], bank[6 + g % 2][:, :].rearrange("p (k e) -> p k e", k=4), fw_h[at].bitcast(F32),
                                        ALU.subtract).then_inc(s["fw_ready"], 1)

                def scaled(dst, ps, lam, add, shape, tmp):
                    link(v.tensor_tensor(tmp, ps, lam.broadcast_to(shape), ALU.mult))
                    return v.tensor_tensor(dst, tmp, add.broadcast_to(shape), ALU.add)

                tm = mtmp[:, :]

                def ends_0():
                    if ly["lora"]:
                        dve.wait_ge(zs["bias_row_moved"], 16)
                    for t in (x8, y8):
                        last = v.memset(t[:, :, :, 0::MH + 1], 0.0)
                    link(last)
                    dve.wait_ge(s["ends"], 32)
                    for p in range(2):
                        for h in range(2):
                            last = v.tensor_tensor(
                                x8[half(p), :, h::2, 1:1 + MH].rearrange("p e b m -> p b e m"), ends[half(h), :, :, p::2],
                                s_all[half(h), 0, h::2].unsqueeze(2).unsqueeze(3).broadcast_to([C, NPAIR, 2, MH]), ALU.mult)
                    last.then_inc(s["x8_ready"], 1)

                def ends_1():
                    dve.wait_ge(s["m1_acc"], 1)
                    for e in range(2):
                        last = scaled(y8[:, e, :, 1:1 + MH], bank[4][:, e * 256:e * 256 + 256].rearrange("p (b m) -> p b m", m=MH),
                                      lam1[:, :].unsqueeze(2), add1[:, :].unsqueeze(2), [P, NB, MH],
                                      tm[:, e * 256:e * 256 + 256].rearrange("p (b m) -> p b m", m=MH))
                    last.then_inc(s["y8_ready"], 1)
                    link(v.memset(z16[:, :, :, 0::2 * MH + 1], 0.0))

                def ends_2():
                    dve.wait_ge(s["m2_acc"], 1)
                    for q in range(2):
                        for e in range(2):
                            link(scaled(z16[:, e, :, 1 + q:1 + 2 * MH:2],
                                        bank[q][:, e * 256:e * 256 + 256].rearrange("p (b m) -> p b m", m=MH),
                                        lam2[:, :].unsqueeze(2), add2[:, :].unsqueeze(2), [P, NB, MH],
                                        tm[:, e * 256:e * 256 + 256].rearrange("p (b m) -> p b m", m=MH)))
                    v.tensor_tensor(z16[half(0), 0, :, 1], z16[half(0), 0, :, 1], add2q[half(0), :], ALU.subtract)
                    v.tensor_tensor(z16[half(1), 1, :, 2 * MH], z16[half(1), 1, :, 2 * MH], add2q[half(1), :],
                                    ALU.subtract).then_inc(s["z16_ready"], 1)
                    link(v.memset(u16[:, :, :, 0::2 * MH + 1], 0.0))

                def ends_3():
                    dve.wait_ge(s["m3_acc"], 1)
                    for e in range(2):
                        last = scaled(u16[:, e, :, 1:1 + 2 * MH], bank[4 + e][:, :].rearrange("p (b m) -> p b m", m=2 * MH),
                                      lam3[:, 0:NB].unsqueeze(2), add3[:, :].unsqueeze(2), [P, NB, 2 * MH],
                                      tm.rearrange("p (b m) -> p b m", m=2 * MH))
                        if e == 0:
                            link(last)
                    last.then_inc(s["u16_ready"], 1)

                def ends_4():
                    dve.wait_ge(s["m4_acc"], 1)
                    link(v.tensor_tensor(tm[:, 0:256].rearrange("p (b m) -> p b m", m=4),
                                         bank[0][:, 0:256].rearrange("p (b m) -> p b m", m=4),
                                         lam4[:, :].unsqueeze(2).broadcast_to([P, NB, 4]), ALU.mult))
                    v.tensor_scalar(edge[:, :, :, :].rearrange("p b g m -> p (b g m)"), tm[:, 0:256], bias[:, 3:4], None,
                                    ALU.add).then_inc(s["edge_ready"], 1)

                def low(dst, ps, lam, high):
                    return stt(out=dst, in0=ps, scalar=lam, in1=high.bitcast(F32), op0=ALU.mult, op1=ALU.subtract)

                def w3_low(j, h):
                    dve.wait_ge(s["w3_hi"], 2 * j + h + 1)
                    low(w3_l[h][:, :], pst[:, :, :, :].rearrange("p a q c -> p (a q c)"), lam3[:, bass.ds(2 * j + h, 1)],
                        w3_h[h][:, :]).then_inc(s["w3_ready"], 1)

                def compose_low(j, lora=False, first=False):
                    for h in range(2):
                        dve.wait_ge(s["p_hi"], 2 * j + h + 1)
                        low(p_l[:, h, :, :].rearrange("p a c -> p (a c)"), comp_ps[h][:, 0:5 * C], lam2[:, bass.ds(2 * j + h, 1)],
                            p_h[:, h, :, :].rearrange("p a c -> p (a c)")).then_inc(s["p_ready"], 1)
                    if first:
                        if ly is layers[0]:
                            for i in (1, 2):
                                prep_bias(ly, link, i)
                        fw_low(0, 2)
                    dve.wait_ge(s["q_hi"], 2 * j + 2)
                    for h in range(2):
                        low(q_l[:, h, :], comp_ps[0][:, 4 * C * h:4 * C * (h + 1)], lam1[:, bass.ds(2 * j + h, 1)],
                            q_h[:, h, :]).then_inc(s["q_ready"], 1)
                    if first:
                        fw_low(2, 4)
                    if lora:
                        gates(j - 1)
                    for h in range(2):
                        w3_low(j + 1, h)
                    if first:
                        ends_0()
                    for h in range(2):
                        dve.wait_ge(s["t_hi"], 2 * j + h + 1)
                        low(tw[h][:, 1, :, 0, :], comp_ps[h][:, 0:NSH * C].rearrange("p (u c) -> p u c", c=C),
                            s_all[:, 0, bass.ds(2 * j + h, 1)], tw[h][:, 0, :, 0, :]).then_inc(s["t_lo"], 1)
                        dve.wait_ge(s["t_lo"], 2 * j + h + 1)
                        v.tensor_copy(tw[h][half(1), :, :, 1, :], tw[h][half(0), :, :, 0, :].bitcast(F32))
                        v.tensor_copy(tw[h][half(0), :, 1:NSH, 1, :], tw[h][half(1), :, 0:NSH - 1, 0, :].bitcast(F32)
                                      ).then_inc(s["t_ready"], 1)

                def ffn_result(j, e):
                    dve.wait_ge(s["ffn_acc"], 2 * j + e + 1)
                    if not e:
                        dve.wait_ge(s["res_load"], 16 * j + 16)
                        dve.wait_ge(s["stored"], stores(j))
                    v.tensor_tensor(xout[:, 512 * e:512 * e + 512], ffn_ps[e][:, :], xres[:, 512 * e:512 * e + 512],
                                    ALU.add).then_inc(s["ffn_out"], 1)

                def turned_low(j, part):
                    ks = (slice(0, 6), slice(6, 8))[part]
                    for h in range(2):
                        dve.wait_ge(s["ct_hi"], 4 * j + 2 * part + h + 1)
                        v.tensor_tensor(ct_l[:, ks, h, :], conv_ps[h][:, :].rearrange("p (k o) -> p k o", o=C)[:, ks, :],
                                        ct_h[:, ks, h, :].bitcast(F32), ALU.subtract).then_inc(s["ct_ready"], 1)

                GSTEPS = 7

                def gates(j):
                    def glink(ins, i):
                        ins.then_inc(zs["zeroed"], 1)
                        dve.wait_ge(zs["zeroed"], GSTEPS * j + i)
                    dve.wait_ge(zs["fold_acc"], j + 1)
                    glink(v.tensor_tensor(gate[:, 0:4], lora_ps[:, P + ZR:P + NZ], const4[:, :], ALU.add), 1)
                    glink(v.tensor_reduce(gate[:, 12:13], gate[:, 0:4], AX_X, ALU.max), 2)
                    v.tensor_scalar(gate[:, 4:8], gate[:, 0:4], gate[:, 12:13], None, ALU.subtract).then_inc(zs["logit_ready"], 1)
                    dve.wait_ge(zs["exp_ready"], j + 1)
                    glink(v.tensor_reduce(gate[:, 13:14], gate[:, 8:12], AX_X, ALU.add), 3)
                    glink(v.reciprocal(gate[:, 14:15], gate[:, 13:14]), 4)
                    glink(v.tensor_scalar(gate[:, 0:4], gate[:, 8:12], gate[:, 14:15], LORA_SCALE, ALU.mult, ALU.mult), 5)
                    glink(v.tensor_tensor(za[:, :].rearrange("p (e r) -> p e r", r=R),
                                          lora_ps[:, P:P + ZR].rearrange("p (e r) -> p e r", r=R),
                                          gate[:, 0:4].unsqueeze(2).broadcast_to([P, E_ACT, R]), ALU.mult), 6)
                    v.tensor_copy(zcat[:, 2 * ZR:3 * ZR].bitcast(F32R), za[:, :])
                    glink(v.tensor_copy(zcat[:, 0:ZR].bitcast(F32R), za[:, :]), 7)
                    v.tensor_tensor(zcat[:, ZR:2 * ZR], za[:, :], zcat[:, 0:ZR], ALU.subtract).then_inc(zs["zcat_ready"], 1)

                for h in range(2):
                    w3_low(0, h)
                compose_low(0, first=True)
                ends_1()
                ends_2()
                fw_low(4, 8)
                ends_3()
                fw_low(8, 12)
                ends_4()
                fw_low(12, 16)
                for part in range(2):
                    turned_low(0, part)

                def body(j, step=None):
                    compose_low(j, ly["lora"])
                    if step is not None:
                        prep(step)
                    turned_low(j, 0)
                    ffn_result(j - 1, 0)
                    ffn_result(j - 1, 1)
                    turned_low(j, 1)

                if n == 0:
                    with dve.Fori(1, PREP) as j:
                        body(j)
                    for step in range(PREPS):
                        body(PREP + step, step)
                with dve.Fori(1 if n else PREP + PREPS, NPAIR) as j:
                    body(j)
                if n == 0:
                    prep_split(layers[1], linker(1))
                if ly["lora"]:
                    gates(NPAIR - 1)
                for e in range(2):
                    ffn_result(NPAIR - 1, e)

        @block.tensor
        def _(pe):
            mm = nc.tensor.matmul

            def three(out, wh, wl, xh, xl, start, stop):
                mm(out, wh, xh, start=start, stop=False, skip_group_check=True)
                mm(out, wh, xl, start=False, stop=False, skip_group_check=True)
                return mm(out, wl, xh, start=False, stop=stop, skip_group_check=True)

            flat = lambda t: t.rearrange("p q c -> p (q c)")

            def prep_mod(ly):
                s = ly["s"]
                pe.wait_ge(s["params"], 16 * (8 if ly["lora"] else 9))
                for l in range(NL):
                    last = nc.tensor.transpose(bank[6][:, l * P:(l + 1) * P], mw_in[:, l, :], ident[:, :])
                last.then_inc(s["modt_acc"], 1)
                pe.wait_ge(s["w2_ready"], 1)
                for l in range(NL):
                    last = mm(bank[7][0:C, l * P:(l + 1) * P], wsum[:, l, :], ident[:, :], start=True, stop=True)
                last.then_inc(s["w2_acc"], 1)

            def prep_wt(ly, g):
                for l in (2 * g, 2 * g + 1):
                    for k in range(K):
                        at = ((l % 2) * K + k) * C
                        last = nc.tensor.transpose(bank[7][:, at:at + C],
                                                   wk[half(0), l, k, :, :].rearrange("p g i -> p (g i)"), ident[0:C, 0:C])
                last.then_inc(ly["s"]["wt_acc"], 1)

            def prep_styles(ly):
                s = ly["s"]
                pe.wait_ge(s["modt"], 2)
                for l in range(NL):
                    last = mm(bank[6][:, l * NB:(l + 1) * NB], mw_t[:, l, :], style_t[:, :], start=True, stop=True)
                last.then_inc(s["s_acc"], 1)
                pe.wait_ge(s["w2_ready"], 2)
                prep_wt(ly, 0)

            def prep_demod(ly):
                s = ly["s"]
                pe.wait_ge(s["s_ready"], 1)
                for l in range(NL):
                    last = mm(bank[6][:, l * NB:(l + 1) * NB], wsum_t[:, l, :], ssq[half(0), l, :], start=True, stop=True)
                last.then_inc(s["d_acc"], 1)
                pe.wait_ge(s["wt_ready"], 1)
                prep_wt(ly, 1)

            def prep_bias(ly, i):
                s = ly["s"]
                if i:
                    pe.wait_ge(s["bias_ready"], i)
                else:
                    pe.wait_ge(s["mst_ready"], 1)
                steps = (((1, 3), m2, add1), (range(3), m3, bc[0]), (range(4), m4, bc[1]))[i]
                for k in steps[0]:
                    last = mm(bank[6][:, 0:NB], flat(steps[1][:, k, :, :]), steps[2][:, :], start=(k == steps[0][0]),
                              stop=(k == steps[0][-1]))
                last.then_inc(s["bias_acc"], 1)

            def prep_b_turn(g):
                if g:
                    pe.wait_ge(zs["bt_ready"], g)
                else:
                    pe.wait_ge(zs["pack_ready"], 1)
                for k in range(4):
                    last = nc.tensor.transpose(bank[7][:, k * P:(k + 1) * P],
                                               b_part[:, (4 * g + k) * P:(4 * g + k + 1) * P], ident[:, :])
                last.then_inc(zs["bt_acc"], 1)

            def prep_rows():
                pe.wait_ge(zs["sel_ready"], 1)
                pe.wait_ge(zs["bt_ready"], 2)
                pe.wait_ge(zs["lora_late"], 32)
                mm(bank[6][:, 256:256 + E_ACT], lsum[:, :], sel16[:, :], start=True, stop=True)
                for k in range(CHUNKS):
                    pos = slice(256 * (k // 2) + k % 2, 256 * (k // 2) + 256, 2)
                    mm(bank[7][:, 64 * k:64 * k + ZR], a_in[:, pos], sel[:, 0, :, :].rearrange("p e r -> p (e r)"),
                       start=(k == 0), stop=True, skip_group_check=True)
                    last = mm(bank[7][:, 64 * k + ZR:64 * k + NZ], r_in[:, pos], sel16[:, :],
                              start=False, stop=True, skip_group_check=True)
                last.then_inc(zs["ar_acc"], 1)

            def prep_b_rows():
                pe.wait_ge(zs["ar_ready"], 1)
                for g in range(2):
                    last = mm(bank[6 + g][0:96, :], sel[:, :, :, :].rearrange("p g e r -> p (g e r)"),
                              b_t[:, 512 * g:512 * g + 512], start=True, stop=True)
                last.then_inc(zs["bb_acc"], 1)

            def prep_between(i):
                if i == 1:
                    prep_styles(layers[1])
                elif i == 5:
                    prep_bias(layers[1], 1)
                    prep_b_turn(1)
                elif i == 6:
                    prep_b_rows()

            def prep_after(i):
                if i == 0:
                    prep_mod(layers[1])
                elif i == 1:
                    prep_demod(layers[1])
                elif i == 4:
                    prep_bias(layers[1], 0)
                    prep_b_turn(0)
                elif i == 5:
                    prep_bias(layers[1], 2)
                    prep_rows()

            for n, ly in enumerate(layers):
                s = ly["s"]
                if n == 0:
                    pe.wait_ge(zs["ident_made"], 2)
                    pe.wait_ge(s["params"], 16 * 9)
                    nc.tensor.transpose(bank[5][:, 0:NB], style_in, ident[0:NB, 0:NB]).then_inc(zs["style_acc"], 1)
                    prep_mod(ly)
                    prep_styles(ly)
                    prep_demod(ly)
                    prep_bias(ly, 0)

                def turn_weights(g0, g1):
                    for g in range(g0, g1):
                        ec = g // 2
                        pe.wait_ge((s["f_load0"], s["f_load1"])[ec % 2], 16 * (ec // 2 + 1))
                        if g >= 2:
                            pe.wait_ge(s["fw_ready"], g - 1)
                        elif g == 0:
                            pe.wait_ge(s["bias_ready"], 3)
                            if ly["lora"]:
                                pe.wait_ge(zs["bb_ready"], 1)
                        for k in range(4):
                            ck = 4 * (g % 2) + k
                            last = nc.tensor.transpose(bank[6 + g % 2][:, k * P:(k + 1) * P],
                                                       f_in[ec % 2][:, 256 * (ck // 2) + ck % 2:256 * (ck // 2) + 256:2], ident[:, :])
                        last.then_inc(s["fw_acc"], 1)

                def ends_1():
                    pe.wait_ge(s["x8_ready"], 1)
                    pe.wait_ge(s["mst_ready"], 1)
                    if n:
                        pe.wait_ge(layers[0]["s"]["ffn_out"], ffn_outs(NPAIR))
                    for sh in range(3):
                        last = mm(bank[4][:, :], flat(m1[:, sh, :, :]), x8[:, :, :, sh:sh + MH].rearrange("p e b m -> p (e b) m"),
                                  start=(sh == 0), stop=(sh == 2))
                    last.then_inc(s["m1_acc"], 1)

                def ends_2():
                    pe.wait_ge(s["y8_ready"], 1)
                    pe.wait_ge(s["t_ready"], 2)
                    for i, (q, sh) in enumerate(((1, 1), (0, 0), (1, 0), (0, -1))):
                        last = mm(bank[q][:, :], flat(m2[:, i, :, :]),
                                  y8[:, :, :, 1 + sh:1 + sh + MH].rearrange("p e b m -> p (e b) m"),
                                  start=(i < 2), stop=(i >= 2))
                    last.then_inc(s["m2_acc"], 1)

                def ends_3():
                    pe.wait_ge(s["z16_ready"], 1)
                    for e in range(2):
                        for sh in range(3):
                            last = mm(bank[4 + e][:, :], flat(m3[:, sh, :, :]), z16[:, e, :, sh:sh + 2 * MH],
                                      start=(sh == 0), stop=(sh == 2))
                    last.then_inc(s["m3_acc"], 1)

                def ends_4():
                    pe.wait_ge(s["u16_ready"], 1)
                    out4 = bank[0][:, 0:4 * NB].rearrange("p (b e m) -> p b e m", e=2, m=2)
                    for e in range(2):
                        for i in range(4):
                            last = mm(out4[:, :, e, :], flat(m4[:, i, :, :]), u16[:, e, :, MH * e + i:MH * e + i + 3:2],
                                      start=(e == 0 and i == 0), stop=(i == 3), skip_group_check=True)
                    last.then_inc(s["m4_acc"], 1)

                flat2 = lambda t, g: t[:, 2 * g:2 * g + 2, :].rearrange("p b n -> p (b n)")

                def stage_p(j):
                    for h in range(2):
                        pe.wait_ge(s["w3_ready"], 2 * j + h + 1)
                        for g in range(2):
                            last = three(comp_ps[h][:, g * C:(g + 4) * C], w3_h[h][:, g * P:(g + 1) * P],
                                         w3_l[h][:, g * P:(g + 1) * P], flat2(dmv_h, g), flat2(dmv_l, g), g == 0, g == 1)
                        last.then_inc(s["p_acc"], 1)

                def stage_q(j):
                    pe.wait_ge(s["p_ready"], 2 * j + 2)
                    out = comp_ps[0][:, :].rearrange("p (h r c) -> p h r c", h=2, c=C)
                    for i, (t, rs) in enumerate(Q_STEPS):
                        a0, cnt = 2 * rs[0] - t + 2, len(rs)
                        src = slice(a0, a0 + 2 * cnt - 1, 2)
                        last = three(out[:, :, rs[0] + 2:rs[0] + 2 + cnt, :], qst_h[:, 1 - t, :], qst_l[:, 1 - t, :],
                                     p_h[:, :, src, :], p_l[:, :, src, :], i == 0, i == 3)
                    last.then_inc(s["q_acc"], 1)

                def stage_t(j):
                    pe.wait_ge(s["q_ready"], 2 * j + 2)
                    for h in range(2):
                        for i, (d, rs) in enumerate(T_STEPS):
                            u0, cnt = (d + 2 * rs[0]) // 2 + 2, len(rs)
                            src = slice((rs[0] + 2) * C, (rs[0] + 2 + cnt) * C)
                            last = three(comp_ps[h][:, u0 * C:(u0 + cnt) * C], tst_h[:, d + 2, :], tst_l[:, d + 2, :],
                                         q_h[:, h, src], q_l[:, h, src], i == 0, i == len(T_STEPS) - 1)
                        last.then_inc(s["t_acc"], 1)

                def stage_conv(j, h, first=False):
                    pe.wait_ge(s["t_ready"], 2 * j + h + 1)
                    pe.wait_ge(s["x_ready"], 2 * j + h + 1)
                    if not first:
                        pe.wait_ge(s["ct_ready"], 4 * j)
                    for u in range(NSH):
                        last = three(conv_ps[h][:, :], flat(tw[h][:, 0, u, :, :]), flat(tw[h][:, 1, u, :, :]),
                                     x_h[h][:, u:u + HL], x_l[h][:, u:u + HL], u == 0, u == NSH - 1)
                    last.then_inc(s["conv_acc"], 1)

                def stage_turn(j):
                    for h in range(2):
                        pe.wait_ge(s["c_mid"], 2 * j + h + 1)
                        pe.wait_ge(s["c_edge"], 2 * j + h + 1)
                        for k in range(HL // P):
                            last = nc.tensor.transpose(conv_ps[h][:, k * P:(k + 1) * P], conv[h][:, k * P:(k + 1) * P], ident[:, :])
                        last.then_inc(s["ct_acc"], 1)

                ctf = lambda t, k: t[:, k, :, :].rearrange("p h o -> p (h o)")

                def ffn_chunk(j, k, es=(0, 1)):
                    for e in es:
                        cols = slice(512 * e, 512 * e + 512)
                        last = three(ffn_ps[e][:, :], ctf(ct_h, k), ctf(ct_l, k), fw_h[:, k, cols], fw_l[:, k, cols],
                                     k == 0, k == CHUNKS - 1 and not ly["lora"])
                    return last

                def ffn_begin(j):
                    pe.wait_ge(s["ct_ready"], 4 * j + 2)
                    if ly["lora"]:
                        pe.wait_ge(s["ct_ready"], 4 * j + 4)
                        for k in range(CHUNKS):
                            for part in (ct_h, ct_l):
                                last = mm(lora_ps[0:2 * NZ, 0:P], ar[:, k, :], ctf(part, k), start=(k == 0 and part is ct_h),
                                          stop=(k == CHUNKS - 1 and part is ct_l), skip_group_check=True)
                        last.then_inc(zs["z_acc"], 1)
                    pe.wait_ge(s["ffn_out"], ffn_outs(j))

                def fold_z(j):
                    if ly["lora"]:
                        pe.wait_ge(zs["z_out"], j + 1)
                        mm(lora_ps[:, P:P + NZ], z_sum[:, :], fold[:, :], start=True, stop=True).then_inc(zs["fold_acc"], 1)

                def turn_z(j):
                    if ly["lora"]:
                        pe.wait_ge(zs["zcat_ready"], j + 1)
                        nc.tensor.transpose(lora_ps[:, 256:256 + P], zcat[:, :], ident[:, :]).then_inc(zs["zt_acc"], 1)

                def ffn_end(j):
                    pe.wait_ge(s["ct_ready"], 4 * j + 4)
                    for e in range(2):
                        for k in (CHUNKS - 2, CHUNKS - 1):
                            last = ffn_chunk(j, k, (e,))
                        if ly["lora"]:
                            if not e:
                                pe.wait_ge(zs["zt_ready"], j + 1)
                            last = mm(ffn_ps[e][:, :], zt[0:98, :], bb[0:98, 512 * e:512 * e + 512], start=False, stop=True,
                                      skip_group_check=True)
                        last.then_inc(s["ffn_acc"], 1)

                if ly["lora"]:
                    pe.wait_ge(zs["bias_row_moved"], 16)
                    pe.wait_ge(zs["fold_made"], 3)
                pe.wait_ge(s["split_ready"], 1)
                stage_p(0)
                if n == 0:
                    for i in (1, 2):
                        prep_bias(ly, i)
                turn_weights(0, 2)
                pe.wait_ge(s["split_ready"], 2)
                stage_q(0)
                turn_weights(2, 4)
                pe.wait_ge(s["split_ready"], 3)
                stage_t(0)
                ends_1()
                stage_conv(0, 0, True)
                ends_2()
                stage_conv(0, 1, True)
                turn_weights(4, 8)
                ends_3()
                turn_weights(8, 12)
                ends_4()
                turn_weights(12, 16)
                pe.wait_ge(s["fw_ready"], 2 * CHUNKS)
                stage_turn(0)
                pe.wait_ge(s["edge_ready"], 1)

                def body(j, step=None):
                    stage_p(j)
                    ffn_begin(j - 1)
                    ffn_chunk(j - 1, 0)
                    stage_q(j)
                    fold_z(j - 1)
                    for k in (1, 2):
                        ffn_chunk(j - 1, k)
                    stage_t(j)
                    for k in (3, 4):
                        ffn_chunk(j - 1, k)
                    turn_z(j - 1)
                    stage_conv(j, 0)
                    if step is not None:
                        prep_between(step)
                    stage_conv(j, 1)
                    ffn_chunk(j - 1, 5)
                    stage_turn(j)
                    ffn_end(j - 1)
                    if step is not None:
                        prep_after(step)

                if n == 0:
                    with pe.Fori(1, PREP) as j:
                        body(j)
                    for step in range(PREPS):
                        body(PREP + step, step)
                with pe.Fori(1 if n else PREP + PREPS, NPAIR) as j:
                    body(j)
                ffn_begin(NPAIR - 1)
                fold_z(NPAIR - 1)
                for k in range(CHUNKS - 2):
                    ffn_chunk(NPAIR - 1, k)
                turn_z(NPAIR - 1)
                ffn_end(NPAIR - 1)


_INS = ['x', 'cond_512', 'L0_cond_weights', 'L0_cond_biases', 'L0_cond_mod_w', 'L0_cond_mod_b', 'L0_ffn_identity',
        'L1_cond_weights', 'L1_cond_biases', 'L1_cond_mod_w', 'L1_cond_mod_b', 'L1_ffn_W_base', 'L1_ffn_b_base',
        'L1_ffn_lora_A', 'L1_ffn_lora_B', 'L1_ffn_router_W', 'L1_ffn_router_b', 'L1_ffn_domain_prior', 'L1_ffn_active']


def kernel(**inputs):
    import concourse.bacc as _bacc
    from concourse import mybir as _mybir
    from concourse.bass_utils import run_bass_kernel_spmd as _run

    nc = _bacc.Bacc("TRN2", target_bir_lowering=False, num_devices=1)
    arrays, aps = {}, {}
    for name in _INS:
        arr = np.ascontiguousarray(inputs[name])
        arrays[f"in_{name}_dram"] = arr
        aps[name] = nc.dram_tensor(f"in_{name}_dram", arr.shape, _mybir.dt.from_np(arr.dtype), kind="ExternalInput").ap()
    aps["out"] = nc.dram_tensor("out_dram", (NB, C, L), F32, kind="ExternalOutput").ap()
    build(nc, aps)
    r = _run(nc, [arrays], core_ids=[0])
    return r.results[0]["out_dram"]
```

```python
from contextlib import ExitStack

import concourse.bass as bass
import numpy as np
from concourse import mybir

ALU = mybir.AluOpType
ACT = mybir.ActivationFunctionType
F32 = mybir.dt.float32
F32R = mybir.dt.float32r
I32 = mybir.dt.int32
AX_X = mybir.AxisListType.X

NB, C, L = 64, 64, 1024
P = 128
NPAIR = NB // 2
HL = L // 2
STYLE = 128
NL, K = 4, 3
PAD = 2
NSH = 2 * PAD + 1
MINI = 8
MH = MINI // 2
CHUNKS = L // P
SCALE = 1.0 / float(np.sqrt(C * K ** 2))
EPS = 1e-8
BLUR = (0.25, 0.75)
E_TOT, E_ACT, R = 16, 4, 8
ZR = E_ACT * R
NZ = ZR + E_ACT
LORA_SCALE = 16.0 / 8.0
PRIOR_EPS = 1e-12

Q_STEPS = [(t, [r for r in range(-2, 2) if -2 <= 2 * r - t <= 2 and not (t == -2 and r == 1)]) for t in (0, -2, -1, 1)]

SCALES = ("s_all", "lam1", "lam2", "lam3", "lam4", "beta")
PREP, PREPS = 2, 7


def half(p):
    return slice(C * p, C * p + C)


def ffn_outs(pairs):
    return 2 * pairs + 2


def stores(pairs):
    return 16 * pairs + 16


def build(nc, a):
    with ExitStack() as ctx:
        def sb(name, shape, dt=F32):
            return ctx.enter_context(nc.sbuf_tensor(name, shape, dt))

        def sem(name):
            return ctx.enter_context(nc.semaphore(name))

        bank = [ctx.enter_context(nc.psum_tensor(f"bank{i}", [P, 512], F32)) for i in range(8)]
        comp_ps, conv_ps, ffn_ps, lora_ps = bank[0:2], bank[2:4], bank[4:6], bank[6]

        x1 = nc.dram_tensor("x1_dram", [NB, C, L], F32, kind="Internal").ap()

        modb = sb("modb", [P, NL])
        bias = sb("bias", [P, NL])
        ident = sb("ident", [P, P])

        style_t = sb("style_t", [STYLE, NB])
        adds = sb("adds", [P, NL, NB])
        add1, add2, add2q, add3 = (adds[:, i, :] for i in range(NL))
        wsum = adds

        wk = sb("wk", [P, NL, K, 2, C])
        wt = sb("wt", [P, NL, K, C])
        blur_n = sb("blur_n", [P, 6, C])
        blur_t = sb("blur_t", [P, 2, 6, C])
        sta = sb("sta", [P, 13, 2, C])
        qst, tst, dmv = sta[:, 0:4], sta[:, 4:9], sta[:, 9:13].rearrange("p (g b) q c -> p g (b q) c", g=2)
        mst = sb("mst", [P, 14, 2, C])
        m1, m2, m3, m4 = mst[:, 0:3], mst[:, 3:7], mst[:, 7:10], mst[:, 10:14]
        pst = sb("pst", [P, 2, 2, C])
        qst_h, qst_l = sb("qst_h", [P, 4, P], F32R), sb("qst_l", [P, 4, P], F32R)
        tst_h, tst_l = sb("tst_h", [P, 5, P], F32R), sb("tst_l", [P, 5, P], F32R)
        dmv_h, dmv_l = sb("dmv_h", [P, 4, P], F32R), sb("dmv_l", [P, 4, P], F32R)

        ends = sb("ends", [P, NPAIR, 2, MINI])
        win = [sb(f"win{i}", [P, 2 * NB * (2 * MH + 2)]) for i in range(2)]
        x8, y8 = (w[:, 0:2 * NB * (MH + 2)].rearrange("p (e b m) -> p e b m", e=2, b=NB) for w in win)
        z16, u16 = (w[:, :].rearrange("p (e b m) -> p e b m", e=2, b=NB) for w in win)
        mtmp = sb("mtmp", [P, 512])
        wsum_t = mtmp[0:C, :].rearrange("i (l o) -> i l o", l=NL)
        ssq = blur_n[:, 0:NL, :]
        bc = [blur_n[:, i, :] for i in range(3)]
        dtmp = ssq
        dvar = wsum
        dsq, d_all = (mtmp[:, i * NL * NB:(i + 1) * NL * NB].rearrange("p (l b) -> p l b", l=NL) for i in range(2))
        style_in = mtmp[0:NB, 0:STYLE]
        edge = sb("edge", [P, NB, 2, 2])

        f_in = [sb(f"f_in{i}", [P, L]) for i in range(2)]
        fw_h = sb("fw_h", [P, CHUNKS, L], F32R)
        fw_l = sb("fw_l", [P, CHUNKS, L], F32R)

        xraw = sb("xraw", [P, 2, L])
        xres = sb("xres", [P, L])
        xout = sb("xout", [P, L])
        x_h = [sb(f"x_h{h}", [P, HL + 2 * PAD], F32R) for h in range(2)]
        x_l = [sb(f"x_l{h}", [P, HL + 2 * PAD], F32R) for h in range(2)]
        w3_h = [sb(f"w3_h{h}", [P, 2 * P], F32R) for h in range(2)]
        w3_l = [sb(f"w3_l{h}", [P, 2 * P], F32R) for h in range(2)]
        p_h, p_l = sb("p_h", [P, 2, 5, C], F32R), sb("p_l", [P, 2, 5, C], F32R)
        q_h, q_l = sb("q_h", [P, 2, 4 * C], F32R), sb("q_l", [P, 2, 4 * C], F32R)
        qx_h, qx_l = sb("qx_h", [P, 2, NSH, C], F32R), sb("qx_l", [P, 2, NSH, C], F32R)
        tw = [sb(f"tw{h}", [P, 2, NSH, 2, C], F32R) for h in range(2)]
        conv_buf = sb("conv_buf", [P, 2, HL])
        conv = [conv_buf[:, h, :] for h in range(2)]
        w_in = win[0][:, 0:NL * C * K].rearrange("p (l i k) -> p l i k", l=NL, k=K)
        mw_in = win[0][:, NL * C * K:NL * C * K + NL * STYLE].rearrange("p (l s) -> p l s", l=NL)
        wsq = win[1][:, 0:NL * C * K].rearrange("p (l i k) -> p l i k", l=NL, k=K)
        mw_t = win[1][:, NL * C * K:NL * C * K + NL * P].rearrange("p (l c) -> p l c", l=NL)
        ct_h = sb("ct_h", [P, CHUNKS, 2, C], F32R)
        ct_l = sb("ct_l", [P, CHUNKS, 2, C], F32R)

        act_i = sb("act_i", [P, E_ACT], I32)
        act_f = sb("act_f", [P, E_ACT])
        act_m = sb("act_m", [P, E_ACT])
        pidx_i = sb("pidx_i", [P, 2], I32)
        pidx = sb("pidx", [P, 3])
        rr_i = sb("rr_i", [P, E_ACT, R], I32)
        rr = sb("rr", [P, E_ACT, R])
        sel = sb("sel", [P, 3, E_ACT, R])
        sel_e = sb("sel_e", [P, E_ACT])
        sel16 = sb("sel16", [E_TOT, E_ACT])
        rb_in = sb("rb_in", [E_TOT, 1])
        pr_in = sb("pr_in", [E_TOT, 1])
        lnp = sb("lnp", [E_TOT, 1])
        const4 = sb("const4", [P, E_ACT])
        ar = sb("ar", [P, CHUNKS, 2 * NZ], F32R)
        fold = sb("fold", [2 * NZ, NZ])
        z_sum = sb("z_sum", [2 * NZ, P])
        lsum = z_sum[0:E_TOT, :]
        bb = sb("bb", [P, L], F32R)
        b_part = win[1][:, 0:L]
        b_pack = b_part.rearrange("p (g e r) -> p g e r", g=CHUNKS, e=E_TOT)
        f_rows = [f_in[0], f_in[1], xres, xout]
        a_in, r_in, bias_in = f_in[0][:, :], win[0][0:E_TOT, 0:L], win[0][96:97, 0:L]
        b_in = f_in[1][:, :].rearrange("p (e g r) -> p e g r", e=E_TOT, g=CHUNKS)
        b_t = f_in[1]
        gate = sb("gate", [P, 16])
        za = sb("za", [P, ZR])
        zcat = sb("zcat", [P, P])
        zt = sb("zt", [P, P], F32R)

        layers = [
            dict(x=a["x"], out=x1, w=a["L0_cond_weights"], b=a["L0_cond_biases"],
                 mw=a["L0_cond_mod_w"], mb=a["L0_cond_mod_b"], f=a["L0_ffn_identity"], lora=False),
            dict(x=x1, out=a["out"], w=a["L1_cond_weights"], b=a["L1_cond_biases"],
                 mw=a["L1_cond_mod_w"], mb=a["L1_cond_mod_b"], f=a["L1_ffn_W_base"], lora=True),
        ]
        names = ("w_load mw_load params f_load0 f_load1 f_load2 f_load3 modt_acc modt s_acc s_ready w2_acc w2_ready d_acc dvar_ready dsqrt "
                 "wt_acc wt_ready x8_ready m1_acc y8_ready m2_acc z16_ready m3_acc u16_ready "
                 "m4_acc edge_ready bias_acc bias_ready fw_acc fw_hi fw_ready chain "
                 "x_load res_load x_hi x_ready w3_hi w3_ready p_acc p_hi p_ready q_acc q_hi q_ready t_acc t_hi "
                 "t_ready qx_ready blur_ready base_ready tst_ready mst_ready split_hi split_ready t_lo conv_acc c_mid c_edge ct_acc ct_hi ct_ready ffn_acc ffn_out stored").split()
        for n, ly in enumerate(layers):
            ly["s"] = {k: sem(f"{k}_{n}") for k in names}
            ly["bias_ps"] = bank[5 + n]
            ly["s_all"] = sb(f"s_all{n}", [P, NL, NB])
            for k, width in (("lam1", NB), ("lam2", NB), ("lam3", NB + 2), ("lam4", NB), ("beta", NB)):
                ly[k] = sb(f"{k}_{n}", [P, width])
        zs = {k: sem(k) for k in (
            "style_load style_acc pack_ready lora_in ident_made bias_row_moved ln_in ln_ready sel_ready bt_acc bt_ready ar_acc "
            "lora_late ar_ready bb_acc bb_ready z_acc logit_ready exp_ready zcat_ready zt_acc zt_ready gate_step sta_zero fold_made z_out fold_acc").split()}

        block = ctx.enter_context(nc.Block())

        @block.sync
        def _(sp):
            def load_params(ly):
                s = ly["s"]
                for g in range(2):
                    sp.dma_start(w_in[half(g)], ly["w"].rearrange("l o i k -> o l i k")).then_inc(s["w_load"], 16)
                for g in range(2):
                    if ly["lora"]:
                        sp.dma_start(mw_in[half(g)], ly["mw"].rearrange("l c s -> c l s")).then_inc(s["mw_load"], 16)
                    sp.dma_start(modb[half(g)], ly["mb"].rearrange("l c -> c l"), allow_slow_non_contiguous=True).then_inc(s["params"], 16)
                    sp.dma_start(bias[half(g)], ly["b"].rearrange("l c -> c l"), allow_slow_non_contiguous=True).then_inc(s["params"], 16)

            def load_lora():
                for dst, src in ((act_i[:, :], a["L1_ffn_active"].unsqueeze(0).broadcast_to([P, E_ACT])),
                                 (a_in, a["L1_ffn_lora_A"].rearrange("e r h -> (e r) h")),
                                 (b_in, a["L1_ffn_lora_B"].rearrange("e (p g) r -> p e g r", g=CHUNKS)),
                                 (rb_in[:, :], a["L1_ffn_router_b"].unsqueeze(1)),
                                 (pr_in[:, :], a["L1_ffn_domain_prior"].unsqueeze(1))):
                    sp.dma_start(dst, src).then_inc(zs["lora_in"], 16)

            def load_f(ly, ec):
                sp.dma_start(f_rows[ec % 4][:, :], ly["f"][ec * P:(ec + 1) * P, :]).then_inc(ly["s"][f"f_load{ec % 4}"], 16)

            def load_x(ly, j):
                x_pair = ly["x"].rearrange("(j h) c l -> j c h l", h=2)
                sp.dma_start(xraw[half(0)], x_pair[j]).then_inc(ly["s"]["x_load"], 16)
                sp.dma_start(xraw[half(1), :, 0:L - 1], x_pair[j, :, :, 1:L]).then_inc(ly["s"]["x_load"], 16)

            def rows(t):
                return t.rearrange("(j h) c l -> j (h c) l", h=2)

            def load_res(ly, j):
                sp.dma_start(xres[:, :], rows(ly["x"])[j]).then_inc(ly["s"]["res_load"], 16)

            def store(ly, j):
                sp.dma_start(rows(ly["out"])[j], xout[:, :]).then_inc(ly["s"]["stored"], 16)

            first, second = layers
            load_params(first)
            for n, ly in enumerate(layers):
                s = ly["s"]
                sp.sem_inc(s["stored"], 16)
                if n:
                    sp.wait_ge(first["s"]["stored"], stores(NPAIR))
                    load_f(ly, 3)
                else:
                    for e in range(2):
                        sp.dma_start(ends[:, :, e, :], rows(ly["x"])[:, :, e * (L - MINI):e * (L - MINI) + MINI]
                                     .rearrange("j r l -> r j l")).then_inc(s["params"], 16)
                    for ec in range(4):
                        load_f(ly, ec)
                    load_x(ly, 0)
                sp.wait_ge(s["x_ready"], 2)
                load_x(ly, 1)
                for ec in range(4, CHUNKS):
                    sp.wait_ge(s["fw_acc"], 2 * (ec - 3))
                    load_f(ly, ec)
                sp.wait_ge(s["fw_acc"], 2 * CHUNKS)
                load_res(ly, 0)
                if not n:
                    sp.wait_ge(s["edge_ready"], 1)
                    load_params(second)
                    load_lora()
                with sp.Fori(2, NPAIR) as j:
                    sp.wait_ge(s["x_ready"], 2 * j)
                    load_x(ly, j)
                    sp.wait_ge(s["ffn_out"], ffn_outs(j - 1))
                    store(ly, j - 2)
                    load_res(ly, j - 1)
                sp.wait_ge(s["ffn_out"], ffn_outs(NPAIR - 1))
                store(ly, NPAIR - 2)
                load_res(ly, NPAIR - 1)
                if not n:
                    sp.wait_ge(s["x_ready"], 2 * NPAIR)
                    sp.wait_ge(s["stored"], stores(1))
                    load_x(second, 0)
                    sp.wait_ge(zs["bb_ready"], 1)
                    for ec in range(2):
                        load_f(second, ec)
                sp.wait_ge(s["ffn_out"], ffn_outs(NPAIR))
                store(ly, NPAIR - 1)
                if not n:
                    load_f(second, 2)
            sp.wait_ge(s["stored"], stores(NPAIR))

        @block.gpsimd
        def _(pool):
            nc.gpsimd.memset(ident[:, :], 0.0).then_inc(zs["ident_made"], 1)
            pool.wait_ge(zs["ident_made"], 1)
            nc.gpsimd.affine_select(out=ident[:, :], in_=ident[:, :], compare_op=ALU.not_equal, fill=1.0, base=0,
                                    pattern=[[-1, P]], channel_multiplier=1).then_inc(zs["ident_made"], 1)
            nc.gpsimd.iota(pidx_i[:, 0:1], [[0, 1]], base=0, channel_multiplier=1).then_inc(zs["ident_made"], 1)
            nc.gpsimd.iota(rr_i[:, :, :], [[0, E_ACT], [1, R]], base=0, channel_multiplier=0).then_inc(zs["ident_made"], 1)
            for h in range(2):
                for t in (x_h[h], x_l[h]):
                    nc.gpsimd.memset(t[:, 0:PAD].bitcast(F32), 0.0)
                    nc.gpsimd.memset(t[:, PAD + HL:2 * PAD + HL].bitcast(F32), 0.0)
            nc.gpsimd.memset(sta[:, :, :, :], 0.0).then_inc(zs["sta_zero"], 1)
            nc.gpsimd.memset(mst[:, :, :, :], 0.0).then_inc(zs["sta_zero"], 1)
            nc.gpsimd.memset(fold[:, :], 0.0).then_inc(zs["fold_made"], 1)
            for g in range(2):
                pool.wait_ge(zs["fold_made"], g + 1)
                nc.gpsimd.affine_select(out=fold[:, :], in_=fold[:, :], compare_op=ALU.not_equal, fill=1.0, base=-NZ * g,
                                        pattern=[[-1, NZ]], channel_multiplier=1).then_inc(zs["fold_made"], 1)
            for ly in layers:
                s = ly["s"]

                def split_low(j, h):
                    src = xraw[:, h, :].rearrange("p (m q) -> p m q", q=2)[:, :, 0]
                    pool.wait_ge(s["x_hi"], 2 * j + h + 1)
                    nc.gpsimd.tensor_tensor(x_l[h][:, PAD:PAD + HL], src, x_h[h][:, PAD:PAD + HL].bitcast(F32),
                                            ALU.subtract).then_inc(s["x_ready"], 1)

                def put_edge(j, h):
                    dst = conv[h][:, :]
                    dst = bass.AP(dst.tensor, dst.offset, [list(dst.ap[0]), [HL - 2, 2], [1, 2]])
                    nc.gpsimd.tensor_copy(dst, edge[:, bass.ds(2 * j + h, 1), :, :].rearrange("p b g m -> p (b g) m")
                                          ).then_inc(s["c_edge"], 1)

                def body(j, first=False):
                    split_low(j, 0)
                    split_low(j, 1)
                    if first:
                        pool.wait_ge(s["edge_ready"], 1)
                        if ly is not layers[0]:
                            pool.wait_ge(layers[0]["s"]["ct_acc"], 2 * NPAIR)
                    else:
                        pool.wait_ge(s["ct_acc"], 2 * j)
                    put_edge(j, 0)
                    put_edge(j, 1)

                for i, (at, hi, lo) in enumerate(((9, dmv_h, dmv_l), (0, qst_h, qst_l), (4, tst_h, tst_l))):
                    pool.wait_ge(s["split_hi"], i + 1)
                    nc.gpsimd.tensor_tensor(lo[:, :, :], sta[:, at:at + hi.shape[1]].rearrange("p a q c -> p a (q c)"),
                                            hi[:, :, :].bitcast(F32), ALU.subtract).then_inc(s["split_ready"], 1)
                body(0, True)
                with pool.Fori(1, NPAIR) as j:
                    body(j)

        @block.scalar
        def _(act):
            def prep_wt(ly, g):
                act.wait_ge(ly["s"]["wt_acc"], g + 1)
                nc.scalar.copy(wt[:, 2 * g:2 * g + 2, :, :], bank[7][:, 0:2 * K * C].rearrange("p (l k o) -> p l k o", l=2, k=K)
                               ).then_inc(ly["s"]["wt_ready"], 1)

            def prep_sqrt(ly):
                act.wait_ge(ly["s"]["dvar_ready"], 1)
                nc.scalar.activation(dsq, dvar[:, :, :], ACT.Sqrt).then_inc(ly["s"]["dsqrt"], 1)

            def prep_mst(ly):
                act.wait_ge(zs["sta_zero"], 2)
                act.wait_ge(ly["s"]["wt_ready"], 2)
                m13 = mst[:, :, :, :].rearrange("p (g i) q c -> p g i q c", g=2)[:, :, 0:3]
                for p in range(2):
                    nc.scalar.copy(m13[half(p), :, 1, p, :], wt[half(p), 0::2, 1, :])
                    nc.scalar.copy(m13[half(p), :, 1 - p:3 - p, 1 - p, :], wt[half(p), 0::2, 0::2, :])
                act.wait_ge(ly["s"]["w2_ready"], 2)
                if ly["lora"]:
                    act.wait_ge(layers[0]["s"]["split_ready"], 3)
                for p in range(2):
                    for q in range(2):
                        nc.scalar.copy(tst[half(p), 1 + p - q:4 + p - q, q, :], wk[half(p), 0, :, 0, :])
                nc.scalar.copy(tst[half(1), 0, 0, :], wk[half(1), 0, 2, 0, :]).then_inc(ly["s"]["tst_ready"], 1)
                act.wait_ge(ly["s"]["blur_ready"], 1)
                for p in range(2):
                    for q in range(2):
                        nc.scalar.copy(m4[half(p), q:q + 3, q, :], blur_t[half(p), 1, p::2, :])

            def prep_m2(ly):
                act.wait_ge(ly["s"]["blur_ready"], 2)
                for p in range(2):
                    last = nc.scalar.copy(m2[half(p), p:p + 3, :, :].rearrange("p i z c -> p (i z c)"),
                                          blur_n[half(p), :, :].rearrange("p n c -> p (n c)"))
                last.then_inc(ly["s"]["mst_ready"], 1)

            def prep_prior():
                act.wait_ge(zs["ln_in"], 1)
                nc.scalar.activation(lnp[:, :], gate[0:E_TOT, 0:1], ACT.Ln).then_inc(zs["ln_ready"], 1)
                nc.scalar.activation(gate[0:E_TOT, 2:3], gate[0:E_TOT, 1:2], ACT.Exp, scale=0.0)

            def prep_late_loads(ly):
                act.wait_ge(ly["s"]["w2_ready"], 2)
                act.wait_ge(ly["s"]["modt_acc"], 1)
                nc.scalar.dma_start(r_in, a["L1_ffn_router_W"]).then_inc(zs["lora_late"], 16)
                nc.scalar.dma_start(bias_in, a["L1_ffn_b_base"].unsqueeze(0)).then_inc(zs["lora_late"], 16)

            def prep(i):
                ly = layers[1]
                if i == 1:
                    prep_late_loads(ly)
                    prep_wt(ly, 0)
                elif i == 2:
                    prep_wt(ly, 1)
                    prep_sqrt(ly)
                elif i == 3:
                    prep_mst(ly)
                elif i == 4:
                    prep_m2(ly)
                elif i == 5:
                    prep_prior()
                elif i == PREPS:
                    act.wait_ge(ly["s"]["base_ready"], 2)
                    w3_high(ly, 0)

            def w3_high(ly, j):
                for h in range(2):
                    nc.scalar.activation(w3_h[h][:, :], pst[:, :, :, :].rearrange("p a q c -> p (a q c)"), ACT.Copy,
                                         scale=ly["lam3"][:, bass.ds(2 * j + h, 1)]).then_inc(ly["s"]["w3_hi"], 1)

            for n, ly in enumerate(layers):
                s = ly["s"]
                s_all, lam1, lam2, lam3, lam4, beta = (ly[k] for k in SCALES)
                if n == 0:
                    nc.scalar.dma_start(style_in, a["cond_512"]).then_inc(zs["style_load"], 16)
                    for g in range(2):
                        nc.scalar.dma_start(mw_in[half(g)], ly["mw"].rearrange("l c s -> c l s")).then_inc(s["mw_load"], 16)
                    act.wait_ge(zs["style_acc"], 1)
                    nc.scalar.copy(style_t[:, :], bank[5][:, 0:NB]).then_inc(s["modt"], 1)
                    act.wait_ge(s["modt_acc"], 1)
                    nc.scalar.copy(mw_t, bank[6][:, :].rearrange("p (l c) -> p l c", l=NL)).then_inc(s["modt"], 1)
                    act.wait_ge(s["w2_acc"], 1)
                    nc.scalar.copy(wsum_t[:, :, :], bank[7][0:C, :].rearrange("p (l o) -> p l o", l=NL)).then_inc(s["modt"], 1)
                    prep_wt(ly, 0)
                    prep_wt(ly, 1)
                    prep_sqrt(ly)
                    prep_mst(ly)

                def fw_high(g0, g1):
                    for g in range(g0, g1):
                        act.wait_ge(s["fw_acc"], g + 1)
                        dst = fw_h[:, 4 * (g % 2):4 * (g % 2) + 4, (g // 2) * P:(g // 2 + 1) * P]
                        nc.scalar.copy(dst, bank[6 + g % 2][:, :].rearrange("p (k e) -> p k e", k=4)).then_inc(s["fw_hi"], 1)

                def x_high(j, first=False):
                    act.wait_ge(s["x_load"], 32 * j + 32)
                    if not first:
                        act.wait_ge(s["conv_acc"], 2 * j)
                    for h in range(2):
                        nc.scalar.copy(x_h[h][:, PAD:PAD + HL],
                                       xraw[:, h, :].rearrange("p (m q) -> p m q", q=2)[:, :, 0]).then_inc(s["x_hi"], 1)

                def p_high(j):
                    for h in range(2):
                        act.wait_ge(s["p_acc"], 2 * j + h + 1)
                        nc.scalar.activation(p_h[:, h, :, :].rearrange("p a c -> p (a c)"), comp_ps[h][:, 0:5 * C], ACT.Copy,
                                             scale=lam2[:, bass.ds(2 * j + h, 1)]).then_inc(s["p_hi"], 1)

                def q_high(j):
                    act.wait_ge(s["q_acc"], j + 1)
                    for h in range(2):
                        nc.scalar.activation(q_h[:, h, :], comp_ps[0][:, 4 * C * h:4 * C * (h + 1)], ACT.Copy,
                                             scale=lam1[:, bass.ds(2 * j + h, 1)]).then_inc(s["q_hi"], 1)
                    act.wait_ge(s["q_hi"], 2 * j + 2)
                    for p in range(2):
                        nc.scalar.copy(qx_h[half(p), :, p:3 + 2 * p, :],
                                       q_h[half(p), :, (1 - p) * C:4 * C].rearrange("p h (r c) -> p h r c", c=C).bitcast(F32)
                                       ).then_inc(s["qx_ready"], 1)

                def t_high(j):
                    for h in range(2):
                        act.wait_ge(s["t_acc"], 2 * j + h + 1)
                        nc.scalar.activation(tw[h][:, 0, :, 0, :], comp_ps[1 - h][:, 0:NSH * C].rearrange("p (u c) -> p u c", c=C),
                                             ACT.Copy, scale=s_all[:, 0, bass.ds(2 * j + h, 1)]).then_inc(s["t_hi"], 1)

                def compose_high(j, lora=False):
                    p_high(j)
                    if lora:
                        act.wait_ge(zs["z_acc"], j)
                        nc.scalar.copy(z_sum[:, :], lora_ps[0:2 * NZ, 0:P]).then_inc(zs["z_out"], 1)
                    q_high(j)
                    if lora:
                        gate_exp(j - 1)
                    x_high(j)
                    t_high(j)
                    w3_high(ly, j + 1)
                    if lora:
                        zt_out(j - 1)

                def conv_scaled(j, h):
                    act.wait_ge(s["conv_acc"], 2 * j + h + 1)
                    nc.scalar.activation(conv[h][:, 2:HL - 2], conv_ps[h][:, 2:HL - 2], ACT.Identity,
                                         scale=lam4[:, bass.ds(2 * j + h, 1)],
                                         bias=beta[:, bass.ds(2 * j + h, 1)]).then_inc(s["c_mid"], 1)

                def turned_high(j, first=False):
                    for part, ks in enumerate((slice(0, 6), slice(6, 8))):
                        if part and not first:
                            act.wait_ge(s["ffn_acc"], 2 * j)
                        for h in range(2):
                            if part:
                                act.wait_ge(s["ct_ready"], 4 * j + h + 1)
                            else:
                                act.wait_ge(s["ct_acc"], 2 * j + h + 1)
                            nc.scalar.copy(ct_h[:, ks, h, :],
                                           conv_ps[h][:, :].rearrange("p (k o) -> p k o", o=C)[:, ks, :]).then_inc(s["ct_hi"], 1)

                def gate_exp(j):
                    act.wait_ge(zs["logit_ready"], j + 1)
                    nc.scalar.activation(gate[:, 8:12], gate[:, 4:8], ACT.Exp).then_inc(zs["exp_ready"], 1)

                def zt_out(j):
                    act.wait_ge(zs["zt_acc"], j + 1)
                    nc.scalar.copy(zt[0:98, :], lora_ps[0:98, 256:256 + P]).then_inc(zs["zt_ready"], 1)

                if n == 0:
                    fw_high(0, 2)
                    act.wait_ge(s["base_ready"], 2)
                    w3_high(ly, 0)
                    prep_m2(ly)
                p_high(0)
                q_high(0)
                if n == 0:
                    fw_high(2, 4)
                w3_high(ly, 1)
                x_high(0, True)
                t_high(0)
                if n:
                    conv_scaled(0, 0)
                    fw_high(0, 4)
                    g = 4
                else:
                    fw_high(4, 6)
                    act.wait_ge(s["bias_ready"], 3)
                    conv_scaled(0, 0)
                    g = 6
                p_high(1)
                fw_high(g, g + 2)
                conv_scaled(0, 1)
                fw_high(g + 2, g + 4 + 2 * n)
                g += 2 + 2 * n
                fw_high(g + 2, g + 4)
                q_high(1)
                w3_high(ly, 2)
                x_high(1)
                fw_high(g + 4, g + 8)
                turned_high(0, True)
                t_high(1)

                def body(j, step=None, composed=False):
                    if not composed:
                        compose_high(j, ly["lora"])
                    elif ly["lora"]:
                        act.wait_ge(zs["z_acc"], j)
                        nc.scalar.copy(z_sum[:, :], lora_ps[0:2 * NZ, 0:P]).then_inc(zs["z_out"], 1)
                        gate_exp(j - 1)
                        zt_out(j - 1)
                    conv_scaled(j, 0)
                    if step is not None:
                        prep(step)
                    conv_scaled(j, 1)
                    turned_high(j)

                body(1, None, True)
                if n == 0:
                    for step in range(PREPS):
                        body(PREP + step, step)
                    act.wait_ge(zs["bb_ready"], 1)
                    nc.scalar.dma_start(bb[97:98, :].bitcast(F32), b_part[96:97, :]).then_inc(zs["bias_row_moved"], 16)
                    with act.Fori(PREP + PREPS, NPAIR - 1) as j:
                        body(j)
                    body(NPAIR - 1, PREPS)
                else:
                    with act.Fori(2, NPAIR) as j:
                        body(j)
                if ly["lora"]:
                    act.wait_ge(zs["z_acc"], NPAIR)
                    nc.scalar.copy(z_sum[:, :], lora_ps[0:2 * NZ, 0:P]).then_inc(zs["z_out"], 1)
                    gate_exp(NPAIR - 1)
                    zt_out(NPAIR - 1)

        @block.vector
        def _(dve):
            v = nc.vector
            stt = v.scalar_tensor_tensor
            steps_done = [0, 0]

            def linker(n):
                def link(ins):
                    steps_done[n] += 1
                    ins.then_inc(layers[n]["s"]["chain"], 1)
                    dve.wait_ge(layers[n]["s"]["chain"], steps_done[n])
                return link

            def prep_squares(ly, link):
                s = ly["s"]
                dve.wait_ge(s["w_load"], 32)
                link(v.tensor_tensor(wsq[:, :, :, :], w_in[:, :, :, :], w_in[:, :, :, :], ALU.mult))
                v.tensor_reduce(wsum[:, :, :].rearrange("p l i -> p (l i)"),
                                wsq[:, :, :, :].rearrange("p l i k -> p (l i) k"), AX_X, ALU.add).then_inc(s["w2_ready"], 1)
                for l in range(NL):
                    for g in range(2):
                        last = v.tensor_copy(wk[:, l, :, g, :], w_in[:, l, :, :].rearrange("p i k -> p k i"))
                last.then_inc(s["w2_ready"], 1)

            def prep_turned(ly, link):
                s = ly["s"]
                dve.wait_ge(s["modt_acc"], 1)
                v.tensor_copy(mw_t, bank[6][:, :].rearrange("p (l c) -> p l c", l=NL)).then_inc(s["modt"], 1)
                dve.wait_ge(s["w2_acc"], 1)
                v.tensor_copy(wsum_t[:, :, :], bank[7][0:C, :].rearrange("p (l o) -> p l o", l=NL)).then_inc(s["modt"], 1)

            def prep_styles(ly, link):
                s, s_all = ly["s"], ly["s_all"]
                dve.wait_ge(s["s_acc"], 1)
                dve.wait_ge(s["params"], 16 * (4 if ly["lora"] else 6))
                link(v.tensor_tensor(s_all[:, :, :], bank[6][:, 0:NL * NB].rearrange("p (l b) -> p l b", l=NL),
                                     modb[:, :].unsqueeze(2).broadcast_to([P, NL, NB]), ALU.add))
                v.tensor_tensor(ssq[:, :, :], s_all[:, :, :], s_all[:, :, :], ALU.mult).then_inc(s["s_ready"], 1)

            def prep_scales(ly, link):
                s = ly["s"]
                s_all, lam1, lam2, lam3, lam4, beta = (ly[k] for k in SCALES)
                dve.wait_ge(s["d_acc"], 1)
                v.tensor_scalar(dvar[:, :, :], bank[6][:, 0:NL * NB].rearrange("p (l b) -> p l b", l=NL),
                                SCALE * SCALE, EPS, ALU.mult, ALU.add).then_inc(s["dvar_ready"], 1)
                if not ly["lora"]:
                    prep_pst(ly)
                dve.wait_ge(s["dsqrt"], 1)
                link(v.reciprocal(dsq, dsq))
                link(v.tensor_tensor(dtmp[:, :, :], dsq, dsq, ALU.mult))
                link(v.tensor_tensor(dtmp[:, :, :], dtmp[:, :, :], dvar[:, :, :], ALU.mult))
                link(v.tensor_scalar(dtmp[:, :, :], dtmp[:, :, :], -0.5, 1.5, ALU.mult, ALU.add))
                link(v.tensor_tensor(d_all[:, :, :], dtmp[:, :, :], dsq, ALU.mult))
                stt(out=lam1[:, :], in0=d_all[:, 0, :], scalar=SCALE, in1=d_all[:, 1, :], op0=ALU.mult, op1=ALU.mult)
                stt(out=lam2[:, :], in0=s_all[:, 1, :], scalar=SCALE, in1=s_all[:, 2, :], op0=ALU.mult, op1=ALU.mult)
                stt(out=lam3[:, 0:NB], in0=d_all[:, 2, :], scalar=SCALE, in1=s_all[:, 3, :], op0=ALU.mult, op1=ALU.mult)
                v.tensor_scalar(lam4[:, :], d_all[:, 3, :], 0.5 * SCALE, None, ALU.mult).then_inc(s["base_ready"], 1)
                v.tensor_scalar(add1[:, :], d_all[:, 1, :], bias[:, 0:1], None, ALU.mult)
                v.tensor_scalar(add2[:, :], s_all[:, 2, :], bias[:, 1:2], 2.0, ALU.mult, ALU.mult)
                v.tensor_scalar(add2q[:, :], s_all[:, 2, :], bias[:, 1:2], 0.25, ALU.mult, ALU.mult)
                link(v.tensor_scalar(add3[:, :], s_all[:, 3, :], bias[:, 2:3], None, ALU.mult))

            def prep_blur_t(ly, link):
                taps = lambda a, b: (blur_t[:, :, a:b, :].rearrange("p l (j n) c -> p l j (n c)", j=2) if b - a == 6
                                     else blur_t[:, :, a:b, :].rearrange("p l n c -> p l (n c)"))
                dve.wait_ge(ly["s"]["wt_ready"], 2)
                w13 = wt[:, 1::2, :, :].rearrange("p l k c -> p l (k c)")
                link(v.tensor_scalar(taps(0, 6), w13.unsqueeze(2).broadcast_to([P, 2, 2, K * C]), BLUR[0], None, ALU.mult))
                link(stt(out=taps(1, 4), in0=w13, scalar=BLUR[1], in1=taps(1, 4), op0=ALU.mult, op1=ALU.add))
                stt(out=taps(2, 5), in0=w13, scalar=BLUR[1], in1=taps(2, 5), op0=ALU.mult, op1=ALU.add
                    ).then_inc(ly["s"]["blur_ready"], 1)

            def prep_blur_n(ly, link):
                w1n = wk[:, 1, :, 0, :]
                for g in range(2):
                    last = v.tensor_scalar(blur_n[:, 3 * g:3 * g + 3, :], w1n, BLUR[0], None, ALU.mult)
                link(last)
                link(stt(out=blur_n[:, 1:4, :], in0=w1n, scalar=BLUR[1], in1=blur_n[:, 1:4, :], op0=ALU.mult, op1=ALU.add))
                stt(out=blur_n[:, 2:5, :], in0=w1n, scalar=BLUR[1], in1=blur_n[:, 2:5, :], op0=ALU.mult, op1=ALU.add
                    ).then_inc(ly["s"]["blur_ready"], 1)

            def prep_dmv(ly, link):
                dve.wait_ge(ly["s"]["blur_ready"], 1)
                dve.wait_ge(zs["sta_zero"], 1)
                if ly["lora"]:
                    dve.wait_ge(layers[0]["s"]["split_ready"], 3)
                for p in range(2):
                    last = v.tensor_copy(dmv[half(p), :, p:p + 3, :], blur_t[half(p), 1, :, :].rearrange("p (i a) c -> p a i c", a=2))
                link(last)

            def prep_qst(ly, link):
                for p in range(2):
                    for h in range(2):
                        last = v.tensor_copy(qst[half(p), h:h + 3, h, :], blur_t[half(p), 0, p::2, :])
                link(last)

            def prep_pst(ly):
                for p in range(2):
                    v.tensor_copy(pst[half(p), 1 - p, :, :], wk[half(p), 2, p:p + 2, 0, :])
                    last = v.tensor_copy(pst[half(p), p, 1 - p, :], wk[half(p), 2, 2 * p, 0, :])
                last.then_inc(ly["s"]["base_ready"], 1)

            def prep_split(ly, parts):
                for at, hi in ((9, dmv_h), (0, qst_h), (4, tst_h))[parts]:
                    if hi is tst_h:
                        dve.wait_ge(ly["s"]["tst_ready"], 1)
                    v.tensor_copy(hi[:, :, :], sta[:, at:at + hi.shape[1]].rearrange("p a q c -> p a (q c)")
                                  ).then_inc(ly["s"]["split_hi"], 1)

            def prep_bias(ly, link, i):
                s = ly["s"]
                dve.wait_ge(s["bias_acc"], i + 1)
                lam, add, dst = ((ly["lam2"][:, :], add2[:, :], bc[0]), (ly["lam3"][:, 0:NB], add3[:, :], bc[1]),
                                 (ly["lam4"][:, :], bias[:, 3:4].broadcast_to([P, NB]), ly["beta"]))[i]
                link(v.tensor_tensor(bc[2][:, :], ly["bias_ps"][:, 0:NB], lam, ALU.mult))
                v.tensor_tensor(dst[:, :], bc[2][:, :], add, ALU.add).then_inc(s["bias_ready"], 1)

            def prep_chosen(link):
                dve.wait_ge(zs["lora_in"], 16 * 5)
                dve.wait_ge(zs["ident_made"], 4)
                v.tensor_copy(b_pack, b_in.rearrange("p e g r -> p g e r")).then_inc(zs["pack_ready"], 1)
                link(v.tensor_copy(act_f[:, :], act_i[:, :]))
                link(v.tensor_scalar(act_m[:, :], act_f[:, :], 0.0, float(E_TOT), ALU.is_lt, ALU.mult))
                link(v.tensor_tensor(act_f[:, :], act_f[:, :], act_m[:, :], ALU.add))
                link(v.tensor_scalar(act_f[:, :], act_f[:, :], 0.0, float(E_TOT - 1), ALU.max, ALU.min))
                link(v.tensor_scalar(pidx_i[:, 1:2], pidx_i[:, 0:1], 3, None, ALU.logical_shift_right))
                link(v.tensor_copy(pidx[:, 0:2], pidx_i[:, 0:2]))
                link(stt(out=pidx[:, 2:3], in0=pidx[:, 1:2], scalar=-float(R), in1=pidx[:, 0:1], op0=ALU.mult, op1=ALU.add))
                link(v.tensor_copy(rr[:, :, :], rr_i[:, :, :]))
                link(v.tensor_scalar(sel_e[:, :], act_f[:, :], pidx[:, 1:2], None, ALU.is_equal))
                v.tensor_scalar(sel16[:, :], act_f[0:E_TOT, :], pidx[0:E_TOT, 0:1], None, ALU.is_equal)
                for g in range(3):
                    stt(out=sel[:, g, :, :], in0=rr[:, :, :], scalar=pidx[:, 2:3],
                        in1=sel_e[:, :].unsqueeze(2).broadcast_to([P, E_ACT, R]), op0=ALU.is_equal, op1=ALU.mult)
                link(v.tensor_scalar(gate[0:E_TOT, 0:1], pr_in[:, :], PRIOR_EPS, None, ALU.add))
                v.tensor_copy(gate[0:E_TOT, 1:2], gate[0:E_TOT, 0:1]).then_inc(zs["ln_in"], 1)

            def prep_b_turned(g):
                dve.wait_ge(zs["bt_acc"], g + 1)
                v.tensor_copy(b_t[:, :].rearrange("e (p g) -> e g p", g=CHUNKS)[:, 4 * g:4 * g + 4, :],
                              bank[7][:, :].rearrange("e (g p) -> e g p", g=4)).then_inc(zs["bt_ready"], 1)

            def prep_prior(link):
                dve.wait_ge(zs["ln_ready"], 1)
                link(v.tensor_tensor(lnp[:, :], lnp[:, :], rb_in[:, :], ALU.add))
                v.tensor_copy(lsum[:, :], lnp[:, :].broadcast_to([E_TOT, P])).then_inc(zs["sel_ready"], 1)

            def prep_rows(link):
                dve.wait_ge(zs["ar_acc"], 1)
                ar_ps = bank[7][:, :].rearrange("p (k n) -> p k n", k=CHUNKS)[:, :, 0:NZ]
                link(v.tensor_copy(ar[:, :, 0:NZ], ar_ps))
                v.tensor_tensor(ar[:, :, NZ:2 * NZ], ar_ps, ar[:, :, 0:NZ].bitcast(F32), ALU.subtract)
                v.tensor_copy(const4[:, :], bank[6][:, 256:256 + E_ACT]).then_inc(zs["ar_ready"], 1)

            def prep_b_rows(link):
                dve.wait_ge(zs["bb_acc"], 1)
                for g in range(2):
                    cols = slice(512 * g, 512 * g + 512)
                    v.tensor_copy(bb[0:64, cols], bank[6 + g][0:64, :])
                    link(v.tensor_copy(b_part[64:96, cols].bitcast(F32R), bank[6 + g][64:96, :]))
                    v.tensor_tensor(bb[64:96, cols], bank[6 + g][64:96, :], b_part[64:96, cols], ALU.subtract)
                dve.wait_ge(zs["lora_late"], 32)
                link(v.tensor_copy(bb[96:97, :], bias_in))
                v.tensor_tensor(b_part[96:97, :], bias_in, bb[96:97, :].bitcast(F32), ALU.subtract).then_inc(zs["bb_ready"], 1)

            def low(dst, ps, lam, high):
                return stt(out=dst, in0=ps, scalar=lam, in1=high.bitcast(F32), op0=ALU.mult, op1=ALU.subtract)

            def w3_low(ly, j):
                for h in range(2):
                    dve.wait_ge(ly["s"]["w3_hi"], 2 * j + h + 1)
                    low(w3_l[h][:, :], pst[:, :, :, :].rearrange("p a q c -> p (a q c)"), ly["lam3"][:, bass.ds(2 * j + h, 1)],
                        w3_h[h][:, :]).then_inc(ly["s"]["w3_ready"], 1)

            def prep(i):
                ly, link = layers[1], linker(1)
                if i == 0:
                    prep_squares(ly, link)
                elif i == 1:
                    prep_turned(ly, link)
                    prep_styles(ly, link)
                elif i == 2:
                    prep_scales(ly, link)
                elif i == 3:
                    prep_blur_t(ly, link)
                    prep_blur_n(ly, link)
                    prep_dmv(ly, link)
                    prep_qst(ly, link)
                elif i == 4:
                    prep_chosen(link)
                elif i == 5:
                    prep_bias(ly, link, 0)
                    prep_b_turned(0)
                    prep_bias(ly, link, 1)
                    prep_b_turned(1)
                    prep_prior(link)
                elif i == 6:
                    prep_bias(ly, link, 2)
                    prep_rows(link)
                    prep_b_rows(link)
                elif i == PREPS:
                    dve.wait_ge(layers[0]["s"]["w3_ready"], 2 * NPAIR + 2)
                    prep_pst(ly)
                    prep_split(ly, slice(0, 3))
                    w3_low(ly, 0)

            def ffn_result(ly, j, e):
                s = ly["s"]
                dve.wait_ge(s["ffn_acc"], 2 * j + e + 1)
                if not e:
                    dve.wait_ge(s["res_load"], 16 * j + 16)
                    dve.wait_ge(s["stored"], stores(j))
                if not ly["lora"]:
                    cols = slice(e * (512 - MINI), e * (512 - MINI) + MINI)
                    v.tensor_tensor(ends[:, bass.ds(j, 1), e, :].rearrange("p b m -> p (b m)"), ffn_ps[e][:, cols],
                                    xres[:, 512 * e + cols.start:512 * e + cols.stop], ALU.add)
                v.tensor_tensor(xout[:, 512 * e:512 * e + 512], ffn_ps[e][:, :], xres[:, 512 * e:512 * e + 512],
                                ALU.add).then_inc(s["ffn_out"], 1)

            for n, ly in enumerate(layers):
                s = ly["s"]
                s_all, lam1, lam2, lam3, lam4, beta = (ly[k] for k in SCALES)
                link = linker(n)
                dve.sem_inc(s["ffn_out"], 2)
                if n == 0:
                    for t in (pst[:, :, :, :], layers[0]["lam3"][:, :], layers[1]["lam3"][:, :], zcat[:, :]):
                        link(v.memset(t, 0.0))
                    v.memset(zcat[:, 96:98], 1.0)
                    for h in range(2):
                        v.memset(tw[h][half(0), :, 0, 1, :].bitcast(F32), 0.0)
                    for t in (qx_h, qx_l):
                        v.memset(t[half(0), :, 3:NSH, :].bitcast(F32), 0.0)
                        v.memset(t[half(1), :, 0, :].bitcast(F32), 0.0)
                    link(v.memset(bb[:, :].bitcast(F32), 0.0))
                    prep_squares(ly, link)
                    prep_styles(ly, link)
                    prep_blur_t(ly, link)
                    prep_scales(ly, link)
                    prep_dmv(ly, link)

                def fw_low(g0, g1):
                    for g in range(g0, g1):
                        dve.wait_ge(s["fw_hi"], g + 1)
                        at = (slice(None), slice(4 * (g % 2), 4 * (g % 2) + 4), slice((g // 2) * P, (g // 2 + 1) * P))
                        v.tensor_tensor(fw_l[at], bank[6 + g % 2][:, :].rearrange("p (k e) -> p k e", k=4), fw_h[at].bitcast(F32),
                                        ALU.subtract).then_inc(s["fw_ready"], 1)

                def scaled(dst, ps, lam, add, shape, tmp):
                    link(v.tensor_tensor(tmp, ps, lam.broadcast_to(shape), ALU.mult))
                    return v.tensor_tensor(dst, tmp, add.broadcast_to(shape), ALU.add)

                tm = mtmp[:, :]

                def ends_0():
                    if ly["lora"]:
                        dve.wait_ge(zs["bias_row_moved"], 16)
                    for t in (x8, y8):
                        last = v.memset(t[:, :, :, 0::MH + 1], 0.0)
                    link(last)
                    if n:
                        dve.wait_ge(layers[0]["s"]["ffn_out"], ffn_outs(NPAIR))
                    else:
                        dve.wait_ge(s["params"], 16 * 6)
                    for p in range(2):
                        for h in range(2):
                            last = v.tensor_tensor(
                                x8[half(p), :, h::2, 1:1 + MH].rearrange("p e b m -> p b e m"), ends[half(h), :, :, p::2],
                                s_all[half(h), 0, h::2].unsqueeze(2).unsqueeze(3).broadcast_to([C, NPAIR, 2, MH]), ALU.mult)
                    last.then_inc(s["x8_ready"], 1)

                def ends_1():
                    dve.wait_ge(s["m1_acc"], 1)
                    both = lambda t: t[:, :].unsqueeze(1).unsqueeze(3)
                    scaled(y8[:, :, :, 1:1 + MH], bank[4][:, :].rearrange("p (e b m) -> p e b m", e=2, m=MH), both(lam1), both(add1),
                           [P, 2, NB, MH], tm.rearrange("p (e b m) -> p e b m", e=2, m=MH)).then_inc(s["y8_ready"], 1)
                    link(v.memset(z16[:, :, :, 0::2 * MH + 1], 0.0))

                def ends_2():
                    dve.wait_ge(s["m2_acc"], 1)
                    both = lambda t: t[:, :].unsqueeze(1).unsqueeze(3)
                    for q in range(2):
                        link(scaled(z16[:, :, :, 1 + q:1 + 2 * MH:2], bank[4 + q][:, :].rearrange("p (e b m) -> p e b m", e=2, m=MH),
                                    both(lam2), both(add2), [P, 2, NB, MH], tm.rearrange("p (e b m) -> p e b m", e=2, m=MH)))
                    v.tensor_tensor(z16[half(0), 0, :, 1], z16[half(0), 0, :, 1], add2q[half(0), :], ALU.subtract)
                    v.tensor_tensor(z16[half(1), 1, :, 2 * MH], z16[half(1), 1, :, 2 * MH], add2q[half(1), :],
                                    ALU.subtract).then_inc(s["z16_ready"], 1)
                    link(v.memset(u16[:, :, :, 0::2 * MH + 1], 0.0))

                def ends_3():
                    dve.wait_ge(s["m3_acc"], 1)
                    for e in range(2):
                        last = scaled(u16[:, e, :, 1:1 + 2 * MH], bank[2 + e][:, :].rearrange("p (b m) -> p b m", m=2 * MH),
                                      lam3[:, 0:NB].unsqueeze(2), add3[:, :].unsqueeze(2), [P, NB, 2 * MH],
                                      tm.rearrange("p (b m) -> p b m", m=2 * MH))
                        if e == 0:
                            link(last)
                    last.then_inc(s["u16_ready"], 1)

                def ends_4():
                    dve.wait_ge(s["m4_acc"], 1)
                    link(v.tensor_tensor(tm[:, 0:256].rearrange("p (b m) -> p b m", m=4),
                                         bank[4][:, 0:256].rearrange("p (b m) -> p b m", m=4),
                                         lam4[:, :].unsqueeze(2).broadcast_to([P, NB, 4]), ALU.mult))
                    v.tensor_scalar(edge[:, :, :, :].rearrange("p b g m -> p (b g m)"), tm[:, 0:256], bias[:, 3:4], None,
                                    ALU.add).then_inc(s["edge_ready"], 1)

                def p_low(j):
                    for h in range(2):
                        dve.wait_ge(s["p_hi"], 2 * j + h + 1)
                        low(p_l[:, h, :, :].rearrange("p a c -> p (a c)"), comp_ps[h][:, 0:5 * C], lam2[:, bass.ds(2 * j + h, 1)],
                            p_h[:, h, :, :].rearrange("p a c -> p (a c)")).then_inc(s["p_ready"], 1)

                def q_low(j):
                    dve.wait_ge(s["q_hi"], 2 * j + 2)
                    for h in range(2):
                        low(q_l[:, h, :], comp_ps[0][:, 4 * C * h:4 * C * (h + 1)], lam1[:, bass.ds(2 * j + h, 1)],
                            q_h[:, h, :]).then_inc(s["q_ready"], 1)
                    dve.wait_ge(s["q_ready"], 2 * j + 2)
                    for p in range(2):
                        v.tensor_copy(qx_l[half(p), :, p:3 + 2 * p, :],
                                      q_l[half(p), :, (1 - p) * C:4 * C].rearrange("p h (r c) -> p h r c", c=C).bitcast(F32)
                                      ).then_inc(s["qx_ready"], 1)

                def t_low(j):
                    for h in range(2):
                        dve.wait_ge(s["t_hi"], 2 * j + h + 1)
                        low(tw[h][:, 1, :, 0, :], comp_ps[1 - h][:, 0:NSH * C].rearrange("p (u c) -> p u c", c=C),
                            s_all[:, 0, bass.ds(2 * j + h, 1)], tw[h][:, 0, :, 0, :]).then_inc(s["t_lo"], 1)
                        dve.wait_ge(s["t_lo"], 2 * j + h + 1)
                        v.tensor_copy(tw[h][half(1), :, :, 1, :], tw[h][half(0), :, :, 0, :].bitcast(F32))
                        v.tensor_copy(tw[h][half(0), :, 1:NSH, 1, :], tw[h][half(1), :, 0:NSH - 1, 0, :].bitcast(F32)
                                      ).then_inc(s["t_ready"], 1)

                def compose_low(j, lora=False):
                    p_low(j)
                    q_low(j)
                    if lora:
                        gates(j - 1)
                    t_low(j)
                    w3_low(ly, j + 1)

                def turned_low(j, part):
                    ks = (slice(0, 6), slice(6, 8))[part]
                    for h in range(2):
                        dve.wait_ge(s["ct_hi"], 4 * j + 2 * part + h + 1)
                        v.tensor_tensor(ct_l[:, ks, h, :], conv_ps[h][:, :].rearrange("p (k o) -> p k o", o=C)[:, ks, :],
                                        ct_h[:, ks, h, :].bitcast(F32), ALU.subtract).then_inc(s["ct_ready"], 1)

                GSTEPS = 7

                def gates(j):
                    def glink(ins, i):
                        ins.then_inc(zs["gate_step"], 1)
                        dve.wait_ge(zs["gate_step"], GSTEPS * j + i)
                    dve.wait_ge(zs["fold_acc"], j + 1)
                    glink(v.tensor_tensor(gate[:, 0:4], lora_ps[:, P + ZR:P + NZ], const4[:, :], ALU.add), 1)
                    glink(v.tensor_reduce(gate[:, 12:13], gate[:, 0:4], AX_X, ALU.max), 2)
                    v.tensor_scalar(gate[:, 4:8], gate[:, 0:4], gate[:, 12:13], None, ALU.subtract).then_inc(zs["logit_ready"], 1)
                    dve.wait_ge(zs["exp_ready"], j + 1)
                    glink(v.tensor_reduce(gate[:, 13:14], gate[:, 8:12], AX_X, ALU.add), 3)
                    glink(v.reciprocal(gate[:, 14:15], gate[:, 13:14]), 4)
                    glink(v.tensor_scalar(gate[:, 0:4], gate[:, 8:12], gate[:, 14:15], LORA_SCALE, ALU.mult, ALU.mult), 5)
                    glink(v.tensor_tensor(za[:, :].rearrange("p (e r) -> p e r", r=R),
                                          lora_ps[:, P:P + ZR].rearrange("p (e r) -> p e r", r=R),
                                          gate[:, 0:4].unsqueeze(2).broadcast_to([P, E_ACT, R]), ALU.mult), 6)
                    v.tensor_copy(zcat[:, 2 * ZR:3 * ZR].bitcast(F32R), za[:, :])
                    glink(v.tensor_copy(zcat[:, 0:ZR].bitcast(F32R), za[:, :]), 7)
                    v.tensor_tensor(zcat[:, ZR:2 * ZR], za[:, :], zcat[:, 0:ZR], ALU.subtract).then_inc(zs["zcat_ready"], 1)

                if n == 0:
                    prep_split(ly, slice(0, 1))
                    w3_low(ly, 0)
                    prep_qst(ly, link)
                    prep_split(ly, slice(1, 3))
                    prep_blur_n(ly, link)
                    p_low(0)
                    ends_0()
                    fw_low(0, 2)
                    prep_bias(ly, link, 0)
                    q_low(0)
                    fw_low(2, 4)
                    prep_bias(ly, link, 1)
                    w3_low(ly, 1)
                    t_low(0)
                    ends_1()
                    fw_low(4, 6)
                    prep_bias(ly, link, 2)
                    g = 6
                else:
                    p_low(0)
                    q_low(0)
                    w3_low(ly, 1)
                    t_low(0)
                    for e in range(2):
                        ffn_result(layers[0], NPAIR - 1, e)
                    ends_0()
                    fw_low(0, 2)
                    ends_1()
                    fw_low(2, 4)
                    g = 4
                p_low(1)
                ends_2()
                fw_low(g, g + 2 + 2 * n)
                g += 2 + 2 * n
                fw_low(g, g + 2)
                ends_3()
                fw_low(g + 2, g + 4)
                q_low(1)
                w3_low(ly, 2)
                fw_low(g + 4, g + 6)
                ends_4()
                fw_low(g + 6, g + 8)
                for part in range(2):
                    turned_low(0, part)
                t_low(1)

                def body(j, step=None, composed=False):
                    if not composed:
                        compose_low(j, ly["lora"])
                    elif ly["lora"]:
                        gates(j - 1)
                    if step is not None:
                        prep(step)
                    turned_low(j, 0)
                    ffn_result(ly, j - 1, 0)
                    ffn_result(ly, j - 1, 1)
                    turned_low(j, 1)

                body(1, None, True)
                if n == 0:
                    for step in range(PREPS):
                        body(PREP + step, step)
                    with dve.Fori(PREP + PREPS, NPAIR - 1) as j:
                        body(j)
                    body(NPAIR - 1, PREPS)
                else:
                    with dve.Fori(2, NPAIR) as j:
                        body(j)
                if n:
                    gates(NPAIR - 1)
                    for e in range(2):
                        ffn_result(ly, NPAIR - 1, e)

        @block.tensor
        def _(pe):
            mm = nc.tensor.matmul

            def three(out, wh, wl, xh, xl, start, stop):
                mm(out, wh, xh, start=start, stop=False, skip_group_check=True)
                mm(out, wh, xl, start=False, stop=False, skip_group_check=True)
                return mm(out, wl, xh, start=False, stop=stop, skip_group_check=True)

            flat = lambda t: t.rearrange("p q c -> p (q c)")

            def prep_mod(ly):
                s = ly["s"]
                pe.wait_ge(s["mw_load"], 32)
                for l in range(NL):
                    last = nc.tensor.transpose(bank[6][:, l * P:(l + 1) * P], mw_in[:, l, :], ident[:, :])
                last.then_inc(s["modt_acc"], 1)
                pe.wait_ge(s["w2_ready"], 1)
                for l in range(NL):
                    last = mm(bank[7][0:C, l * P:(l + 1) * P], wsum[:, l, :], ident[:, :], start=True, stop=True)
                last.then_inc(s["w2_acc"], 1)

            def prep_wt(ly, g):
                for l in (2 * g, 2 * g + 1):
                    for k in range(K):
                        at = ((l % 2) * K + k) * C
                        last = nc.tensor.transpose(bank[7][:, at:at + C],
                                                   wk[half(0), l, k, :, :].rearrange("p g i -> p (g i)"), ident[0:C, 0:C])
                last.then_inc(ly["s"]["wt_acc"], 1)

            def prep_styles(ly):
                s = ly["s"]
                copies = 2 if ly["lora"] else 3
                pe.wait_ge(s["modt"], copies - 1)
                for l in range(NL):
                    last = mm(bank[6][:, l * NB:(l + 1) * NB], mw_t[:, l, :], style_t[:, :], start=True, stop=True)
                last.then_inc(s["s_acc"], 1)
                pe.wait_ge(s["modt"], copies)
                pe.wait_ge(s["w2_ready"], 2)
                prep_wt(ly, 0)

            def prep_demod(ly):
                s = ly["s"]
                pe.wait_ge(s["wt_ready"], 1)
                prep_wt(ly, 1)
                pe.wait_ge(s["s_ready"], 1)
                for l in range(NL):
                    last = mm(bank[6][:, l * NB:(l + 1) * NB], wsum_t[:, l, :], ssq[half(0), l, :], start=True, stop=True)
                last.then_inc(s["d_acc"], 1)

            def prep_bias(ly, i):
                s = ly["s"]
                if i:
                    pe.wait_ge(s["bias_ready"], i)
                else:
                    pe.wait_ge(s["mst_ready"], 1)
                steps = (((1, 3), m2, add1), (range(3), m3, bc[0]), (range(4), m4, bc[1]))[i]
                for k in steps[0]:
                    last = mm(ly["bias_ps"][:, 0:NB], flat(steps[1][:, k, :, :]), steps[2][:, :], start=(k == steps[0][0]),
                              stop=(k == steps[0][-1]))
                last.then_inc(s["bias_acc"], 1)

            def prep_b_turn(g):
                if g:
                    pe.wait_ge(zs["bt_ready"], g)
                else:
                    pe.wait_ge(zs["pack_ready"], 1)
                for k in range(4):
                    last = nc.tensor.transpose(bank[7][:, k * P:(k + 1) * P],
                                               b_part[:, (4 * g + k) * P:(4 * g + k + 1) * P], ident[:, :])
                last.then_inc(zs["bt_acc"], 1)

            def prep_rows():
                pe.wait_ge(zs["sel_ready"], 1)
                pe.wait_ge(zs["bt_ready"], 2)
                pe.wait_ge(zs["lora_late"], 32)
                mm(bank[6][:, 256:256 + E_ACT], lsum[:, :], sel16[:, :], start=True, stop=True)
                for k in range(CHUNKS):
                    pos = slice(256 * (k // 2) + k % 2, 256 * (k // 2) + 256, 2)
                    mm(bank[7][:, 64 * k:64 * k + ZR], a_in[:, pos], sel[:, 0, :, :].rearrange("p e r -> p (e r)"),
                       start=(k == 0), stop=True, skip_group_check=True)
                    last = mm(bank[7][:, 64 * k + ZR:64 * k + NZ], r_in[:, pos], sel16[:, :],
                              start=False, stop=True, skip_group_check=True)
                last.then_inc(zs["ar_acc"], 1)

            def prep_b_rows():
                pe.wait_ge(zs["ar_ready"], 1)
                for g in range(2):
                    last = mm(bank[6 + g][0:96, :], sel[:, :, :, :].rearrange("p g e r -> p (g e r)"),
                              b_t[:, 512 * g:512 * g + 512], start=True, stop=True)
                last.then_inc(zs["bb_acc"], 1)

            def prep_between(i):
                if i == 1:
                    prep_styles(layers[1])
                elif i == 5:
                    prep_bias(layers[1], 1)
                    prep_b_turn(1)
                elif i == 6:
                    prep_b_rows()

            def prep_after(i):
                if i == 0:
                    prep_mod(layers[1])
                elif i == 1:
                    prep_demod(layers[1])
                elif i == 4:
                    prep_bias(layers[1], 0)
                    prep_b_turn(0)
                elif i == 5:
                    prep_bias(layers[1], 2)
                    prep_rows()

            ctf = lambda t, k: t[:, k, :, :].rearrange("p h o -> p (h o)")

            def ffn_chunk(ly, j, k, es=(0, 1)):
                for e in es:
                    cols = slice(512 * e, 512 * e + 512)
                    last = three(ffn_ps[e][:, :], ctf(ct_h, k), ctf(ct_l, k), fw_h[:, k, cols], fw_l[:, k, cols],
                                 k == 0, k == CHUNKS - 1 and not ly["lora"])
                return last

            def z_product(ly, j):
                if ly["lora"]:
                    pe.wait_ge(ly["s"]["ct_ready"], 4 * j + 4)
                    for k in range(CHUNKS):
                        for part in (ct_h, ct_l):
                            last = mm(lora_ps[0:2 * NZ, 0:P], ar[:, k, :], ctf(part, k), start=(k == 0 and part is ct_h),
                                      stop=(k == CHUNKS - 1 and part is ct_l), skip_group_check=True)
                    last.then_inc(zs["z_acc"], 1)

            def ffn_begin(ly, j):
                s = ly["s"]
                pe.wait_ge(s["ct_ready"], 4 * j + 2)
                pe.wait_ge(s["ffn_out"], ffn_outs(j))

            def ffn_end(ly, j, begun=False):
                s = ly["s"]
                pe.wait_ge(s["ct_ready"], 4 * j + 4)
                for e in range(2):
                    for k in (CHUNKS - 2, CHUNKS - 1)[begun and not e:]:
                        last = ffn_chunk(ly, j, k, (e,))
                    if ly["lora"]:
                        if not e:
                            pe.wait_ge(zs["zt_ready"], j + 1)
                        last = mm(ffn_ps[e][:, :], zt[0:98, :], bb[0:98, 512 * e:512 * e + 512], start=False, stop=True,
                                  skip_group_check=True)
                    last.then_inc(s["ffn_acc"], 1)

            for n, ly in enumerate(layers):
                s = ly["s"]
                if n == 0:
                    pe.wait_ge(zs["ident_made"], 2)
                    pe.wait_ge(zs["style_load"], 16)
                    nc.tensor.transpose(bank[5][:, 0:NB], style_in, ident[0:NB, 0:NB]).then_inc(zs["style_acc"], 1)
                    prep_mod(ly)
                    prep_styles(ly)
                    prep_demod(ly)

                def turn_weights(g0, g1):
                    for g in range(g0, g1):
                        ec = g // 2
                        pe.wait_ge(s[f"f_load{ec % 4}"], 16 * (ec // 4 + 1))
                        if g >= 2:
                            pe.wait_ge(s["fw_ready"], g - 1)
                        elif g == 0:
                            if ly["lora"]:
                                pe.wait_ge(s["bias_ready"], 3)
                                pe.wait_ge(zs["bb_ready"], 1)
                            else:
                                pe.wait_ge(s["dvar_ready"], 1)
                                pe.wait_ge(s["wt_ready"], 2)
                        for k in range(4):
                            ck = 4 * (g % 2) + k
                            last = nc.tensor.transpose(bank[6 + g % 2][:, k * P:(k + 1) * P],
                                                       f_rows[ec % 4][:, 256 * (ck // 2) + ck % 2:256 * (ck // 2) + 256:2], ident[:, :])
                        last.then_inc(s["fw_acc"], 1)

                def ends_1():
                    pe.wait_ge(s["x8_ready"], 1)
                    pe.wait_ge(s["mst_ready"], 1)
                    if n:
                        pe.wait_ge(layers[0]["s"]["ffn_out"], ffn_outs(NPAIR))
                    for sh in range(3):
                        last = mm(bank[4][:, :], flat(m1[:, sh, :, :]), x8[:, :, :, sh:sh + MH].rearrange("p e b m -> p (e b) m"),
                                  start=(sh == 0), stop=(sh == 2))
                    last.then_inc(s["m1_acc"], 1)

                def ends_2():
                    pe.wait_ge(s["y8_ready"], 1)
                    pe.wait_ge(s["bias_ready"], 3)
                    for i, (q, sh) in enumerate(((1, 1), (0, 0), (1, 0), (0, -1))):
                        last = mm(bank[4 + q][:, :], flat(m2[:, i, :, :]),
                                  y8[:, :, :, 1 + sh:1 + sh + MH].rearrange("p e b m -> p (e b) m"),
                                  start=(i < 2), stop=(i >= 2))
                    last.then_inc(s["m2_acc"], 1)

                def ends_3():
                    pe.wait_ge(s["z16_ready"], 1)
                    pe.wait_ge(s["c_mid"], 2)
                    for e in range(2):
                        for sh in range(3):
                            last = mm(bank[2 + e][:, :], flat(m3[:, sh, :, :]), z16[:, e, :, sh:sh + 2 * MH],
                                      start=(sh == 0), stop=(sh == 2))
                    last.then_inc(s["m3_acc"], 1)

                def ends_4():
                    pe.wait_ge(s["u16_ready"], 1)
                    out4 = bank[4][:, 0:4 * NB].rearrange("p (b e m) -> p b e m", e=2, m=2)
                    for e in range(2):
                        for i in range(4):
                            last = mm(out4[:, :, e, :], flat(m4[:, i, :, :]), u16[:, e, :, MH * e + i:MH * e + i + 3:2],
                                      start=(e == 0 and i == 0), stop=(i == 3), skip_group_check=True)
                    last.then_inc(s["m4_acc"], 1)

                flat2 = lambda t, g: t[:, 2 * g:2 * g + 2, :].rearrange("p b n -> p (b n)")

                def stage_p(j):
                    for h in range(2):
                        pe.wait_ge(s["w3_ready"], 2 * j + h + 1)
                        for g in range(2):
                            last = three(comp_ps[h][:, g * C:(g + 4) * C], w3_h[h][:, g * P:(g + 1) * P],
                                         w3_l[h][:, g * P:(g + 1) * P], flat2(dmv_h, g), flat2(dmv_l, g), g == 0, g == 1)
                        last.then_inc(s["p_acc"], 1)

                def stage_q(j):
                    pe.wait_ge(s["p_ready"], 2 * j + 2)
                    out = comp_ps[0][:, :].rearrange("p (h r c) -> p h r c", h=2, c=C)
                    for i, (t, rs) in enumerate(Q_STEPS):
                        a0, cnt = 2 * rs[0] - t + 2, len(rs)
                        src = slice(a0, a0 + 2 * cnt - 1, 2)
                        last = three(out[:, :, rs[0] + 2:rs[0] + 2 + cnt, :], qst_h[:, 1 - t, :], qst_l[:, 1 - t, :],
                                     p_h[:, :, src, :], p_l[:, :, src, :], i == 0, i == 3)
                    last.then_inc(s["q_acc"], 1)

                def stage_t(j, between=None):
                    for h in range(2):
                        pe.wait_ge(s["q_ready"], 2 * j + h + 1)
                        three(comp_ps[1 - h][:, 0:4 * C], tst_h[:, 2, :], tst_l[:, 2, :], q_h[:, h, :], q_l[:, h, :], True, False)
                    if between is not None:
                        ffn_chunk(ly, j - 1, between, (0,))
                    pe.wait_ge(s["qx_ready"], 4 * j + 4)
                    for h in range(2):
                        three(comp_ps[1 - h][:, 0:NSH * C], tst_h[:, 0, :], tst_l[:, 0, :],
                              flat(qx_h[:, h, :, :]), flat(qx_l[:, h, :, :]), False, True).then_inc(s["t_acc"], 1)

                def stage_conv(j, h, first=False):
                    pe.wait_ge(s["t_ready"], 2 * j + h + 1)
                    pe.wait_ge(s["x_ready"], 2 * j + h + 1)
                    if not first:
                        pe.wait_ge(s["ct_ready"], 4 * j)
                    for u in range(NSH):
                        last = three(conv_ps[h][:, :], flat(tw[h][:, 0, u, :, :]), flat(tw[h][:, 1, u, :, :]),
                                     x_h[h][:, u:u + HL], x_l[h][:, u:u + HL], u == 0, u == NSH - 1)
                    last.then_inc(s["conv_acc"], 1)

                def stage_turn(j):
                    for h in range(2):
                        pe.wait_ge(s["c_mid"], 2 * j + h + 1)
                        pe.wait_ge(s["c_edge"], 2 * j + h + 1)
                        for k in range(HL // P):
                            last = nc.tensor.transpose(conv_ps[h][:, k * P:(k + 1) * P], conv[h][:, k * P:(k + 1) * P], ident[:, :])
                        last.then_inc(s["ct_acc"], 1)

                def fold_z(j):
                    if ly["lora"]:
                        pe.wait_ge(zs["z_out"], j + 1)
                        mm(lora_ps[:, P:P + NZ], z_sum[:, :], fold[:, :], start=True, stop=True).then_inc(zs["fold_acc"], 1)

                def turn_z(j):
                    if ly["lora"]:
                        pe.wait_ge(zs["zcat_ready"], j + 1)
                        nc.tensor.transpose(lora_ps[:, 256:256 + P], zcat[:, :], ident[:, :]).then_inc(zs["zt_acc"], 1)

                if ly["lora"]:
                    pe.wait_ge(zs["bias_row_moved"], 16)
                    pe.wait_ge(zs["fold_made"], 3)
                if n == 0:
                    turn_weights(0, 2)
                pe.wait_ge(s["split_ready"], 1)
                stage_p(0)
                if n == 0:
                    prep_bias(ly, 0)
                else:
                    ffn_begin(layers[0], NPAIR - 1)
                    for k in (0, 1):
                        ffn_chunk(layers[0], NPAIR - 1, k)
                pe.wait_ge(s["split_ready"], 2)
                stage_q(0)
                if n == 0:
                    turn_weights(2, 4)
                    prep_bias(ly, 1)
                else:
                    for k in (2, 3):
                        ffn_chunk(layers[0], NPAIR - 1, k)
                pe.wait_ge(s["split_ready"], 3)
                stage_t(0)
                if n:
                    for k in (4, 5):
                        ffn_chunk(layers[0], NPAIR - 1, k)
                    ffn_end(layers[0], NPAIR - 1)
                    stage_conv(0, 0, True)
                    turn_weights(0, 2)
                    ends_1()
                    turn_weights(2, 4)
                    g = 4
                else:
                    ends_1()
                    turn_weights(4, 6)
                    prep_bias(ly, 2)
                    stage_conv(0, 0, True)
                    g = 6
                pe.wait_ge(s["t_ready"], 2)
                stage_p(1)
                ends_2()
                turn_weights(g, g + 2)
                stage_conv(0, 1, True)
                turn_weights(g + 2, g + 2 + 2 * n)
                g += 2 + 2 * n
                turn_weights(g, g + 2)
                ends_3()
                turn_weights(g + 2, g + 4)
                stage_q(1)
                turn_weights(g + 4, g + 6)
                ends_4()
                turn_weights(g + 6, g + 8)
                stage_turn(0)
                stage_t(1)
                pe.wait_ge(s["fw_ready"], 2 * CHUNKS)
                pe.wait_ge(s["edge_ready"], 1)

                def body(j, step=None, composed=False):
                    if not composed:
                        stage_p(j)
                    z_product(ly, j - 1)
                    ffn_begin(ly, j - 1)
                    ffn_chunk(ly, j - 1, 0)
                    if not ly["lora"]:
                        ffn_chunk(ly, j - 1, 1, (0,))
                    if not composed:
                        stage_q(j)
                    fold_z(j - 1)
                    ffn_chunk(ly, j - 1, 1, (0, 1) if ly["lora"] else (1,))
                    ffn_chunk(ly, j - 1, 2)
                    if composed or ly["lora"]:
                        if not composed:
                            stage_t(j)
                        ffn_chunk(ly, j - 1, 3)
                    else:
                        stage_t(j, 3)
                        ffn_chunk(ly, j - 1, 3, (1,))
                    ffn_chunk(ly, j - 1, 4)
                    if not ly["lora"]:
                        ffn_chunk(ly, j - 1, 5, (0,))
                    turn_z(j - 1)
                    stage_conv(j, 0)
                    if step is not None:
                        prep_between(step)
                    stage_conv(j, 1)
                    if ly["lora"]:
                        ffn_chunk(ly, j - 1, 5)
                    else:
                        ffn_chunk(ly, j - 1, 5, (1,))
                        pe.wait_ge(s["ct_ready"], 4 * j)
                        ffn_chunk(ly, j - 1, 6, (0,))
                    stage_turn(j)
                    ffn_end(ly, j - 1, not ly["lora"])
                    if step is not None:
                        prep_after(step)

                body(1, None, True)
                if n == 0:
                    for step in range(PREPS):
                        body(PREP + step, step)
                with pe.Fori(2 if n else PREP + PREPS, NPAIR) as j:
                    body(j)
                if n:
                    ffn_begin(ly, NPAIR - 1)
                    ffn_chunk(ly, NPAIR - 1, 0)
                    z_product(ly, NPAIR - 1)
                    ffn_chunk(ly, NPAIR - 1, 1)
                    fold_z(NPAIR - 1)
                    for k in range(2, CHUNKS - 2):
                        ffn_chunk(ly, NPAIR - 1, k)
                    turn_z(NPAIR - 1)
                    ffn_end(ly, NPAIR - 1)


_INS = ['x', 'cond_512', 'L0_cond_weights', 'L0_cond_biases', 'L0_cond_mod_w', 'L0_cond_mod_b', 'L0_ffn_identity',
        'L1_cond_weights', 'L1_cond_biases', 'L1_cond_mod_w', 'L1_cond_mod_b', 'L1_ffn_W_base', 'L1_ffn_b_base',
        'L1_ffn_lora_A', 'L1_ffn_lora_B', 'L1_ffn_router_W', 'L1_ffn_router_b', 'L1_ffn_domain_prior', 'L1_ffn_active']


def kernel(**inputs):
    import concourse.bacc as _bacc
    from concourse import mybir as _mybir
    from concourse.bass_utils import run_bass_kernel_spmd as _run

    nc = _bacc.Bacc("TRN2", target_bir_lowering=False, num_devices=1)
    arrays, aps = {}, {}
    for name in _INS:
        arr = np.ascontiguousarray(inputs[name])
        arrays[f"in_{name}_dram"] = arr
        aps[name] = nc.dram_tensor(f"in_{name}_dram", arr.shape, _mybir.dt.from_np(arr.dtype), kind="ExternalInput").ap()
    aps["out"] = nc.dram_tensor("out_dram", (NB, C, L), F32, kind="ExternalOutput").ap()
    build(nc, aps)
    r = _run(nc, [arrays], core_ids=[0])
    return r.results[0]["out_dram"]
```
